# Optimizing a Trainium2 kernel written in Bass

```python
import numpy as np
import jax
import jax.numpy as jnp

def _softmax(x, axis=-1):
    return jax.nn.softmax(x, axis=axis)

def _gelu(x):
    return jax.nn.gelu(x, approximate=True)

def _silu(x):
    return jax.nn.silu(x)

def _sigmoid(x):
    return jax.nn.sigmoid(x)

def _layernorm(x, axis=-1, eps=1e-05):
    m = jnp.mean(x, axis=axis, keepdims=True)
    v = jnp.var(x, axis=axis, keepdims=True)
    return (x - m) / jnp.sqrt(v + eps)

def _scatter_add(tgt, idx, src, axis=0):
    return tgt.at[idx].add(src)

def _segment_sum(src, seg, n):
    return jax.ops.segment_sum(src, seg, n)
kernel_name = 'mk_macaron_d1_jaxref_r8_fdc081'

def setup_inputs(seed: int=0):
    np.random.seed(seed)
    _w = jnp.asarray

    def _L0_attn_setup():
        import jax, jax.numpy as jnp
        import numpy as np
        EMBED_DIM = 128
        NUM_HEADS = 16
        HEAD_DIM = EMBED_DIM // NUM_HEADS
        MASKED = True
        key = jax.random.key(seed)
        ks = jax.random.split(key, 9)
        B, S, E = (4, 256, EMBED_DIM)
        sc = 1.0 / np.sqrt(E)
        return {'x': jax.random.normal(ks[0], (B, S, E), jnp.float32), 'wq': jax.random.normal(ks[1], (E, E), jnp.float32) * sc, 'bq': jax.random.normal(ks[2], (E,), jnp.float32) * 0.02, 'wk': jax.random.normal(ks[3], (E, E), jnp.float32) * sc, 'bk': jax.random.normal(ks[4], (E,), jnp.float32) * 0.02, 'wv': jax.random.normal(ks[5], (E, E), jnp.float32) * sc, 'bv': jax.random.normal(ks[6], (E,), jnp.float32) * 0.02, 'wo': jax.random.normal(ks[7], (E, E), jnp.float32) * sc, 'bo': jax.random.normal(ks[8], (E,), jnp.float32) * 0.02}
    _L0_attn_in = _L0_attn_setup()

    def _L0_ffn_setup():
        import jax, jax.numpy as jnp
        import numpy as np
        N_EXP = 8
        TOP_K = 2
        CAPACITY_FACTOR = 1.25
        key = jax.random.key(seed)
        ks = jax.random.split(key, 5)
        B, T, D = (4, 128, 128)
        H = 4 * D
        E = N_EXP
        x = jax.random.normal(ks[0], (B, T, D), jnp.float32)
        gate_w = jax.random.normal(ks[1], (D, E), jnp.float32) * 0.02
        c_fc = jax.random.normal(ks[2], (E, D, H), jnp.float32) * 0.02
        fc_bias = jnp.zeros((E, 1, H), jnp.float32)
        c_proj = jax.random.normal(ks[3], (E, H, D), jnp.float32) * 0.02
        proj_bias = jnp.zeros((E, 1, D), jnp.float32)
        return dict(x=x, gate_w=gate_w, c_fc=c_fc, fc_bias=fc_bias, c_proj=c_proj, proj_bias=proj_bias)
    _L0_ffn_in = _L0_ffn_setup()
    _d = {'L0_attn_x': _L0_attn_in['x'], 'L0_attn_wq': _L0_attn_in['wq'], 'L0_attn_bq': _L0_attn_in['bq'], 'L0_attn_wk': _L0_attn_in['wk'], 'L0_attn_bk': _L0_attn_in['bk'], 'L0_attn_wv': _L0_attn_in['wv'], 'L0_attn_bv': _L0_attn_in['bv'], 'L0_attn_wo': _L0_attn_in['wo'], 'L0_attn_bo': _L0_attn_in['bo'], 'L0_ffn_gate_w': _L0_ffn_in['gate_w'], 'L0_ffn_c_fc': _L0_ffn_in['c_fc'], 'L0_ffn_fc_bias': _L0_ffn_in['fc_bias'], 'L0_ffn_c_proj': _L0_ffn_in['c_proj'], 'L0_ffn_proj_bias': _L0_ffn_in['proj_bias']}
    _x0 = _d['L0_attn_x']
    _d['L0_attn_x'] = jax.random.normal(jax.random.fold_in(jax.random.key(seed), 1), (4, 1024, 128), dtype=_x0.dtype)
    del _x0
    return _d

def reference(L0_attn_x, L0_attn_wq, L0_attn_bq, L0_attn_wk, L0_attn_bk, L0_attn_wv, L0_attn_bv, L0_attn_wo, L0_attn_bo, L0_ffn_gate_w, L0_ffn_c_fc, L0_ffn_fc_bias, L0_ffn_c_proj, L0_ffn_proj_bias):

    def _L0_attn_ref(x, wq, bq, wk, bk, wv, bv, wo, bo):
        import jax, jax.numpy as jnp
        import numpy as np
        EMBED_DIM = 128
        NUM_HEADS = 16
        HEAD_DIM = EMBED_DIM // NUM_HEADS
        MASKED = True
        B, S, E = x.shape
        H, Dh = (NUM_HEADS, HEAD_DIM)

        def split(t):
            return t.reshape(B, S, H, Dh).transpose(0, 2, 1, 3)
        q = split(x @ wq.T + bq)
        k = split(x @ wk.T + bk)
        v = split(x @ wv.T + bv)
        scale = Dh ** 0.5
        scores = jnp.einsum('bhsd,bhtd->bhst', q, k) / scale
        if MASKED:
            causal = jnp.tril(jnp.ones((S, S), dtype=bool))
            scores = jnp.where(causal, scores, -jnp.inf)
        weights = jax.nn.softmax(scores, axis=-1)
        ctx = jnp.einsum('bhst,bhtd->bhsd', weights, v)
        ctx = ctx.transpose(0, 2, 1, 3).reshape(B, S, E)
        return ctx @ wo.T + bo

    def _L0_ffn_ref(x, gate_w, c_fc, fc_bias, c_proj, proj_bias):
        import jax, jax.numpy as jnp
        import numpy as np
        N_EXP = 8
        TOP_K = 2
        CAPACITY_FACTOR = 1.25
        B, T, D = x.shape
        n = B * T
        E, k = (N_EXP, TOP_K)
        cap = int(CAPACITY_FACTOR * n * k / E)
        xt = x.reshape(n, D)
        logits = xt @ gate_w
        top_logits, top_idx = jax.lax.top_k(logits, k)
        masked = jnp.full_like(logits, -jnp.inf)
        masked = masked.at[jnp.arange(n)[:, None], top_idx].set(top_logits)
        router_probs = jax.nn.softmax(masked, axis=-1)
        exp_mask = jax.nn.one_hot(top_idx, E, dtype=jnp.int32)
        exp_mask = jnp.transpose(exp_mask, (1, 0, 2))
        exp_rank = jnp.cumsum(exp_mask.reshape(k * n, E), axis=0) - 1
        exp_rank = exp_rank.reshape(k, n, E)
        exp_mask = exp_mask * (exp_rank < cap).astype(jnp.int32)
        used_capacity = jnp.sum(exp_mask, axis=(0, 1))
        exp_rank = jnp.sum(exp_mask * exp_rank, axis=-1)
        exp_weights = exp_mask.astype(x.dtype) * router_probs[None]
        rank_oh = jax.nn.one_hot(exp_rank, cap, dtype=x.dtype)
        cb_weight = jnp.einsum('kne,knc->nec', exp_weights, rank_oh)
        sec_mask = (cb_weight != 0).astype(x.dtype)
        exp_batches = jnp.einsum('nec,nd->ecd', sec_mask, xt)
        h = jnp.einsum('ecd,edh->ech', exp_batches, c_fc) + fc_bias
        h = jax.nn.gelu(h, approximate=False)
        exp_out = jnp.einsum('ech,ehd->ecd', h, c_proj) + proj_bias
        out = jnp.einsum('nec,ecd->nd', cb_weight, exp_out)
        return out.reshape(B, T, D)
    x = L0_attn_x
    x = x + 0.5 * _L0_ffn_ref(_layernorm(x, axis=-1), L0_ffn_gate_w, L0_ffn_c_fc, L0_ffn_fc_bias, L0_ffn_c_proj, L0_ffn_proj_bias)
    x = x + _L0_attn_ref(_layernorm(x, axis=-1), L0_attn_wq, L0_attn_bq, L0_attn_wk, L0_attn_bk, L0_attn_wv, L0_attn_bv, L0_attn_wo, L0_attn_bo)
    x = x + 0.5 * _L0_ffn_ref(_layernorm(x, axis=-1), L0_ffn_gate_w, L0_ffn_c_fc, L0_ffn_fc_bias, L0_ffn_c_proj, L0_ffn_proj_bias)
    return x

_drawn_inputs = setup_inputs


def setup_inputs(seed=0):
    import zlib

    import numpy as np

    out = dict(_drawn_inputs(seed))
    spreads = {'L0_ffn_fc_bias': (0.0, 0.452), 'L0_ffn_proj_bias': (0.0, 0.1)}
    factors = {'L0_attn_bq': 8.0, 'L0_attn_bk': 8.0, 'L0_attn_bo': 2.694}
    for name, (base, spread) in spreads.items():
        noise = np.random.default_rng([zlib.crc32(name.encode()), seed]).standard_normal(out[name].shape)
        drawn = base * np.exp(spread * noise) if base else spread * noise
        out[name] = jnp.asarray(drawn.astype(out[name].dtype))
    for name, factor in factors.items():
        out[name] = (out[name] * factor).astype(out[name].dtype)
    return out
```

```python
import concourse.bass as bass
from concourse import mybir
from contextlib import ExitStack


def macaron_block_kernel(nc, x, wq, bq, wk, bk, wv, bv, wo, bo, gate_w, c_fc, fc_bias, c_proj, proj_bias, out):
    f32, bf16, i32 = mybir.dt.float32, mybir.dt.bfloat16, mybir.dt.int32
    ALU, ACT, AX = mybir.AluOpType, mybir.ActivationFunctionType, mybir.AxisListType

    P = 128
    B, S, D = x.shape
    N = B * S
    E, _, F = c_fc.shape
    FB = F // P
    T = S // P
    NH, DH = 16, D // 16
    TOPK = 2
    CAP = int(1.25 * N * TOPK / E)
    CT = CAP // P
    EPS = 1e-5
    NEG = -3.0e38
    ROW = D + 4
    C_ID, C_P0, C_P1 = D, D + 1, D + 2
    SKIP = 1.0e6

    HS = 4
    NG = NH // HS
    Q_PART = [0, 0, 0, 1, 1, 2]
    K_PART = [0, 1, 2, 0, 1, 0]
    KS = len(Q_PART) * DH
    HALF = S // 2
    SCALE = float(DH) ** -0.5
    VW = 32

    UNITS = [(1, k) for k in range(T)] + [(0, k) for k in range(T // 2)]
    NU = len(UNITS)

    def unit_queries(u):
        hf, kb = UNITS[u]
        q0 = max(hf * HALF, kb * P)
        return q0, (hf + 1) * HALF - q0

    MASKED = [u for u in range(NU) if UNITS[u][1] * P >= UNITS[u][0] * HALF]
    AUNITS = []
    for h in range(HS):
        for qt in range(T // 2, T):
            AUNITS += [(h, qt, 0, HALF, False), (h, qt, HALF, (qt + 1) * P - HALF, True)]
    NA1 = len(AUNITS)
    for h in range(HS):
        for qt in range(T // 2):
            AUNITS.append((h, qt, 0, (qt + 1) * P, True))
    NA = len(AUNITS)
    A_IN_SLOT = [6, 6, 6, 6, 6, 4, 3, 1, 5, 3, 2, 0]
    assert sum(A_IN_SLOT) == NA and sum(A_IN_SLOT[:6]) >= NA1
    A_FROM = [sum(A_IN_SLOT[:u]) for u in range(NU + 1)]
    U_MA = 8

    def bank_uses(first, final):
        uses = []
        for g in range(NG):
            uses.append(("max0", g))
            if not (first and g == 0):
                uses.append(("ctx0", g - 1))
            if g == 0 and not first:
                uses += ["o_t0", "o_t1", "o_p0", "o_p1"]
            if g == 1 and not final:
                uses += ["x_t0", "x_t1", "q0", "q1", "k0"]
            if g == 2:
                if not final:
                    uses += ["v0", "v1"]
                if not first:
                    uses += ["r_t0", "r_t1", "r_lg"]
            if not (final and g == NG - 1):
                uses.append(("max1", g + 1))
            if g == 1 and not final:
                uses.append("k1")
            if g == 2 and not first:
                uses.append("r_rk")
            uses.append(("ctx1", g))
        return uses

    PRO = ["x_t0", "x_t1", "q0", "q1", "k0", "k1", "v0", "v1", ("max1", 0)]
    FIRST_USES, MID_USES, LAST_USES = bank_uses(True, False), bank_uses(False, False), bank_uses(False, True)
    TAIL = [("ctx0", NG - 1), "o_t0", "o_t1", "o_p0", "o_p1", "r_t0", "r_t1", "r_lg", "r_rk"]
    TAIL_AT = len(PRO) + len(FIRST_USES) + (B - 2) * len(MID_USES) + len(LAST_USES)

    xf = x.rearrange("b s d -> (b s) d")
    bucket = nc.dram_tensor("bucket", [E * 2 * CAP, ROW], f32, kind="Internal").ap()
    mid = nc.dram_tensor("mid", [N + CAP, D], f32, kind="Internal").ap()
    last = nc.dram_tensor("last", [N + CAP, D], f32, kind="Internal").ap()
    q_stack = nc.dram_tensor("q_stack", [B * NH * KS, S], bf16, kind="Internal").ap()
    k_stack = nc.dram_tensor("k_stack", [B * NH * KS, S], bf16, kind="Internal").ap()
    max_rows = nc.dram_tensor("max_rows", [2 * 3 * HS, HALF], bf16, kind="Internal").ap()

    whole = ExitStack()
    with whole:
        def maker(stack):
            def make(name, shape, dt=f32):
                return stack.enter_context(nc.sbuf_tensor(name, shape, dt))
            return make

        def sem(name):
            return whole.enter_context(nc.semaphore(name))

        sb = maker(whole)
        two_banks = [whole.enter_context(nc.psum_tensor(f"banks{i}", [P, 2, 512], f32)) for i in range(4)]
        bank = [two_banks[i // 2][:, i % 2, :] for i in range(8)]

        ident = sb("ident", [P, P])
        identb = sb("identb", [P, P], bf16)
        before = sb("before", [P, P], bf16)
        onesb = sb("onesb", [P, P], bf16)
        onesf = sb("onesf", [P, P])
        gate = sb("gate", [P, E])
        place = sb("place", [P, T, E])
        half_neg = sb("half_neg", [P, T])
        tok_id0 = sb("tok_id0", [P, T])
        tok_id = sb("tok_id", [P, T])
        slot_of = sb("slot_of", [P, CT])
        spare = sb("spare", [P, CT])
        sign = sb("sign", [P, T, TOPK])
        slot0 = sb("slot0", [P, T, TOPK])
        taken = sb("taken", [P, TOPK, E])
        firsts = sb("firsts", [P, E])
        total = sb("total", [P, E])
        is_first = sb("is_first", [P, E, CT])
        is_used = sb("is_used", [P, E, CT])
        window = sb("window", [P, E], i32)
        e_base = sb("e_base", [P, E])
        iota_i = sb("iota_i", [P, 64], i32)
        wqT, wkT, wvT, woT = (sb(n, [P, P]) for n in ("wqT", "wkT", "wvT", "woT"))
        bq_c, bk_c = sb("bq_c", [P, 1]), sb("bk_c", [P, 1])
        bv_r, bo_r = sb("bv_r", [P, P]), sb("bo_r", [P, P])
        bias_up = sb("bias_up", [P, E * FB])
        causal = sb("causal", [P, 512])
        rows = [sb(f"rows{i}", [P, T, ROW]) for i in range(2)]
        stat = sb("stat", [P, T, 6])
        mv = sb("mv", [P, T, 2])
        var_e = sb("var_e", [P, T])
        rstd = sb("rstd", [P, T])
        xT = sb("xT", [P, S])
        lg = sb("lg", [P, T, E])
        lg2 = sb("lg2", [P, T, E])
        eq = sb("eq", [P, T, E])
        cand = sb("cand", [P, T, E])
        top = sb("top", [P, T, TOPK])
        chosen = sb("chosen", [P, T, TOPK])
        hot = sb("hot", [P, T, TOPK, E], bf16)
        gap = sb("gap", [P, T])
        eg = sb("eg", [P, T])
        es = sb("es", [P, T])
        ranks = sb("ranks", [P, T, TOPK, E])
        rank = sb("rank", [P, T, TOPK])
        over = sb("over", [P, T, TOPK])
        place_in = sb("place_in", [P, T, TOPK])
        row_ix = [sb(f"row_ix{i}", [P, TOPK, T], i32) for i in range(2)]

        scattered = [sem(f"scattered{i}") for i in range(2)]
        r_stat, r_rstd, r_rows, r_hot, r_exp, r_idx, r_chain = (
            sem(n) for n in ("r_stat", "r_rstd", "r_rows", "r_hot", "r_exp", "r_idx", "r_chain"))

        passed = sem("passed")

        def wait(eng, s, n):
            if not (isinstance(n, int) and n <= 0):
                eng.wait_ge(s, n)

        def wait_apart(eng, s, n):
            wait(eng, s, n)
            if not isinstance(n, int):
                eng.sem_inc(passed, 1)

        def pairs(eng, count, body):
            body(0, 0)
            body(0, 1)
            with eng.Fori(1, count) as h:
                body(h, 0)
                body(h, 1)

        class Steps:
            def __init__(self, eng, s, base, total):
                self.eng, self.s, self.base, self.total, self.k = eng, s, base, total, 0

            def __call__(self, ins):
                ins.then_inc(self.s, 1)
                self.k += 1
                self.eng.wait_ge(self.s, self.base + self.k)

            def end(self):
                assert self.k == self.total, (self.k, self.total)

        ROUTER_STEPS = 20

        def router_stats(dve, xin, call):
            for t in range(T):
                i = nc.vector.bn_stats(stat[:, t, :], xin[:, t, :])
            i.then_inc(r_chain, 1)
            wait_apart(dve, r_chain, call * ROUTER_STEPS + 1)
            for t in range(T):
                i = nc.vector.bn_aggr(mv[:, t, :], stat[:, t, :])
            i.then_inc(r_chain, 1)
            dve.wait_ge(r_chain, call * ROUTER_STEPS + 2)
            nc.vector.tensor_scalar(var_e[:], mv[:, :, 1], EPS, None, ALU.add).then_inc(r_stat, 1)

        def router_rstd(pool, call):
            wait_apart(pool, r_stat, call + 1)
            nc.gpsimd.tensor_tensor(rstd[:], var_e[:], half_neg[:], ALU.pow).then_inc(r_rstd, 1)

        def router_norm(dve, xin, call, buf, use):
            dve.wait_ge(r_rstd, call + 1)
            wait(dve, scattered[buf], use * 16 * TOPK * T)
            nc.vector.tensor_copy(rows[buf][:, :, C_ID], tok_id[:])
            for t in range(T):
                i = nc.vector.tensor_scalar(rows[buf][:, t, 0:D], xin[:, t, :], mv[:, t, 0:1], rstd[:, t:t + 1],
                                            ALU.subtract, ALU.mult)
            i.then_inc(r_rows, 1)

        def router_transpose(pe, call, buf, half, tb, full):
            if half == 0:
                pe.wait_ge(r_rows, call + 1)
            for t in range(4):
                i = nc.tensor.transpose(tb[:, t * P:(t + 1) * P], rows[buf][:, 4 * half + t, 0:D], ident[:])
            i.then_inc(full, 1)

        def router_logits(pe, lb, full):
            for t in range(T):
                i = nc.tensor.matmul(lb[:, t * E:(t + 1) * E], xT[:, t * P:(t + 1) * P], gate[:], start=True, stop=True)
            i.then_inc(full, 1)

        def router_top2(dve, lb, call, evac, evac_n):
            step = Steps(dve, r_chain, call * ROUTER_STEPS + 2, ROUTER_STEPS - 2)
            nc.vector.tensor_scalar(tok_id[:], tok_id[:], float(S), None, ALU.add)
            i = nc.vector.tensor_copy(lg[:].rearrange("p t e -> p (t e)"), lb[:, 0:T * E])
            i.then_inc(evac, 1)
            dve.wait_ge(evac, evac_n)
            step(nc.vector.tensor_reduce(top[:, :, 0], lg[:], AX.X, ALU.max))


            def one_hot(l, k):
                wide = top[:, :, k:k + 1].broadcast_to([P, T, E])
                step(nc.vector.tensor_tensor(eq[:], l[:], wide, ALU.is_equal))
                step(nc.vector.tensor_tensor(cand[:], eq[:], place[:], ALU.mult))
                step(nc.vector.tensor_reduce(chosen[:, :, k], cand[:], AX.X, ALU.max))
                return nc.vector.tensor_tensor(hot[:, :, k, :], place[:], chosen[:, :, k:k + 1].broadcast_to([P, T, E]),
                                               ALU.is_equal)
            step(one_hot(lg, 0))
            step(nc.vector.scalar_tensor_tensor(lg2[:], hot[:, :, 0, :], NEG, lg[:], ALU.mult, ALU.add))
            step(nc.vector.tensor_reduce(top[:, :, 1], lg2[:], AX.X, ALU.max))
            one_hot(lg2, 1).then_inc(r_hot, 1)
            nc.vector.tensor_tensor(gap[:], top[:, :, 1], top[:, :, 0], ALU.subtract).then_inc(r_hot, 1)
            return step

        def router_exp(act, call):
            act.wait_ge(r_hot, 2 * call + 2)
            nc.scalar.activation(eg[:], gap[:], ACT.Exp).then_inc(r_exp, 1)

        def router_ranks(pe, call, rb, full):
            pe.wait_ge(r_hot, 2 * call + 1)
            W = TOPK * E
            h = hot[:].rearrange("p t k e -> p (t k e)")
            nc.tensor.matmul(rb[:, 0:T * W], before[:], h, start=True, stop=False)
            for s in range(1, T):
                nc.tensor.matmul(rb[:, s * W:T * W], onesb[:], h[:, 0:(T - s) * W], start=False, stop=s == T - 1)
            for t in range(T):
                i = nc.tensor.matmul(rb[:, T * W:T * W + W], onesb[:], h[:, t * W:(t + 1) * W], start=t == 0, stop=t == T - 1)
            i.then_inc(full, 1)

        def router_rows(dve, call, buf, rb, evac, step):
            W = TOPK * E
            tk = taken[:].rearrange("p k e -> p (k e)")
            step(nc.vector.tensor_tensor(ranks[:].rearrange("p t k e -> p t (k e)"),
                                         rb[:, 0:T * W].rearrange("p (t w) -> p t w", w=W),
                                         tk[:, None, :].broadcast_to([P, T, W]), ALU.add))
            nc.vector.tensor_tensor(tk, tk, rb[:, T * W:T * W + W], ALU.add).then_inc(evac, 1)
            step(nc.vector.tensor_tensor(ranks[:], ranks[:], hot[:], ALU.mult))
            step(nc.vector.tensor_reduce(rank[:], ranks[:], AX.X, ALU.add))
            nc.vector.tensor_scalar(over[:], rank[:], float(CAP), SKIP, ALU.is_ge, ALU.mult)
            step(nc.vector.tensor_tensor(place_in[:], rank[:], sign[:], ALU.mult))
            step(nc.vector.scalar_tensor_tensor(place_in[:], chosen[:], -2.0 * CAP, place_in[:], ALU.mult, ALU.add))
            step(nc.vector.tensor_tensor(place_in[:], place_in[:], over[:], ALU.add))
            dve.wait_ge(r_exp, call + 1)
            step(nc.vector.tensor_scalar(es[:], eg[:], 1.0, None, ALU.add))
            step(nc.vector.reciprocal(gap[:], es[:]))
            nc.vector.tensor_copy(rows[buf][:, :, C_P0], gap[:])
            nc.vector.tensor_tensor(rows[buf][:, :, C_P1], gap[:], eg[:], ALU.mult)
            nc.vector.tensor_tensor(row_ix[buf][:].rearrange("p k t -> p t k"), place_in[:], slot0[:],
                                    ALU.add).then_inc(r_idx, 1)
            step.end()

        def router_scatter(pool, buf, n):
            k, t = divmod(n, T)
            nc.gpsimd.indirect_dma_start(bucket[:, :], bass.IndirectOffsetOnAxis(ap=row_ix[buf][:, k, t:t + 1], axis=0),
                                         rows[buf][:, t, :], None, bounds_check=E * 2 * CAP - 1,
                                         oob_is_err=False).then_inc(scattered[buf], 16)

        def router_windows(dve, s, at):
            nc.vector.tensor_scalar(firsts[:], taken[:, 0, :], float(CAP), None, ALU.min).then_inc(s, 1)
            dve.wait_ge(s, at + 1)
            nc.vector.tensor_tensor(total[:], firsts[:], taken[:, 1, :], ALU.add)
            nc.vector.tensor_tensor(window[:], e_base[:], firsts[:], ALU.subtract)
            nc.vector.tensor_tensor(is_first[:], slot_of[:, None, :].broadcast_to([P, E, CT]),
                                    firsts[:, :, None].broadcast_to([P, E, CT]), ALU.is_lt).then_inc(s, 1)
            dve.wait_ge(s, at + 2)
            nc.vector.tensor_tensor(is_used[:], slot_of[:, None, :].broadcast_to([P, E, CT]),
                                    total[:, :, None].broadcast_to([P, E, CT]), ALU.is_lt).then_inc(s, 1)

        s_in, s_w, s_gate, s_zero, s_fill, s_copy = (sem(n) for n in ("s_in", "s_w", "s_gate", "s_zero", "s_fill", "s_copy"))
        s_iota, s_const, s_cdve, s_wt, s_wev = (sem(n) for n in ("s_iota", "s_const", "s_cdve", "s_wt", "s_wev"))
        r1_ld = [sem(f"r1_ld{i}") for i in range(2)]
        r1_full, r1_evac, win1 = sem("r1_full"), sem("r1_evac"), sem("win1")
        with ExitStack() as part:
            sb1 = maker(part)
            zero = sb1("zero", [P, 2 * CAP // P * ROW])
            wraw = sb1("wraw", [P, 4, P])
            braw = sb1("braw", [E * FB, P])
            xin = [sb1(f"xin{i}", [P, T, D]) for i in range(2)]
            block = part.enter_context(nc.Block())
            NCONST = 9

            @block.sync
            def _(sp):
                def load(h, buf):
                    wait_apart(sp, r_rows, 2 * h)
                    sp.dma_start(xin[buf][:], xf[bass.ds((2 * h + buf) * S, S), :].rearrange("(t p) d -> p t d", p=P)
                                 ).then_inc(r1_ld[buf], 16)

                pairs(nc.sync, B // 2, load)

            @block.gpsimd
            def _(pool):
                nc.gpsimd.iota(iota_i[:, 0:CT], pattern=[[P, CT]], base=0, channel_multiplier=1)
                nc.gpsimd.iota(iota_i[:, 32:32 + T], pattern=[[P, T]], base=0, channel_multiplier=1)
                nc.gpsimd.iota(iota_i[:, 48:48 + E], pattern=[[-1, E]], base=E, channel_multiplier=0).then_inc(s_iota, 1)
                wait_apart(pool, s_cdve, 1)
                for tile_ in (ident, identb):
                    nc.gpsimd.affine_select(out=tile_[:], in_=tile_[:], compare_op=ALU.not_equal, fill=1.0, base=0,
                                            pattern=[[-1, P]], channel_multiplier=1).then_inc(s_const, 1)
                nc.gpsimd.affine_select(out=before[:], in_=before[:], compare_op=ALU.is_gt, fill=0.0, base=0,
                                        pattern=[[1, P]], channel_multiplier=-1).then_inc(s_const, 1)
                nc.gpsimd.affine_select(out=causal[:, 512 - P:512], in_=causal[:, 512 - P:512], compare_op=ALU.is_ge,
                                        fill=NEG, base=0, pattern=[[-1, P]], channel_multiplier=1).then_inc(s_const, 1)

                def scatter(call, buf, more):
                    wait_apart(pool, r_idx, call + 1)
                    for n in range(TOPK * T):
                        router_scatter(pool, buf, n)
                        if n == 3 and more:
                            router_rstd(pool, call + 1)

                router_rstd(pool, 0)
                wait_apart(pool, s_fill, 16 * E)
                scatter(0, 0, True)
                scatter(1, 1, True)
                if B > 4:
                    with nc.gpsimd.Fori(1, B // 2 - 1) as h:
                        scatter(2 * h, 0, True)
                        scatter(2 * h + 1, 1, True)
                scatter(B - 2, 0, True)
                scatter(B - 1, 1, False)
                for buf in range(2):
                    wait_apart(pool, scattered[buf], B // 2 * 16 * TOPK * T)

            @block.vector
            def _(dve):
                nc.vector.memset(ident[:], 0.0)
                nc.vector.memset(identb[:], 0.0)
                nc.vector.memset(before[:], 1.0)
                nc.vector.memset(causal[:], 0.0).then_inc(s_cdve, 1)
                nc.vector.memset(zero[:], 0.0).then_inc(s_zero, 1)
                nc.vector.memset(onesb[:], 1.0)
                nc.vector.memset(onesf[:], 1.0)
                nc.vector.memset(half_neg[:], -0.5)
                nc.vector.memset(taken[:], 0.0)
                for buf in range(2):
                    nc.vector.memset(rows[buf][:, :, D:ROW], 0.0)
                nc.vector.memset(sign[:, :, 0], -1.0)
                nc.vector.memset(sign[:, :, 1], 1.0)
                nc.vector.memset(slot0[:, :, 0], 2.0 * CAP * E + CAP - 1)
                nc.vector.memset(slot0[:, :, 1], 2.0 * CAP * E + CAP)
                dve.wait_ge(s_iota, 1)
                nc.vector.tensor_copy(slot_of[:], iota_i[:, 0:CT])
                nc.vector.tensor_copy(tok_id0[:], iota_i[:, 32:32 + T])
                nc.vector.tensor_copy(tok_id[:], iota_i[:, 32:32 + T])
                nc.vector.tensor_copy(place[:], iota_i[:, None, 48:48 + E].broadcast_to([P, T, E]))
                nc.vector.tensor_scalar(spare[:], iota_i[:, 0:CT], float(N), None, ALU.add)
                nc.vector.tensor_scalar(e_base[:], iota_i[:, 48:48 + E], -2.0 * CAP, 2.0 * CAP * E + CAP, ALU.mult,
                                        ALU.add).then_inc(s_cdve, 1)
                dve.wait_ge(s_cdve, 2)
                def route(h, buf):
                    call = 2 * h + buf
                    dve.wait_ge(r1_ld[buf], 16 * h + 16)
                    router_stats(dve, xin[buf], call)
                    router_norm(dve, xin[buf], call, buf, h)
                    dve.wait_ge(r1_full, 4 * call + 3)
                    step = router_top2(dve, bank[0], call, r1_evac, 4 * call + 3)
                    dve.wait_ge(r1_full, 4 * call + 4)
                    router_rows(dve, call, buf, bank[0], r1_evac, step)

                pairs(nc.vector, B // 2, route)
                dve.wait_ge(r_chain, B * ROUTER_STEPS)
                dve.wait_ge(r1_evac, 4 * B)
                router_windows(dve, win1, 0)
                for n, w in enumerate((wqT, wkT, wvT, woT)):
                    dve.wait_ge(s_wt, n + 1)
                    nc.vector.tensor_copy(w[:], bank[1 + n][:, 0:P])
                dve.wait_ge(s_wt, 5)
                nc.vector.tensor_copy(bias_up[:], bank[5][:, 0:E * FB])

            @block.scalar
            def _(act):
                act.dma_start(gate[:], gate_w).then_inc(s_gate, 16)
                act.wait_ge(s_zero, 1)
                for e in range(E):
                    act.dma_start(bucket[e * 2 * CAP:(e + 1) * 2 * CAP, :].rearrange("(p r) c -> p (r c)", p=P),
                                  zero[:]).then_inc(s_fill, 16)
                for n, w in enumerate((wq, wk, wv, wo)):
                    act.dma_start(wraw[:, n, :], w).then_inc(s_w, 16)
                act.dma_start(braw[:], fc_bias.rearrange("e o (b p) -> (e o b) p", p=P)).then_inc(s_w, 16)
                act.dma_start(bq_c[:], bq.rearrange("(p o) -> p o", o=1)).then_inc(s_w, 16)
                act.dma_start(bk_c[:], bk.rearrange("(p o) -> p o", o=1)).then_inc(s_w, 16)
                act.dma_start(bv_r[:], bv.rearrange("(o n) -> o n", o=1).broadcast_to([P, D])).then_inc(s_w, 16)
                act.dma_start(bo_r[:], bo.rearrange("(o n) -> o n", o=1).broadcast_to([P, D])).then_inc(s_w, 16)
                act.dma_start(mid[0:N, :], xf).then_inc(s_copy, 16)
                for dst in (mid, last):
                    act.dma_start(dst[N:N + CAP, :].rearrange("(p r) d -> p (r d)", p=P), zero[:, 0:CT * D]).then_inc(s_copy, 16)
                with nc.scalar.Fori(0, B) as call:
                    for half in range(2):
                        act.wait_ge(r1_full, 4 * call + half + 1)
                        nc.scalar.copy(xT[:, half * 512:half * 512 + 512], bank[0][:]).then_inc(r1_evac, 1)
                    router_exp(act, call)
                act.wait_ge(s_copy, 48)
                act.wait_ge(s_w, 16 * 9)

            @block.tensor
            def _(pe):
                pe.wait_ge(s_const, 4)
                pe.wait_ge(s_gate, 16)
                def route(h, buf):
                    call = 2 * h + buf
                    for half in range(2):
                        wait(pe, r1_evac, 4 * call + half)
                        router_transpose(pe, call, buf, half, bank[0], r1_full)
                    wait(pe, r1_evac, 4 * call + 2)
                    router_logits(pe, bank[0], r1_full)
                    wait(pe, r1_evac, 4 * call + 3)
                    router_ranks(pe, call, bank[0], r1_full)

                pairs(nc.tensor, B // 2, route)
                pe.wait_ge(s_w, 16 * 9)
                for n in range(4):
                    nc.tensor.transpose(bank[1 + n][:, 0:P], wraw[:, n, :], ident[:]).then_inc(s_wt, 1)
                nc.tensor.transpose(bank[5][:, 0:E * FB], braw[:], ident[0:E * FB, 0:E * FB]).then_inc(s_wt, 1)

        CHUNKS = [(0, 4), (4, 4), (8, CT - 8)]
        NC = len(CHUNKS)
        EXPERT_STEPS = 7

        def experts(tag, dest, final):
            rows_ld = [sem(f"rows_ld{tag}{i}") for i in range(2)]
            w_ld = [sem(f"w_ld{tag}{i}") for i in range(2)]
            t_full, t_evac, h_full, h_done, y_full, y_done, y_ready, added, e_chain, e_out = (
                sem(f"{n}{tag}") for n in ("t_full", "t_evac", "h_full", "h_done", "y_full", "y_done", "y_ready",
                                           "added", "e_chain", "e_out"))
            with ExitStack() as part:
                sbe = maker(part)
                xb = [sbe(f"xb{tag}{i}", [P, CT, ROW]) for i in range(2)]
                wfc = [sbe(f"wfc{tag}{i}", [P, F]) for i in range(2)]
                wpj = [sbe(f"wpj{tag}{i}", [P, FB, D]) for i in range(2)]
                bfc = [sbe(f"bfc{tag}{i}", [P, FB]) for i in range(2)]
                bpj = [sbe(f"bpj{tag}{i}", [P, D]) for i in range(2)]
                xbT = [sbe(f"xbT{tag}{i}", [P, CAP]) for i in range(2)]
                hT = [sbe(f"hT{tag}{i}", [P, FB, 512]) for i in range(2)]
                ys = [sbe(f"ys{tag}{i}", [P, CT, D]) for i in range(2)]
                pw = sbe(f"pw{tag}", [P, CT])
                pd = sbe(f"pd{tag}", [P, CT])
                ti = sbe(f"ti{tag}", [P, CT])
                ids = [sbe(f"ids{tag}{i}", [P, CT], i32) for i in range(2)]
                block = part.enter_context(nc.Block())
                t_bank, y_bank, h_bank = bank[0:2], bank[2:4], bank[4:8]

                @block.sync
                def _(sp):
                    def load(h, q):
                        e = 2 * h + q
                        at = nc.sync.value_load(window[0:1, bass.ds(e, 1)], min_val=0, max_val=(2 * E - 1) * CAP)
                        wait_apart(sp, t_full, NC * (e - 1))
                        wait_apart(sp, e_chain, EXPERT_STEPS * (e - 1))
                        sp.dma_start(xb[q][:], bucket[bass.ds(at, CAP), :].rearrange("(t p) c -> p t c", p=P)
                                     ).then_inc(rows_ld[q], 16)
                        wait_apart(sp, y_done, NC * (e - 1))
                        sp.dma_start(wfc[q][:], c_fc.rearrange("e d f -> (e d) f")[bass.ds(e * D, D), :]
                                     ).then_inc(w_ld[q], 16)
                        sp.dma_start(wpj[q][:], c_proj.rearrange("e f d -> (e f) d")[bass.ds(e * F, F), :]
                                     .rearrange("(b p) d -> p b d", p=P)).then_inc(w_ld[q], 16)
                        sp.dma_start(bpj[q][:], proj_bias.rearrange("e o d -> (e o) d")[bass.ds(e, 1), :]
                                     .broadcast_to([P, D])).then_inc(w_ld[q], 16)

                    pairs(nc.sync, E // 2, load)
                    if final:
                        wait_apart(sp, added, E * CT * 16)
                        sp.dma_start(out.rearrange("b s d -> (b s) d"), dest[0:N, :]).then_inc(e_out, 16)
                        wait_apart(sp, e_out, 16)

                @block.tensor
                def _(pe):
                    def transposes(e, q, use):
                        pe.wait_ge(rows_ld[q], 16 * use + 16)
                        for g, (t0, n) in enumerate(CHUNKS):
                            wait(pe, t_evac, NC * e + g - 1)
                            for t in range(n):
                                i = nc.tensor.transpose(t_bank[g % 2 if q == 0 else (g + 1) % 2][:, t * P:(t + 1) * P],
                                                        xb[q][:, t0 + t, 0:D], ident[:])
                            i.then_inc(t_full, 1)

                    def up(c, cc, q, e):
                        t0, n = CHUNKS[cc]
                        pe.wait_ge(t_evac, NC * e + cc + 1)
                        for b in range(FB):
                            wait(pe, h_done, FB * (c - 1) + b + 1)
                            nc.tensor.matmul(h_bank[b][:, 0:n * P], wfc[q][:, b * P:(b + 1) * P],
                                             xbT[q][:, t0 * P:(t0 + n) * P], start=True, stop=True).then_inc(h_full, 1)

                    def down(c, cc, q):
                        t0, n = CHUNKS[cc]
                        par = (cc + NC * q) % 2
                        pe.wait_ge(h_done, FB * (c + 1))
                        wait(pe, y_done, c - 1)
                        for t in range(n):
                            for b in range(FB):
                                i = nc.tensor.matmul(y_bank[par][:, t * P:(t + 1) * P], hT[par][:, b, t * P:(t + 1) * P],
                                                     wpj[q][:, b, :], start=b == 0, stop=b == FB - 1)
                        i.then_inc(y_full, 1)

                    def expert(e, q, use, more):
                        c = NC * e
                        pe.wait_ge(w_ld[q], 48 * use + 48)
                        up(c, 0, q, e)
                        up(c + 1, 1, q, e)
                        down(c, 0, q)
                        up(c + 2, 2, q, e)
                        down(c + 1, 1, q)
                        if more:
                            transposes(e + 1, 1 - q, use + q)
                        down(c + 2, 2, q)

                    transposes(0, 0, 0)
                    expert(0, 0, 0, True)
                    expert(1, 1, 0, True)
                    with nc.tensor.Fori(1, E // 2 - 1) as h:
                        expert(2 * h, 0, h, True)
                        expert(2 * h + 1, 1, h, True)
                    expert(E - 2, 0, E // 2 - 1, True)
                    expert(E - 1, 1, E // 2 - 1, False)

                @block.scalar
                def _(act):
                    def gelus(h, q):
                        e = 2 * h + q
                        for cc, (t0, n) in enumerate(CHUNKS):
                            c = NC * e + cc
                            par = (cc + NC * q) % 2
                            if cc == 0:
                                act.wait_ge(e_chain, EXPERT_STEPS * e + 1)
                            wait(act, y_full, c - 1)
                            for b in range(FB):
                                act.wait_ge(h_full, FB * c + b + 1)
                                nc.scalar.activation(hT[par][:, b, 0:n * P], h_bank[b][:, 0:n * P], ACT.Gelu,
                                                     bias=bfc[q][:, b:b + 1]).then_inc(h_done, 1)
                    pairs(nc.scalar, E // 2, gelus)

                @block.vector
                def _(dve):
                    def turned(e, q, g):
                        t0, n = CHUNKS[g]
                        dve.wait_ge(t_full, NC * e + g + 1)
                        if g == 0:
                            wait(dve, y_full, NC * (e - 1))
                        nc.vector.tensor_copy(xbT[q][:, t0 * P:(t0 + n) * P],
                                              t_bank[g % 2 if q == 0 else (g + 1) % 2][:, 0:n * P]).then_inc(t_evac, 1)

                    def numbers(e, q, use):
                        step = Steps(dve, e_chain, e * EXPERT_STEPS, EXPERT_STEPS)
                        wait(dve, h_done, FB * NC * (e - 1))
                        step(nc.vector.tensor_copy(bfc[q][:], bias_up[:, bass.ds(e * FB, FB)]))
                        dve.wait_ge(rows_ld[q], 16 * use + 16)
                        wait(dve, added, 16 * CT * (e - 1))
                        one, used = is_first[:, bass.ds(e, 1), :], is_used[:, bass.ds(e, 1), :]
                        one = one.rearrange("p o t -> p (o t)")
                        used = used.rearrange("p o t -> p (o t)")
                        nc.vector.tensor_tensor(ti[:], xb[q][:, :, C_ID], spare[:], ALU.subtract)
                        step(nc.vector.tensor_tensor(pd[:], xb[q][:, :, C_P0], xb[q][:, :, C_P1], ALU.subtract))
                        step(nc.vector.tensor_tensor(pd[:], pd[:], one, ALU.mult))
                        step(nc.vector.tensor_tensor(pd[:], pd[:], xb[q][:, :, C_P1], ALU.add))
                        step(nc.vector.tensor_tensor(ti[:], ti[:], used, ALU.mult))
                        step(nc.vector.scalar_tensor_tensor(pw[:], pd[:], 0.5, used, ALU.mult, ALU.mult))
                        step(nc.vector.tensor_tensor(ids[q][:], ti[:], spare[:], ALU.add))
                        step.end()

                    def weighted(e, q, cc):
                        t0, n = CHUNKS[cc]
                        c = NC * e + cc
                        par = (cc + NC * q) % 2
                        dve.wait_ge(y_full, c + 1)
                        y = ys[q][:, t0:t0 + n, :]
                        nc.vector.tensor_tensor(y, y_bank[par][:, 0:n * P].rearrange("p (t d) -> p t d", d=D),
                                                bpj[q][:, None, :].broadcast_to([P, n, D]), ALU.add).then_inc(y_done, 1)
                        dve.wait_ge(y_done, c + 1)
                        nc.vector.tensor_tensor(y, y, pw[:, t0:t0 + n, None].broadcast_to([P, n, D]),
                                                ALU.mult).then_inc(y_ready, 1)

                    def expert(e, q, use, more):
                        numbers(e, q, use)
                        dve.wait_ge(w_ld[q], 48 * use + 48)
                        weighted(e, q, 0)
                        weighted(e, q, 1)
                        if more:
                            for g in range(NC):
                                turned(e + 1, 1 - q, g)
                        weighted(e, q, 2)

                    for g in range(NC):
                        turned(0, 0, g)
                    expert(0, 0, 0, True)
                    expert(1, 1, 0, True)
                    with nc.vector.Fori(1, E // 2 - 1) as h:
                        expert(2 * h, 0, h, True)
                        expert(2 * h + 1, 1, h, True)
                    expert(E - 2, 0, E // 2 - 1, True)
                    expert(E - 1, 1, E // 2 - 1, False)

                @block.gpsimd
                def _(pool):
                    def send(h, q):
                        e = 2 * h + q
                        wait_apart(pool, added, e * CT * 16)
                        for cc, (t0, n) in enumerate(CHUNKS):
                            wait_apart(pool, y_ready, NC * e + cc + 1)
                            for t in range(t0, t0 + n):
                                nc.gpsimd.indirect_dma_start(
                                    dest[:, :], bass.IndirectOffsetOnAxis(ap=ids[q][:, t:t + 1], axis=0),
                                    ys[q][:, t, :], None, compute_op=ALU.add).then_inc(added, 16)

                    pairs(nc.gpsimd, E // 2, send)
                    wait_apart(pool, added, E * CT * 16)

        experts(1, mid, False)

        a_full, a_done, masked, pv_done, o_done, c_full, c_evac, parts_ok, v_copied, v_ready = (
            sem(n) for n in ("a_full", "a_done", "masked", "pv_done", "o_done", "c_full", "c_evac", "parts_ok",
                             "v_copied", "v_ready"))
        st_full = [sem(f"st_full{i}") for i in range(2)]
        exp_done = [sem(f"exp_done{i}") for i in range(2)]
        qa_ld = [sem(f"qa_ld{i}") for i in range(2)]
        qb_ld = [sem(f"qb_ld{i}") for i in range(2)]
        kp_ld = [sem(f"kp_ld{i}") for i in range(NG)]
        max_ld = [[sem(f"max_ld{hf}{i}") for i in range(2)] for hf in range(2)]
        max_st, x1_ld, x2_ld, x2_st, x2_bias, stack_st = (
            sem(n) for n in ("max_st", "x1_ld", "x2_ld", "x2_st", "x2_bias", "stack_st"))
        n_stat, n_rstd, n_done, n_chain, part_one, rest_ok, split_ok, cleared, p_chain, v_ones, ctx_chain, win2 = (
            sem(n) for n in ("n_stat", "n_rstd", "n_done", "n_chain", "part_one", "rest_ok", "split_ok", "cleared",
                             "p_chain", "v_ones", "ctx_chain", "win2"))
        later_ok = sem("later_ok")
        with ExitStack() as part:
            sba = maker(part)
            qa = [sba(f"qa{i}", [P, HS, S], bf16) for i in range(2)]
            qb = [sba(f"qb{i}", [P, HS, S], bf16) for i in range(2)]
            kp = [sba(f"kp{i}", [P, HS // 2, S], bf16) for i in range(NG)]
            pt = [sba(f"pt{i}", [P, HS, 512]) for i in range(3)]
            v_all = sba("v_all", [P, B * T, NH, DH + 1])
            vs = [sba(f"vs{i}", [P, T, HS, VW]) for i in range(2)]
            o_sb = sba("o_sb", [P, S])
            ctx = sba("ctx", [P, T, D])
            ctxT = sba("ctxT", [P, S])
            x1 = sba("x1", [P, T, D])
            xn = sba("xn", [P, T, D])
            xnT = sba("xnT", [P, S])
            x2 = sba("x2", [P, T, D])
            parts = [[sba(f"{n}{j}", [P, S], bf16) for j in range(3)] for n in ("qp", "kq")]
            rest = sba("rest", [P, 2, 512])
            n_st = sba("n_st", [P, T, 6])
            n_mv = sba("n_mv", [P, T, 2])
            n_var = sba("n_var", [P, T])
            n_rs = sba("n_rs", [P, T])
            dump = sba("dump", [P, 4, 512], bf16)
            m_diag = sba("m_diag", [P, HS, T])
            m_first = sba("m_first", [P, HS, T // 2])
            m_neg = sba("m_neg", [P, HS, T // 2])
            m_parts = [sba(f"m_parts{i}", [P, 3, HS, T // 2], bf16) for i in range(2)]
            MR = 3 * HS * T // 2
            m_rows = [sba(f"m_rows{i}", [MR, P], bf16) for i in range(2)]
            recip = sba("recip", [P, T // 2, HS])
            block = part.enter_context(nc.Block())
            a_bank, o_bank, c_bank = bank[4:6], bank[6], bank[7]
            m_bank = c_bank.bitcast(bf16)
            two = two_banks[0:2]

            def use_of(uses, base):
                return {name: base + i for i, name in enumerate(uses)}

            class Batch:
                def __init__(self, b, kind):
                    self.b, self.kind = b, kind
                    self.first, self.final = kind == "first", kind == "final"
                    uses = {"first": FIRST_USES, "mid": MID_USES, "final": LAST_USES}[kind]
                    if self.first:
                        base = len(PRO)
                    else:
                        base = len(PRO) + len(FIRST_USES) + (b - 1) * len(MID_USES)
                    self.at = {name: base + i for i, name in enumerate(uses)}

            pro_at = {name: i for i, name in enumerate(PRO)}
            tail_at = {name: TAIL_AT + i for i, name in enumerate(TAIL)}

            def sweep(eng, step):
                for g in range(NG):
                    step(Batch(0, "first"), g)
                with eng.Fori(1, B - 1) as b:
                    for g in range(NG):
                        step(Batch(b, "mid"), g)
                for g in range(NG):
                    step(Batch(B - 1, "final"), g)

            R2_USE = B // 2

            LOADS = 2 * 16
            STORES = 2 * (KS // DH) * 16

            @block.sync
            def _(sp):
                def load_stack(dst, stack, b, g, done):
                    src = stack[bass.ds(b * NH * KS + g * HS * KS, HS * KS), :].rearrange("(i s r) n -> s r i n", s=2, r=KS)
                    for s in range(2):
                        sp.dma_start(dst(s), src[s]).then_inc(done, 16)

                def load_q(dst, b, g, done):
                    load_stack(lambda s: dst[64 * s:64 * s + KS].rearrange("p (i s) n -> p s i n", s=2)[:, s],
                               q_stack, b, g, done)

                def load_k(b, g):
                    load_stack(lambda s: kp[g][64 * s:64 * s + KS], k_stack, b, g, kp_ld[g])

                def step(bt, g):
                    b, at = bt.b, bt.at
                    n, p = NG * b + g, g % 2
                    more = not (bt.final and g == NG - 1)
                    if more:
                        wait_apart(sp, st_full[1], NU * n)
                        nb, ng = (b, g + 1) if g < NG - 1 else (b + 1, 0)
                        load_q(qb[1 - p], nb, ng, qb_ld[1 - p])
                    move(at[("max0", g)], 0, b, g, 2 * n + 1)
                    if g == 0:
                        if not bt.final:
                            wait_apart(sp, n_done, b + 1)
                            sp.dma_start(x1[:], mid[bass.ds((b + 1) * S, S), :].rearrange("(t p) d -> p t d", p=P)
                                         ).then_inc(x1_ld, 16)
                        if not bt.first:
                            wait_apart(sp, r_rows, B + b - 1)
                            sp.dma_start(x2[:], mid[bass.ds((b - 1) * S, S), :].rearrange("(t p) d -> p t d", p=P)
                                         ).then_inc(x2_ld, 16)
                    if g == 1 and not bt.first:
                        store_x2(at, b - 1)
                    if g == 2 and not bt.first:
                        wait_apart(sp, x2_st, 16 * b)
                    if g == 2 and not bt.final:
                        store_stacks(b + 1)
                    if not (bt.final and g >= 2):
                        nb, ng = (b, g + 2) if g < 2 else (b + 1, g - 2)
                        if g >= 2:
                            wait_apart(sp, stack_st, STORES * (b + 2))
                        load_q(qa[p], nb, ng, qa_ld[p])
                        load_k(nb, ng)
                    if more:
                        nb, ng = (b, g + 1) if g < NG - 1 else (b + 1, 0)
                        move(at[("max1", g + 1)], 1, nb, ng, 2 * n + 2)

                def move(use, hf, b, g, k):
                    par = g % 2
                    wait_apart(sp, c_evac, use + 1)
                    wait_apart(sp, max_ld[hf][1 - par], 32 * (2 * b + (g + 1) // 2))
                    flat = max_rows.rearrange("r (t q) -> (r t) q", q=P)
                    sp.dma_start(flat[hf * MR:(hf + 1) * MR, :], m_rows[hf][:]).then_inc(max_st, 16)
                    wait_apart(sp, max_st, 16 * (k + 1))
                    for s in range(2):
                        src = max_rows[hf * 3 * HS:(hf + 1) * 3 * HS, :].rearrange("(c i s) n -> s c i n", c=3, s=2)[s]
                        dst = qb[par][64 * s + KS:64 * s + KS + 3].rearrange("p (i s) n -> p s i n", s=2)[:, s, :,
                                                                            hf * HALF:(hf + 1) * HALF]
                        sp.dma_start(dst, src).then_inc(max_ld[hf][par], 16)

                def store_stacks(b):
                    wait_apart(sp, split_ok, 4 * (b + 1))
                    for stack, tiles, order in ((q_stack, parts[0], Q_PART), (k_stack, parts[1], K_PART)):
                        for c, j in enumerate(order):
                            dst = stack[bass.ds(b * NH * KS, NH * KS), :].rearrange("(h c d) n -> c h d n", h=NH, d=DH)[c]
                            sp.dma_start(dst, tiles[j][:]).then_inc(stack_st, 16)

                def store_x2(at, b):
                    wait_apart(sp, c_evac, at["o_p1"] + 1)
                    sp.dma_start(last[bass.ds(b * S, S), :].rearrange("(t p) d -> p t d", p=P), x2[:]).then_inc(x2_st, 16)

                sp.dma_start(x1[:], mid[0:S, :].rearrange("(t p) d -> p t d", p=P)).then_inc(x1_ld, 16)
                store_stacks(0)
                wait_apart(sp, stack_st, STORES)
                wait_apart(sp, cleared, 2)
                load_q(qa[0], 0, 0, qa_ld[0])
                load_k(0, 0)
                load_q(qb[0], 0, 0, qb_ld[0])
                load_q(qa[1], 0, 1, qa_ld[1])
                load_k(0, 1)
                move(pro_at[("max1", 0)], 1, 0, 0, 0)
                sweep(nc.sync, step)
                b = B - 1
                wait_apart(sp, r_rows, B + b)
                sp.dma_start(x2[:], mid[b * S:(b + 1) * S, :].rearrange("(t p) d -> p t d", p=P)).then_inc(x2_ld, 16)
                store_x2(tail_at, b)
                wait_apart(sp, x2_st, 16 * B)

            @block.tensor
            def _(pe):
                def score(par, g, b, n, u, pair):
                    hf, kb = UNITS[u]
                    q0, w = unit_queries(u)
                    wait(pe, exp_done[pair], NU * n + u)
                    for s in range(2):
                        i = nc.tensor.matmul(two[pair][:, s, 0:w], kp[g][:, pair, kb * P:(kb + 1) * P],
                                             qb[par][:, 2 * pair + s, q0:q0 + w], start=True, stop=True)
                    i.then_inc(st_full[pair], 1)

                def maxima(n, g, b, a0, a1):
                    par = g % 2
                    for a in range(a0, a1):
                        h, qt, k0, w, diag = AUNITS[a]
                        if a == 0:
                            pe.wait_ge(qa_ld[par], LOADS * uses_of(b, g))
                            pe.wait_ge(kp_ld[g], LOADS * (b + 1))
                        wait(pe, a_done, NA * n + a - 1)
                        nc.tensor.matmul(a_bank[a % 2][:, 0:w], qa[par][:, h, qt * P:(qt + 1) * P],
                                         kp[g][:, h // 2, k0:k0 + w], start=True, stop=True).then_inc(a_full, 1)

                def uses_of(b, g):
                    return 2 * b + g // 2 + 1

                def values(par, n, u):
                    hf, kb = UNITS[u]
                    q0, w = unit_queries(u)
                    if u in (0, T):
                        wait(pe, o_done, 2 * n + u // T)
                        if u == 0:
                            pe.wait_ge(v_copied, n + 1)
                    if u in MASKED:
                        pe.wait_ge(masked, len(MASKED) * n + MASKED.index(u) + 1)
                    else:
                        pe.wait_ge(exp_done[1], NU * n + u + 1)
                    for h in range(HS):
                        i = nc.tensor.matmul(o_bank[VW * h:VW * h + VW, q0 - hf * HALF:q0 - hf * HALF + w],
                                             vs[par][:, kb, h, :], pt[u % 3][:, h, 0:w],
                                             start=u in (0, T), stop=u in (T - 1, NU - 1))
                    i.then_inc(pv_done, 1)

                def bank_free(use):
                    wait(pe, c_evac, use)

                def max_rows_of(use, n, hf):
                    bank_free(use)
                    wait_apart(pe, parts_ok, 2 * n + (1 if hf else 2))
                    nc.tensor.transpose(m_bank[0:MR, 0:P], m_parts[hf][:].rearrange("p c h t -> p (c h t)"),
                                        identb[:]).then_inc(c_full, 1)

                def turn(use, src, half):
                    bank_free(use)
                    for t in range(4):
                        i = nc.tensor.transpose(c_bank[:, t * P:(t + 1) * P], src(4 * half + t), ident[:])
                    i.then_inc(c_full, 1)

                def context(use, n, hf):
                    pe.wait_ge(o_done, 2 * n + (1 if hf else 2))
                    turn(use, lambda t: o_sb[:, t * P:(t + 1) * P], hf)

                def project(use, w, half):
                    bank_free(use)
                    nc.tensor.matmul(c_bank, w[:], xnT[:, half * 512:half * 512 + 512], start=True,
                                     stop=True).then_inc(c_full, 1)

                def by_token(use, srcT, w, half):
                    bank_free(use)
                    for t in range(4):
                        c = (4 * half + t) * P
                        i = nc.tensor.matmul(c_bank[:, t * P:(t + 1) * P], srcT[:, c:c + P], w[:], start=True, stop=True)
                    i.then_inc(c_full, 1)

                def norm_task(at, name, b):
                    if name == "x_t0":
                        pe.wait_ge(n_done, b + 1)
                    if name in ("x_t0", "x_t1"):
                        turn(at[name], lambda t: xn[:, t, :], int(name[-1]))
                    elif name[0] in "qk":
                        project(at[name], wqT if name[0] == "q" else wkT, int(name[-1]))
                    else:
                        by_token(at[name], xnT, wvT, int(name[-1]))

                def out_task(at, name, call):
                    if name in ("o_t0", "o_t1"):
                        turn(at[name], lambda t: ctx[:, t, :], int(name[-1]))
                    elif name in ("o_p0", "o_p1"):
                        by_token(at[name], ctxT, woT, int(name[-1]))
                    elif name in ("r_t0", "r_t1"):
                        bank_free(at[name])
                        router_transpose(pe, call, 0, int(name[-1]), c_bank, c_full)
                    elif name == "r_lg":
                        bank_free(at[name])
                        router_logits(pe, c_bank, c_full)
                    else:
                        bank_free(at[name])
                        router_ranks(pe, call, c_bank, c_full)

                def step(bt, g):
                    b, at = bt.b, bt.at
                    n, par = NG * b + g, g % 2
                    more = not (bt.final and g == NG - 1)
                    nb, ng = (b, g + 1) if g < NG - 1 else (b + 1, 0)
                    pe.wait_ge(qb_ld[par], LOADS * uses_of(b, g))
                    for u in range(NU):
                        if u == 0:
                            pe.wait_ge(max_ld[1][par], 32 * uses_of(b, g))
                        if u == T:
                            pe.wait_ge(max_ld[0][par], 32 * uses_of(b, g))
                        mid_a = (A_FROM[u] + A_FROM[u + 1]) // 2
                        score(par, g, b, n, u, 0)
                        if more:
                            maxima(n + 1, ng, nb, A_FROM[u], mid_a)
                        score(par, g, b, n, u, 1)
                        if more:
                            maxima(n + 1, ng, nb, mid_a, A_FROM[u + 1])
                        if u > 0:
                            values(par, n, u - 1)
                        if u == 1:
                            max_rows_of(at[("max0", g)], n, 0)
                        if u == 2 and ("ctx0", g - 1) in at:
                            context(at[("ctx0", g - 1)], n - 1, 0)
                        if g == 0 and not bt.first and 3 <= u <= 6:
                            out_task(at, ("o_t0", "o_t1", "o_p0", "o_p1")[u - 3], B + b - 1)
                        if g == 1 and not bt.final and 3 <= u <= 7:
                            norm_task(at, ("x_t0", "x_t1", "q0", "q1", "k0")[u - 3], b + 1)
                        if g == 2 and not bt.final and 3 <= u <= 4:
                            norm_task(at, ("v0", "v1")[u - 3], b + 1)
                        if g == 2 and not bt.first and 5 <= u <= 7:
                            out_task(at, ("r_t0", "r_t1", "r_lg")[u - 5], B + b - 1)
                        if u == U_MA and more:
                            max_rows_of(at[("max1", g + 1)], n + 1, 1)
                        if u == 9 and g == 1 and not bt.final:
                            norm_task(at, "k1", b + 1)
                        if u == 9 and g == 2 and not bt.first:
                            out_task(at, "r_rk", B + b - 1)
                        if u == 10:
                            context(at[("ctx1", g)], n, 1)
                    values(par, n, NU - 1)

                for name in PRO[:-1]:
                    norm_task(pro_at, name, 0)
                pe.wait_ge(cleared, 2)
                maxima(0, 0, 0, 0, NA)
                max_rows_of(pro_at[("max1", 0)], 0, 1)
                sweep(nc.tensor, step)
                context(tail_at[("ctx0", NG - 1)], NG * B - 1, 0)
                for name in TAIL[1:]:
                    out_task(tail_at, name, 2 * B - 1)

            @block.scalar
            def _(act):
                def take(use, dst, src=None):
                    act.wait_ge(c_full, use + 1)
                    nc.scalar.copy(dst, c_bank if src is None else src).then_inc(c_evac, 1)

                def take_max(use, k, hf):
                    wait(act, max_st, 16 * k)
                    take(use, m_rows[hf][:], m_bank[0:MR, 0:P])

                def take_o(n, hf, read):
                    act.wait_ge(pv_done, NU * n + (T if hf else NU))
                    wait(act, c_full, read)
                    nc.scalar.copy(o_sb[:, hf * HALF:(hf + 1) * HALF], o_bank).then_inc(o_done, 1)

                def first_part(use, b, which, half):
                    act.wait_ge(c_full, use + 1)
                    if half == 0:
                        wait(act, stack_st, STORES * b)
                    nc.scalar.activation(parts[which][0][:, half * 512:half * 512 + 512], c_bank, ACT.Identity,
                                         bias=(bq_c, bk_c)[which][:]).then_inc(part_one, 1)

                def norm_task(at, name, b):
                    half = int(name[-1])
                    if name[0] == "x":
                        take(at[name], xnT[:, half * 512:half * 512 + 512])
                    elif name[0] in "qk":
                        first_part(at[name], b, "qk".index(name[0]), half)

                def out_take(at, name):
                    half = int(name[-1])
                    dst = ctxT if name[0] == "o" else xT
                    take(at[name], dst[:, half * 512:half * 512 + 512])

                def step(bt, g):
                    b, at = bt.b, bt.at
                    n = NG * b + g
                    more = not (bt.final and g == NG - 1)
                    for u in range(NU):
                        q0, w = unit_queries(u)
                        for pair in range(2):
                            if pair == 0:
                                wait(act, pv_done, NU * n + u - 2)
                            act.wait_ge(st_full[pair], NU * n + u + 1)
                            nc.scalar.activation(pt[u % 3][:, 2 * pair:2 * pair + 2, 0:w], two[pair][:, :, 0:w], ACT.Exp,
                                                 scale=SCALE).then_inc(exp_done[pair], 1)
                        if u == 0 and not (bt.first and g == 0):
                            take_o(n - 1, 0, at[("max0", g)])
                        if u == 1:
                            take_max(at[("max0", g)], 2 * n + 1, 0)
                        if g == 0 and not bt.first and 3 <= u <= 4:
                            out_take(at, ("o_t0", "o_t1")[u - 3])
                        if g == 1 and not bt.final and 3 <= u <= 7:
                            norm_task(at, ("x_t0", "x_t1", "q0", "q1", "k0")[u - 3], b + 1)
                        if g == 2 and not bt.first and 5 <= u <= 6:
                            out_take(at, ("r_t0", "r_t1")[u - 5])
                        if u == 8:
                            take_o(n, 1, at[("max0", g)] + 1)
                        if u == U_MA and more:
                            take_max(at[("max1", g + 1)], 2 * n + 2, 1)
                        if u == 9 and g == 1 and not bt.final:
                            norm_task(at, "k1", b + 1)
                        if u == 9 and g == 2 and not bt.first:
                            router_exp(act, B + b - 1)

                for name in PRO[:6]:
                    norm_task(pro_at, name, 0)
                take_max(pro_at[("max1", 0)], 0, 1)
                sweep(nc.scalar, step)
                take_o(NG * B - 1, 0, tail_at[("ctx0", NG - 1)])
                for name in ("o_t0", "o_t1", "r_t0", "r_t1"):
                    out_take(tail_at, name)
                router_exp(act, 2 * B - 1)

            @block.vector
            def _(dve):
                def reduce(n, a0, a1):
                    for a in range(a0, a1):
                        h, qt, k0, w, diag = AUNITS[a]
                        if a == 0:
                            wait(dve, parts_ok, 2 * n)
                        (wait_apart if diag else wait)(dve, a_full, NA * n + a + 1)
                        if diag:
                            i = nc.vector.tensor_tensor_reduce(out=dump[:, a % 4, 0:w], in0=a_bank[a % 2][:, 0:w],
                                                               in1=causal[:, 512 - w:512], scale=1.0, scalar=NEG,
                                                               op0=ALU.add, op1=ALU.max,
                                                               accum_out=m_diag[:, h, qt:qt + 1])
                        else:
                            i = nc.vector.tensor_reduce(m_first[:, h, qt - T // 2:qt - T // 2 + 1],
                                                        a_bank[a % 2][:, 0:w], AX.X, ALU.max)
                        i.then_inc(a_done, 1)
                        if a == NA1 - 1:
                            dve.wait_ge(a_done, NA * n + NA1)
                            nc.vector.tensor_tensor(m_first[:], m_first[:], m_diag[:, :, T // 2:T],
                                                    ALU.max).then_inc(later_ok, 1)

                def context(use, n, g, hf):
                    dve.wait_ge(c_full, use + 1)
                    v = c_bank.rearrange("p (t h w) -> p t h w", t=4, h=HS)
                    nc.vector.reciprocal(recip[:], v[:, :, :, DH]).then_inc(ctx_chain, 1)
                    dve.wait_ge(ctx_chain, 2 * n + (1 if hf else 2))
                    nc.vector.tensor_tensor(
                        ctx[:, 4 * hf:4 * hf + 4, g * HS * DH:(g + 1) * HS * DH].rearrange("p t (h d) -> p t h d", h=HS),
                        v[:, :, :, 0:DH], recip[:, :, :, None].broadcast_to([P, 4, HS, DH]), ALU.mult).then_inc(c_evac, 1)

                def stats(b):
                    dve.wait_ge(x1_ld, 16 * (b + 1))
                    for t in range(T):
                        i = nc.vector.bn_stats(n_st[:, t, :], x1[:, t, :])
                    i.then_inc(n_chain, 1)
                    wait_apart(dve, n_chain, 2 * b + 1)
                    for t in range(T):
                        i = nc.vector.bn_aggr(n_mv[:, t, :], n_st[:, t, :])
                    i.then_inc(n_chain, 1)
                    dve.wait_ge(n_chain, 2 * b + 2)
                    nc.vector.tensor_scalar(n_var[:], n_mv[:, :, 1], EPS, None, ALU.add).then_inc(n_stat, 1)

                def norm(b):
                    dve.wait_ge(n_rstd, b + 1)
                    for t in range(T):
                        i = nc.vector.tensor_scalar(xn[:, t, :], x1[:, t, :], n_mv[:, t, 0:1], n_rs[:, t:t + 1],
                                                    ALU.subtract, ALU.mult)
                    i.then_inc(n_done, 1)

                def remainder(use, b, which, half):
                    k = 4 * b + 2 * which + half
                    dve.wait_ge(part_one, k + 1)
                    wait(dve, split_ok, k - 1)
                    nc.vector.scalar_tensor_tensor(rest[:, half, :], c_bank, (bq_c, bk_c)[which][:],
                                                   parts[which][0][:, half * 512:half * 512 + 512],
                                                   ALU.add, ALU.subtract).then_inc(c_evac, 1)

                def norm_task(at, name, b):
                    half = int(name[-1])
                    if name[0] in "qk":
                        remainder(at[name], b, "qk".index(name[0]), half)
                    elif name[0] == "v":
                        dve.wait_ge(c_full, at[name] + 1)
                        nc.vector.tensor_tensor(
                            v_all[:, bass.ds(b * T + 4 * half, 4), :, 0:DH],
                            c_bank.rearrange("p (t h d) -> p t h d", t=4, d=DH),
                            bv_r[:].rearrange("p (h d) -> p h d", d=DH)[:, None, :, :].broadcast_to([P, 4, NH, DH]),
                            ALU.add).then_inc(c_evac, 1)

                def add_out(at, name, b):
                    half = int(name[-1])
                    dve.wait_ge(c_full, at[name] + 1)
                    dve.wait_ge(x2_bias, b + 1)
                    v = x2[:, 4 * half:4 * half + 4, :]
                    nc.vector.tensor_tensor(v, c_bank.rearrange("p (t d) -> p t d", t=4), v, ALU.add).then_inc(c_evac, 1)

                held = {}

                def out_task(at, name, b):
                    call = B + b
                    if name in ("o_p0", "o_p1"):
                        add_out(at, name, b)
                    elif name == "r_lg":
                        dve.wait_ge(c_full, at[name] + 1)
                        held["step"] = router_top2(dve, c_bank, call, c_evac, at[name] + 1)
                    elif name == "r_rk":
                        dve.wait_ge(c_full, at[name] + 1)
                        router_rows(dve, call, 0, c_bank, c_evac, held["step"])

                def step(bt, g):
                    b, at = bt.b, bt.at
                    n = NG * b + g
                    more = not (bt.final and g == NG - 1)
                    for u in range(NU):
                        if more:
                            reduce(n + 1, A_FROM[u], A_FROM[u + 1])
                        if u == 2 and ("ctx0", g - 1) in at:
                            context(at[("ctx0", g - 1)], n - 1, (g - 1) % NG, 0)
                        if g == 0 and not bt.first and 5 <= u <= 6:
                            out_task(at, ("o_p0", "o_p1")[u - 5], b - 1)
                        if g == 0 and not bt.final:
                            if u == 8:
                                stats(b + 1)
                            if u == 11:
                                norm(b + 1)
                        if g == 1 and not bt.final and 5 <= u <= 7:
                            norm_task(at, ("q0", "q1", "k0")[u - 5], b + 1)
                        if g == 1 and not bt.final and u == 9:
                            norm_task(at, "k1", b + 1)
                        if g == 1 and not bt.first:
                            if u == 8:
                                dve.wait_ge(c_evac, at["o_p1"] + 1)
                                router_stats(dve, x2, B + b - 1)
                            if u == 11:
                                router_norm(dve, x2, B + b - 1, 0, b - 1 + R2_USE)
                        if g == 2 and not bt.final and 3 <= u <= 4:
                            norm_task(at, ("v0", "v1")[u - 3], b + 1)
                        if g == 2 and not bt.first and u == 7:
                            out_task(at, "r_lg", b - 1)
                        if g == 2 and not bt.first and u == 9:
                            out_task(at, "r_rk", b - 1)
                        if u == 10:
                            context(at[("ctx1", g)], n, g, 1)

                for t_ in qa + qb:
                    i = nc.vector.memset(t_[:], 0.0)
                i.then_inc(cleared, 1)
                nc.vector.tensor_copy(tok_id[:], tok_id0[:])
                nc.vector.memset(taken[:], 0.0)
                stats(0)
                norm(0)
                for name in PRO[2:8]:
                    norm_task(pro_at, name, 0)
                reduce(0, 0, NA)
                sweep(nc.vector, step)
                b = B - 1
                context(tail_at[("ctx0", NG - 1)], NG * B - 1, NG - 1, 0)
                out_task(tail_at, "o_p0", b)
                out_task(tail_at, "o_p1", b)
                dve.wait_ge(c_evac, tail_at["o_p1"] + 1)
                router_stats(dve, x2, B + b)
                router_norm(dve, x2, B + b, 0, b + R2_USE)
                out_task(tail_at, "r_lg", b)
                out_task(tail_at, "r_rk", b)
                dve.wait_ge(r_chain, 2 * B * ROUTER_STEPS)
                router_windows(dve, win2, 0)

            @block.gpsimd
            def _(pool):
                PART_STEPS = 4

                def split_max(n, hf, k, used):
                    if hf:
                        wait_apart(pool, later_ok, n + 1)
                    else:
                        wait_apart(pool, a_done, NA * n + NA)
                    wait_apart(pool, c_full, used)
                    wait_apart(pool, parts_ok, k)
                    base, c = PART_STEPS * k, [0]

                    def step(i):
                        c[0] += 1
                        i.then_inc(p_chain, 1)
                        wait_apart(pool, p_chain, base + c[0])

                    mp = m_parts[hf]
                    m = m_first[:] if hf else m_diag[:, :, 0:T // 2]
                    step(nc.gpsimd.tensor_scalar(m_neg[:], m, -1.0, None, ALU.mult))
                    step(nc.gpsimd.tensor_copy(mp[:, 0], m_neg[:]))
                    step(nc.gpsimd.tensor_tensor(m_neg[:], m_neg[:], mp[:, 0], ALU.subtract))
                    step(nc.gpsimd.tensor_copy(mp[:, 1], m_neg[:]))
                    nc.gpsimd.tensor_tensor(mp[:, 2], m_neg[:], mp[:, 1], ALU.subtract).then_inc(parts_ok, 1)

                def split(use, b, which, half):
                    k = 4 * b + 2 * which + half
                    s = slice(half * 512, half * 512 + 512)
                    wait_apart(pool, c_evac, use + 1)
                    nc.gpsimd.tensor_copy(parts[which][1][:, s], rest[:, half, :]).then_inc(rest_ok, 1)
                    wait_apart(pool, rest_ok, k + 1)
                    nc.gpsimd.tensor_tensor(parts[which][2][:, s], rest[:, half, :], parts[which][1][:, s],
                                            ALU.subtract).then_inc(split_ok, 1)

                def copy_v(b, g, n, ready):
                    wait_apart(pool, pv_done, NU * (n - 1))
                    if g == 0:
                        wait_apart(pool, c_evac, ready)
                    nc.gpsimd.tensor_copy(vs[g % 2][:, :, :, 0:DH + 1],
                                          v_all[:, bass.ds(b * T, T), g * HS:(g + 1) * HS, :]).then_inc(v_copied, 1)

                def mask(n, u):
                    wait_apart(pool, exp_done[1], NU * n + u + 1)
                    v = pt[u % 3][:, :, 0:P]
                    nc.gpsimd.affine_select(out=v, in_=v, compare_op=ALU.is_ge, fill=0.0, base=0,
                                            pattern=[[0, HS], [1, P]], channel_multiplier=-1).then_inc(masked, 1)

                def rstd1(b):
                    wait_apart(pool, n_stat, b + 1)
                    nc.gpsimd.tensor_tensor(n_rs[:], n_var[:], half_neg[:], ALU.pow).then_inc(n_rstd, 1)

                def bias_x2(b):
                    wait_apart(pool, x2_ld, 16 * (b + 1))
                    nc.gpsimd.tensor_tensor(x2[:], x2[:], bo_r[:, None, :].broadcast_to([P, T, D]), ALU.add).then_inc(x2_bias, 1)

                def step(bt, g):
                    b, at = bt.b, bt.at
                    n = NG * b + g
                    more = not (bt.final and g == NG - 1)
                    nb, ng = (b, g + 1) if g < NG - 1 else (b + 1, 0)
                    for u in range(NU):
                        if u == 0 and more:
                            copy_v(nb, ng, n + 1, at[("max0", g)])
                        if u in MASKED:
                            mask(n, u)
                        if g == 0 and not bt.first and u == 4:
                            bias_x2(b - 1)
                        if g == 0 and not bt.final and u == 9:
                            rstd1(b + 1)
                        if g == 1 and not bt.final and u in (6, 7, 8, 10):
                            k = (6, 7, 8, 10).index(u)
                            split(at[("q0", "q1", "k0", "k1")[k]], b + 1, k // 2, k % 2)
                        if g == 1 and not bt.first and u == 9:
                            router_rstd(pool, B + b - 1)
                        if g == 3 and not bt.first:
                            if u == 0:
                                wait_apart(pool, r_idx, B + b)
                            for k in ((2 * u, 2 * u + 1) if u < 4 else (u + 4,)):
                                router_scatter(pool, 0, k)
                        if u == 7 and more:
                            split_max(n + 1, 1, 2 * n + 2, at[("max0", g)] + 1)
                        if u == NU - 1 and more:
                            split_max(n + 1, 0, 2 * n + 3, at[("max1", g + 1)] + 1)

                for t_ in kp:
                    i = nc.gpsimd.memset(t_[:], 1.0)
                i.then_inc(cleared, 1)
                for t_ in vs:
                    nc.gpsimd.memset(t_[:], 0.0)
                nc.gpsimd.memset(v_all[:, :, :, DH], 1.0).then_inc(v_ones, 1)
                rstd1(0)
                for k in range(4):
                    split(pro_at[("q0", "q1", "k0", "k1")[k]], 0, k // 2, k % 2)
                wait_apart(pool, v_ones, 1)
                copy_v(0, 0, 0, pro_at["v1"] + 1)
                split_max(0, 1, 0, 0)
                split_max(0, 0, 1, 0)
                sweep(nc.gpsimd, step)
                b = B - 1
                bias_x2(b)
                router_rstd(pool, B + b)
                wait_apart(pool, r_idx, 2 * B)
                for k in range(TOPK * T):
                    router_scatter(pool, 0, k)
                wait_apart(pool, scattered[0], (R2_USE + B) * 16 * TOPK * T)

        experts(2, last, True)


_INS = ["L0_attn_x", "L0_attn_wq", "L0_attn_bq", "L0_attn_wk", "L0_attn_bk", "L0_attn_wv", "L0_attn_bv", "L0_attn_wo",
        "L0_attn_bo", "L0_ffn_gate_w", "L0_ffn_c_fc", "L0_ffn_fc_bias", "L0_ffn_c_proj", "L0_ffn_proj_bias"]
_OUTS = [((4, 1024, 128), "float32")]


def kernel(**inputs):
    import numpy as _np
    import concourse.bacc as _bacc
    from concourse import mybir as _mybir
    from concourse.bass_utils import run_bass_kernel_spmd as _run

    nc = _bacc.Bacc("TRN2", target_bir_lowering=False, num_devices=1)
    arrays, args = {}, []
    for name in _INS:
        a = _np.ascontiguousarray(inputs[name])
        arrays[f"in_{name}_dram"] = a
        args.append(nc.dram_tensor(f"in_{name}_dram", a.shape, _mybir.dt.from_np(a.dtype), kind="ExternalInput").ap())
    for i, (shape, dtype) in enumerate(_OUTS):
        dt = _mybir.dt.from_np(_np.dtype(dtype))
        args.append(nc.dram_tensor(f"out_{i}_dram", shape, dt, kind="ExternalOutput").ap())
    macaron_block_kernel(nc, *args)
    r = _run(nc, [arrays], core_ids=[0])
    got = tuple(r.results[0][f"out_{i}_dram"] for i in range(len(_OUTS)))
    return got[0]
```

```python
import concourse.bass as bass
from concourse import mybir
from contextlib import ExitStack


def macaron_block_kernel(nc, x, wq, bq, wk, bk, wv, bv, wo, bo, gate_w, c_fc, fc_bias, c_proj, proj_bias, out):
    f32, bf16, i32 = mybir.dt.float32, mybir.dt.bfloat16, mybir.dt.int32
    ALU, ACT, AX = mybir.AluOpType, mybir.ActivationFunctionType, mybir.AxisListType

    P = 128
    B, S, D = x.shape
    N = B * S
    E, _, F = c_fc.shape
    FB = F // P
    T = S // P
    NH, DH = 16, D // 16
    TOPK = 2
    CAP = int(1.25 * N * TOPK / E)
    CT = CAP // P
    EPS = 1e-5
    NEG = -3.0e38
    ROW = D + 4
    C_ID, C_P0, C_P1 = D, D + 1, D + 2
    SKIP = 1.0e6

    HS = 4
    NG = NH // HS
    Q_PART = [0, 0, 0, 1, 1, 2]
    K_PART = [0, 1, 2, 0, 1, 0]
    KS = len(Q_PART) * DH
    HALF = S // 2
    SCALE = float(DH) ** -0.5
    VW = 32

    UNITS = [(1, k) for k in range(T)] + [(0, k) for k in range(T // 2)]
    NU = len(UNITS)

    def unit_queries(u):
        hf, kb = UNITS[u]
        q0 = max(hf * HALF, kb * P)
        return q0, (hf + 1) * HALF - q0

    MASKED = [u for u in range(NU) if UNITS[u][1] * P >= UNITS[u][0] * HALF]
    AUNITS = []
    for hf in (1, 0):
        for qt in range(hf * T // 2, (hf + 1) * T // 2):
            for j in range(qt // 2):
                AUNITS += [(qt, (0, 1), 2 * j * P, 2 * P, False, j), (qt, (2, 3), 2 * j * P, 2 * P, False, j)]
            if qt % 2:
                AUNITS.append((qt, range(HS), (qt - 1) * P, P, False, T // 2 - 1))
            AUNITS.append((qt, range(HS), qt * P, P, True, T // 2))
        if hf:
            NA1 = len(AUNITS)
    NA = len(AUNITS)
    A_IN_SLOT = [4, 4, 4, 4, 4, 3, 2, 1, 4, 3, 2, 1]
    assert sum(A_IN_SLOT) == NA and sum(A_IN_SLOT[:8]) >= NA1
    A_FROM = [sum(A_IN_SLOT[:u]) for u in range(NU + 1)]
    LAG = 2
    PTS = LAG + 2
    U_MA = 8

    def bank_uses(first, final):
        uses = []
        for g in range(NG):
            uses.append(("max0", g))
            if not (first and g == 0):
                uses.append(("ctx0", g - 1))
            if g == 0 and not first:
                uses += ["o_t0", "o_t1", "o_p0", "o_p1"]
            if g == 1 and not final:
                uses += ["x_t0", "x_t1", "q0", "q1", "k0"]
            if g == 2:
                if not first:
                    uses += ["r_t0", "r_t1", "r_lg"]
                if not final:
                    uses += ["v0", "v1"]
            if not (final and g == NG - 1):
                uses.append(("max1", g + 1))
            if g == 1 and not final:
                uses.append("k1")
            if g == 2 and not first:
                uses.append("r_rk")
            uses.append(("ctx1", g))
        return uses

    PRO = ["x_t0", "x_t1", "q0", "q1", "k0", "k1", "v0", "v1", ("max1", 0)]
    FIRST_USES, MID_USES, LAST_USES = bank_uses(True, False), bank_uses(False, False), bank_uses(False, True)
    TAIL = [("ctx0", NG - 1), "o_t0", "o_t1", "o_p0", "o_p1", "r_t0", "r_t1", "r_lg", "r_rk"]
    TAIL_AT = len(PRO) + len(FIRST_USES) + (B - 2) * len(MID_USES) + len(LAST_USES)

    xf = x.rearrange("b s d -> (b s) d")
    bucket = nc.dram_tensor("bucket", [E * 2 * CAP, ROW], f32, kind="Internal").ap()
    mid = nc.dram_tensor("mid", [N + CAP, D], f32, kind="Internal").ap()
    last = nc.dram_tensor("last", [N + CAP, D], f32, kind="Internal").ap()
    q_stack = nc.dram_tensor("q_stack", [B * NH * KS, S], bf16, kind="Internal").ap()
    k_stack = nc.dram_tensor("k_stack", [B * NH * KS, S], bf16, kind="Internal").ap()
    max_rows = nc.dram_tensor("max_rows", [2 * 3 * HS, HALF], bf16, kind="Internal").ap()

    whole = ExitStack()
    with whole:
        def maker(stack):
            def make(name, shape, dt=f32):
                return stack.enter_context(nc.sbuf_tensor(name, shape, dt))
            return make

        def sem(name):
            return whole.enter_context(nc.semaphore(name))

        sb = maker(whole)
        two_banks = [whole.enter_context(nc.psum_tensor(f"banks{i}", [P, 2, 512], f32)) for i in range(4)]
        bank = [two_banks[i // 2][:, i % 2, :] for i in range(8)]

        ident = sb("ident", [P, P])
        identb = sb("identb", [P, P], bf16)
        before = sb("before", [P, P], bf16)
        onesb = sb("onesb", [P, P], bf16)
        onesf = sb("onesf", [P, P])
        gate = sb("gate", [P, E])
        place = sb("place", [P, T, E])
        half_neg = sb("half_neg", [P, T])
        tok_id0 = sb("tok_id0", [P, T])
        tok_id = sb("tok_id", [P, T])
        slot_of = sb("slot_of", [P, CT])
        spare = sb("spare", [P, CT])
        sign = sb("sign", [P, T, TOPK])
        slot0 = sb("slot0", [P, T, TOPK])
        taken = sb("taken", [P, TOPK, E])
        firsts = sb("firsts", [P, E])
        total = sb("total", [P, E])
        is_first = sb("is_first", [P, E, CT])
        is_used = sb("is_used", [P, E, CT])
        window = sb("window", [P, E], i32)
        e_base = sb("e_base", [P, E])
        iota_i = sb("iota_i", [P, 64], i32)
        wqT, wkT, wvT, woT = (sb(n, [P, P]) for n in ("wqT", "wkT", "wvT", "woT"))
        bq_c, bk_c = sb("bq_c", [P, 1]), sb("bk_c", [P, 1])
        bv_r, bo_r = sb("bv_r", [P, P]), sb("bo_r", [P, P])
        bias_up = sb("bias_up", [P, E * FB])
        causal = sb("causal", [P, HS, P], bf16)
        rows = [sb(f"rows{i}", [P, T, ROW]) for i in range(2)]
        stat = sb("stat", [P, T, 6])
        mv = sb("mv", [P, T, 2])
        var_e = sb("var_e", [P, T])
        rstd = sb("rstd", [P, T])
        neg_mean = sb("neg_mean", [P, T])
        shift = sb("shift", [P, T])
        xT = sb("xT", [P, S])
        lg = sb("lg", [P, T, E])
        lg2 = sb("lg2", [P, T, E])
        eq = sb("eq", [P, T, E])
        cand = sb("cand", [P, T, E])
        top = sb("top", [P, T, TOPK])
        chosen = sb("chosen", [P, T, TOPK])
        hot = sb("hot", [P, T, TOPK, E], bf16)
        gap = sb("gap", [P, T])
        eg = sb("eg", [P, T])
        es = sb("es", [P, T])
        ranks = sb("ranks", [P, T, TOPK, E])
        rank = sb("rank", [P, T, TOPK])
        over = sb("over", [P, T, TOPK])
        place_in = sb("place_in", [P, T, TOPK])
        row_ix = [sb(f"row_ix{i}", [P, TOPK, T], i32) for i in range(2)]

        scattered = [sem(f"scattered{i}") for i in range(2)]
        r_stat, r_rstd, r_shift, r_rows, r_hot, r_exp, r_idx, r_chain = (
            sem(n) for n in ("r_stat", "r_rstd", "r_shift", "r_rows", "r_hot", "r_exp", "r_idx", "r_chain"))

        passed = sem("passed")

        def wait(eng, s, n):
            if not (isinstance(n, int) and n <= 0):
                eng.wait_ge(s, n)

        def wait_apart(eng, s, n):
            wait(eng, s, n)
            if not isinstance(n, int):
                eng.sem_inc(passed, 1)

        def pairs(eng, count, body):
            body(0, 0)
            body(0, 1)
            with eng.Fori(1, count) as h:
                body(h, 0)
                body(h, 1)

        class Steps:
            def __init__(self, eng, s, base, total):
                self.eng, self.s, self.base, self.total, self.k = eng, s, base, total, 0

            def __call__(self, ins):
                ins.then_inc(self.s, 1)
                self.k += 1
                self.eng.wait_ge(self.s, self.base + self.k)

            def end(self):
                assert self.k == self.total, (self.k, self.total)

        ROUTER_STEPS = 20

        def router_sums(xin, t0, t1):
            for t in range(t0, t1):
                i = nc.vector.bn_stats(stat[:, t, :], xin[:, t, :])
            if t1 == T:
                i.then_inc(r_chain, 1)

        def router_moments(dve, call):
            wait_apart(dve, r_chain, call * ROUTER_STEPS + 1)
            for t in range(T):
                i = nc.vector.bn_aggr(mv[:, t, :], stat[:, t, :])
            i.then_inc(r_chain, 1)
            dve.wait_ge(r_chain, call * ROUTER_STEPS + 2)
            nc.vector.tensor_scalar(neg_mean[:], mv[:, :, 0], -1.0, None, ALU.mult)
            nc.vector.tensor_scalar(var_e[:], mv[:, :, 1], EPS, None, ALU.add).then_inc(r_stat, 1)

        def router_rstd(pool, call):
            wait_apart(pool, r_stat, call + 1)
            nc.gpsimd.tensor_tensor(rstd[:], var_e[:], half_neg[:], ALU.pow).then_inc(r_rstd, 1)

        def router_shift(pool, k):
            wait_apart(pool, r_rstd, B + k + 1)
            nc.gpsimd.tensor_tensor(shift[:], neg_mean[:], rstd[:], ALU.mult).then_inc(r_shift, 1)

        def router_numbers(dve, buf, use):
            wait(dve, scattered[buf], use * 16 * TOPK * T)
            return nc.vector.tensor_copy(rows[buf][:, :, C_ID], tok_id[:])

        def router_norm(dve, xin, call, buf, use):
            dve.wait_ge(r_rstd, call + 1)
            router_numbers(dve, buf, use)
            for t in range(T):
                i = nc.vector.tensor_scalar(rows[buf][:, t, 0:D], xin[:, t, :], mv[:, t, 0:1], rstd[:, t:t + 1],
                                            ALU.subtract, ALU.mult)
            i.then_inc(r_rows, 1)

        def router_transpose(pe, call, buf, half, tb, full):
            if half == 0:
                pe.wait_ge(r_rows, call + 1)
            for t in range(4):
                i = nc.tensor.transpose(tb[:, t * P:(t + 1) * P], rows[buf][:, 4 * half + t, 0:D], ident[:])
            i.then_inc(full, 1)

        def router_logits(pe, lb, full):
            for t in range(T):
                i = nc.tensor.matmul(lb[:, t * E:(t + 1) * E], xT[:, t * P:(t + 1) * P], gate[:], start=True, stop=True)
            i.then_inc(full, 1)

        def router_top2(dve, lb, call, evac, evac_n):
            step = Steps(dve, r_chain, call * ROUTER_STEPS + 2, ROUTER_STEPS - 2)
            nc.vector.tensor_scalar(tok_id[:], tok_id[:], float(S), None, ALU.add)
            i = nc.vector.tensor_copy(lg[:].rearrange("p t e -> p (t e)"), lb[:, 0:T * E])
            i.then_inc(evac, 1)
            dve.wait_ge(evac, evac_n)
            step(nc.vector.tensor_reduce(top[:, :, 0], lg[:], AX.X, ALU.max))


            def one_hot(l, k):
                wide = top[:, :, k:k + 1].broadcast_to([P, T, E])
                step(nc.vector.tensor_tensor(eq[:], l[:], wide, ALU.is_equal))
                step(nc.vector.tensor_tensor(cand[:], eq[:], place[:], ALU.mult))
                step(nc.vector.tensor_reduce(chosen[:, :, k], cand[:], AX.X, ALU.max))
                return nc.vector.tensor_tensor(hot[:, :, k, :], place[:], chosen[:, :, k:k + 1].broadcast_to([P, T, E]),
                                               ALU.is_equal)
            step(one_hot(lg, 0))
            step(nc.vector.scalar_tensor_tensor(lg2[:], hot[:, :, 0, :], NEG, lg[:], ALU.mult, ALU.add))
            step(nc.vector.tensor_reduce(top[:, :, 1], lg2[:], AX.X, ALU.max))
            one_hot(lg2, 1).then_inc(r_hot, 1)
            nc.vector.tensor_tensor(gap[:], top[:, :, 1], top[:, :, 0], ALU.subtract).then_inc(r_hot, 1)
            return step

        def router_exp(act, call):
            act.wait_ge(r_hot, 2 * call + 2)
            nc.scalar.activation(eg[:], gap[:], ACT.Exp).then_inc(r_exp, 1)

        def router_ranks(pe, call, rb, full):
            pe.wait_ge(r_hot, 2 * call + 1)
            W = TOPK * E
            h = hot[:].rearrange("p t k e -> p (t k e)")
            nc.tensor.matmul(rb[:, 0:T * W], before[:], h, start=True, stop=False)
            for s in range(1, T):
                nc.tensor.matmul(rb[:, s * W:T * W], onesb[:], h[:, 0:(T - s) * W], start=False, stop=s == T - 1)
            for t in range(T):
                i = nc.tensor.matmul(rb[:, T * W:T * W + W], onesb[:], h[:, t * W:(t + 1) * W], start=t == 0, stop=t == T - 1)
            i.then_inc(full, 1)

        def router_rank(rb, evac, step):
            W = TOPK * E
            tk = taken[:].rearrange("p k e -> p (k e)")
            step(nc.vector.tensor_tensor(ranks[:].rearrange("p t k e -> p t (k e)"),
                                         rb[:, 0:T * W].rearrange("p (t w) -> p t w", w=W),
                                         tk[:, None, :].broadcast_to([P, T, W]), ALU.add))
            nc.vector.tensor_tensor(tk, tk, rb[:, T * W:T * W + W], ALU.add).then_inc(evac, 1)
            step(nc.vector.tensor_tensor(ranks[:], ranks[:], hot[:], ALU.mult))
            step(nc.vector.tensor_reduce(rank[:], ranks[:], AX.X, ALU.add))

        def router_rows(dve, call, buf, step):
            nc.vector.tensor_scalar(over[:], rank[:], float(CAP), SKIP, ALU.is_ge, ALU.mult)
            step(nc.vector.tensor_tensor(place_in[:], rank[:], sign[:], ALU.mult))
            step(nc.vector.scalar_tensor_tensor(place_in[:], chosen[:], -2.0 * CAP, place_in[:], ALU.mult, ALU.add))
            step(nc.vector.tensor_tensor(place_in[:], place_in[:], over[:], ALU.add))
            dve.wait_ge(r_exp, call + 1)
            step(nc.vector.tensor_scalar(es[:], eg[:], 1.0, None, ALU.add))
            step(nc.vector.reciprocal(gap[:], es[:]))
            nc.vector.tensor_copy(rows[buf][:, :, C_P0], gap[:])
            nc.vector.tensor_tensor(rows[buf][:, :, C_P1], gap[:], eg[:], ALU.mult)
            nc.vector.tensor_tensor(row_ix[buf][:].rearrange("p k t -> p t k"), place_in[:], slot0[:],
                                    ALU.add).then_inc(r_idx, 1)
            step.end()

        def router_scatter(pool, buf, n):
            k, t = divmod(n, T)
            nc.gpsimd.indirect_dma_start(bucket[:, :], bass.IndirectOffsetOnAxis(ap=row_ix[buf][:, k, t:t + 1], axis=0),
                                         rows[buf][:, t, :], None, bounds_check=E * 2 * CAP - 1,
                                         oob_is_err=False).then_inc(scattered[buf], 16)

        def router_windows(dve, s, at):
            nc.vector.tensor_scalar(firsts[:], taken[:, 0, :], float(CAP), None, ALU.min).then_inc(s, 1)
            dve.wait_ge(s, at + 1)
            nc.vector.tensor_tensor(total[:], firsts[:], taken[:, 1, :], ALU.add)
            nc.vector.tensor_tensor(window[:], e_base[:], firsts[:], ALU.subtract)
            nc.vector.tensor_tensor(is_first[:], slot_of[:, None, :].broadcast_to([P, E, CT]),
                                    firsts[:, :, None].broadcast_to([P, E, CT]), ALU.is_lt).then_inc(s, 1)
            dve.wait_ge(s, at + 2)
            nc.vector.tensor_tensor(is_used[:], slot_of[:, None, :].broadcast_to([P, E, CT]),
                                    total[:, :, None].broadcast_to([P, E, CT]), ALU.is_lt).then_inc(s, 1)

        s_in, s_w, s_gate, s_zero, s_fill, s_copy = (sem(n) for n in ("s_in", "s_w", "s_gate", "s_zero", "s_fill", "s_copy"))
        s_iota, s_const, s_cdve, s_wt, s_wev = (sem(n) for n in ("s_iota", "s_const", "s_cdve", "s_wt", "s_wev"))
        r1_ld = [sem(f"r1_ld{i}") for i in range(2)]
        r1_full, r1_evac, win1 = sem("r1_full"), sem("r1_evac"), sem("win1")
        with ExitStack() as part:
            sb1 = maker(part)
            zero = sb1("zero", [P, 2 * CAP // P * ROW])
            wraw = sb1("wraw", [P, 4, P])
            braw = sb1("braw", [E * FB, P])
            xin = [sb1(f"xin{i}", [P, T, D]) for i in range(2)]
            block = part.enter_context(nc.Block())
            NCONST = 9

            @block.sync
            def _(sp):
                def load(h, buf):
                    wait_apart(sp, r_rows, 2 * h)
                    sp.dma_start(xin[buf][:], xf[bass.ds((2 * h + buf) * S, S), :].rearrange("(t p) d -> p t d", p=P)
                                 ).then_inc(r1_ld[buf], 16)

                pairs(nc.sync, B // 2, load)

            @block.gpsimd
            def _(pool):
                nc.gpsimd.iota(iota_i[:, 0:CT], pattern=[[P, CT]], base=0, channel_multiplier=1)
                nc.gpsimd.iota(iota_i[:, 32:32 + T], pattern=[[P, T]], base=0, channel_multiplier=1)
                nc.gpsimd.iota(iota_i[:, 48:48 + E], pattern=[[-1, E]], base=E, channel_multiplier=0).then_inc(s_iota, 1)
                wait_apart(pool, s_cdve, 1)
                for tile_ in (ident, identb):
                    nc.gpsimd.affine_select(out=tile_[:], in_=tile_[:], compare_op=ALU.not_equal, fill=1.0, base=0,
                                            pattern=[[-1, P]], channel_multiplier=1).then_inc(s_const, 1)
                nc.gpsimd.affine_select(out=before[:], in_=before[:], compare_op=ALU.is_gt, fill=0.0, base=0,
                                        pattern=[[1, P]], channel_multiplier=-1).then_inc(s_const, 1)
                nc.gpsimd.affine_select(out=causal[:], in_=causal[:], compare_op=ALU.is_ge, fill=NEG, base=0,
                                        pattern=[[0, HS], [-1, P]], channel_multiplier=1).then_inc(s_const, 1)

                def scatter(call, buf, more):
                    wait_apart(pool, r_idx, call + 1)
                    for n in range(TOPK * T):
                        router_scatter(pool, buf, n)
                        if n == 3 and more:
                            router_rstd(pool, call + 1)

                router_rstd(pool, 0)
                wait_apart(pool, s_fill, 16 * E)
                scatter(0, 0, True)
                scatter(1, 1, True)
                if B > 4:
                    with nc.gpsimd.Fori(1, B // 2 - 1) as h:
                        scatter(2 * h, 0, True)
                        scatter(2 * h + 1, 1, True)
                scatter(B - 2, 0, True)
                scatter(B - 1, 1, False)
                for buf in range(2):
                    wait_apart(pool, scattered[buf], B // 2 * 16 * TOPK * T)

            @block.vector
            def _(dve):
                nc.vector.memset(ident[:], 0.0)
                nc.vector.memset(identb[:], 0.0)
                nc.vector.memset(before[:], 1.0)
                nc.vector.memset(causal[:], 0.0).then_inc(s_cdve, 1)
                nc.vector.memset(zero[:], 0.0).then_inc(s_zero, 1)
                nc.vector.memset(onesb[:], 1.0)
                nc.vector.memset(onesf[:], 1.0)
                nc.vector.memset(half_neg[:], -0.5)
                nc.vector.memset(taken[:], 0.0)
                for buf in range(2):
                    nc.vector.memset(rows[buf][:, :, D:ROW], 0.0)
                nc.vector.memset(sign[:, :, 0], -1.0)
                nc.vector.memset(sign[:, :, 1], 1.0)
                nc.vector.memset(slot0[:, :, 0], 2.0 * CAP * E + CAP - 1)
                nc.vector.memset(slot0[:, :, 1], 2.0 * CAP * E + CAP)
                dve.wait_ge(s_iota, 1)
                nc.vector.tensor_copy(slot_of[:], iota_i[:, 0:CT])
                nc.vector.tensor_copy(tok_id0[:], iota_i[:, 32:32 + T])
                nc.vector.tensor_copy(tok_id[:], iota_i[:, 32:32 + T])
                nc.vector.tensor_copy(place[:], iota_i[:, None, 48:48 + E].broadcast_to([P, T, E]))
                nc.vector.tensor_scalar(spare[:], iota_i[:, 0:CT], float(N), None, ALU.add)
                nc.vector.tensor_scalar(e_base[:], iota_i[:, 48:48 + E], -2.0 * CAP, 2.0 * CAP * E + CAP, ALU.mult,
                                        ALU.add).then_inc(s_cdve, 1)
                dve.wait_ge(s_cdve, 2)
                def route(h, buf):
                    call = 2 * h + buf
                    dve.wait_ge(r1_ld[buf], 16 * h + 16)
                    router_sums(xin[buf], 0, T)
                    router_moments(dve, call)
                    router_norm(dve, xin[buf], call, buf, h)
                    dve.wait_ge(r1_full, 4 * call + 3)
                    step = router_top2(dve, bank[0], call, r1_evac, 4 * call + 3)
                    dve.wait_ge(r1_full, 4 * call + 4)
                    router_rank(bank[0], r1_evac, step)
                    router_rows(dve, call, buf, step)

                pairs(nc.vector, B // 2, route)
                dve.wait_ge(r_chain, B * ROUTER_STEPS)
                dve.wait_ge(r1_evac, 4 * B)
                router_windows(dve, win1, 0)
                for n, w in enumerate((wqT, wkT, wvT, woT)):
                    dve.wait_ge(s_wt, n + 1)
                    nc.vector.tensor_copy(w[:], bank[1 + n][:, 0:P])
                dve.wait_ge(s_wt, 5)
                nc.vector.tensor_copy(bias_up[:], bank[5][:, 0:E * FB])

            @block.scalar
            def _(act):
                act.dma_start(gate[:], gate_w).then_inc(s_gate, 16)
                act.wait_ge(s_zero, 1)
                for e in range(E):
                    act.dma_start(bucket[e * 2 * CAP:(e + 1) * 2 * CAP, :].rearrange("(p r) c -> p (r c)", p=P),
                                  zero[:]).then_inc(s_fill, 16)
                for n, w in enumerate((wq, wk, wv, wo)):
                    act.dma_start(wraw[:, n, :], w).then_inc(s_w, 16)
                act.dma_start(braw[:], fc_bias.rearrange("e o (b p) -> (e o b) p", p=P)).then_inc(s_w, 16)
                act.dma_start(bq_c[:], bq.rearrange("(p o) -> p o", o=1)).then_inc(s_w, 16)
                act.dma_start(bk_c[:], bk.rearrange("(p o) -> p o", o=1)).then_inc(s_w, 16)
                act.dma_start(bv_r[:], bv.rearrange("(o n) -> o n", o=1).broadcast_to([P, D])).then_inc(s_w, 16)
                act.dma_start(bo_r[:], bo.rearrange("(o n) -> o n", o=1).broadcast_to([P, D])).then_inc(s_w, 16)
                act.dma_start(mid[0:N, :], xf).then_inc(s_copy, 16)
                for dst in (mid, last):
                    act.dma_start(dst[N:N + CAP, :].rearrange("(p r) d -> p (r d)", p=P), zero[:, 0:CT * D]).then_inc(s_copy, 16)
                with nc.scalar.Fori(0, B) as call:
                    for half in range(2):
                        act.wait_ge(r1_full, 4 * call + half + 1)
                        nc.scalar.copy(xT[:, half * 512:half * 512 + 512], bank[0][:]).then_inc(r1_evac, 1)
                    router_exp(act, call)
                act.wait_ge(s_copy, 48)
                act.wait_ge(s_w, 16 * 9)

            @block.tensor
            def _(pe):
                pe.wait_ge(s_const, 4)
                pe.wait_ge(s_gate, 16)
                def route(h, buf):
                    call = 2 * h + buf
                    for half in range(2):
                        wait(pe, r1_evac, 4 * call + half)
                        router_transpose(pe, call, buf, half, bank[0], r1_full)
                    wait(pe, r1_evac, 4 * call + 2)
                    router_logits(pe, bank[0], r1_full)
                    wait(pe, r1_evac, 4 * call + 3)
                    router_ranks(pe, call, bank[0], r1_full)

                pairs(nc.tensor, B // 2, route)
                pe.wait_ge(s_w, 16 * 9)
                for n in range(4):
                    nc.tensor.transpose(bank[1 + n][:, 0:P], wraw[:, n, :], ident[:]).then_inc(s_wt, 1)
                nc.tensor.transpose(bank[5][:, 0:E * FB], braw[:], ident[0:E * FB, 0:E * FB]).then_inc(s_wt, 1)

        CHUNKS = [(0, 4), (4, 4), (8, CT - 8)]
        NC = len(CHUNKS)
        EXPERT_STEPS = 7

        def experts(tag, dest, final):
            rows_ld = [sem(f"rows_ld{tag}{i}") for i in range(2)]
            w_ld = [sem(f"w_ld{tag}{i}") for i in range(2)]
            t_full, t_evac, h_full, h_done, y_full, y_done, y_ready, added, e_chain, e_out = (
                sem(f"{n}{tag}") for n in ("t_full", "t_evac", "h_full", "h_done", "y_full", "y_done", "y_ready",
                                           "added", "e_chain", "e_out"))
            with ExitStack() as part:
                sbe = maker(part)
                xb = [sbe(f"xb{tag}{i}", [P, CT, ROW]) for i in range(2)]
                wfc = [sbe(f"wfc{tag}{i}", [P, F]) for i in range(2)]
                wpj = [sbe(f"wpj{tag}{i}", [P, FB, D]) for i in range(2)]
                bfc = [sbe(f"bfc{tag}{i}", [P, FB]) for i in range(2)]
                bpj = [sbe(f"bpj{tag}{i}", [P, D]) for i in range(2)]
                xbT = [sbe(f"xbT{tag}{i}", [P, CAP]) for i in range(2)]
                hT = [sbe(f"hT{tag}{i}", [P, FB, 512]) for i in range(2)]
                ys = [sbe(f"ys{tag}{i}", [P, CT, D]) for i in range(2)]
                pw = sbe(f"pw{tag}", [P, CT])
                pd = sbe(f"pd{tag}", [P, CT])
                ti = sbe(f"ti{tag}", [P, CT])
                ids = [sbe(f"ids{tag}{i}", [P, CT], i32) for i in range(2)]
                block = part.enter_context(nc.Block())
                t_bank, y_bank, h_bank = bank[0:2], bank[2:4], bank[4:8]

                @block.sync
                def _(sp):
                    def load(h, q):
                        e = 2 * h + q
                        at = nc.sync.value_load(window[0:1, bass.ds(e, 1)], min_val=0, max_val=(2 * E - 1) * CAP)
                        wait_apart(sp, t_full, NC * (e - 1))
                        wait_apart(sp, e_chain, EXPERT_STEPS * (e - 1))
                        sp.dma_start(xb[q][:], bucket[bass.ds(at, CAP), :].rearrange("(t p) c -> p t c", p=P)
                                     ).then_inc(rows_ld[q], 16)
                        wait_apart(sp, y_done, NC * (e - 1))
                        sp.dma_start(wfc[q][:], c_fc.rearrange("e d f -> (e d) f")[bass.ds(e * D, D), :]
                                     ).then_inc(w_ld[q], 16)
                        sp.dma_start(wpj[q][:], c_proj.rearrange("e f d -> (e f) d")[bass.ds(e * F, F), :]
                                     .rearrange("(b p) d -> p b d", p=P)).then_inc(w_ld[q], 16)
                        sp.dma_start(bpj[q][:], proj_bias.rearrange("e o d -> (e o) d")[bass.ds(e, 1), :]
                                     .broadcast_to([P, D])).then_inc(w_ld[q], 16)

                    pairs(nc.sync, E // 2, load)
                    if final:
                        wait_apart(sp, added, E * CT * 16)
                        sp.dma_start(out.rearrange("b s d -> (b s) d"), dest[0:N, :]).then_inc(e_out, 16)
                        wait_apart(sp, e_out, 16)

                @block.tensor
                def _(pe):
                    def transposes(e, q, use):
                        pe.wait_ge(rows_ld[q], 16 * use + 16)
                        for g, (t0, n) in enumerate(CHUNKS):
                            wait(pe, t_evac, NC * e + g - 1)
                            for t in range(n):
                                i = nc.tensor.transpose(t_bank[g % 2 if q == 0 else (g + 1) % 2][:, t * P:(t + 1) * P],
                                                        xb[q][:, t0 + t, 0:D], ident[:])
                            i.then_inc(t_full, 1)

                    def up(c, cc, q, e):
                        t0, n = CHUNKS[cc]
                        pe.wait_ge(t_evac, NC * e + cc + 1)
                        for b in range(FB):
                            wait(pe, h_done, FB * (c - 1) + b + 1)
                            nc.tensor.matmul(h_bank[b][:, 0:n * P], wfc[q][:, b * P:(b + 1) * P],
                                             xbT[q][:, t0 * P:(t0 + n) * P], start=True, stop=True).then_inc(h_full, 1)

                    def down(c, cc, q):
                        t0, n = CHUNKS[cc]
                        par = (cc + NC * q) % 2
                        pe.wait_ge(h_done, FB * (c + 1))
                        wait(pe, y_done, c - 1)
                        for t in range(n):
                            for b in range(FB):
                                i = nc.tensor.matmul(y_bank[par][:, t * P:(t + 1) * P], hT[par][:, b, t * P:(t + 1) * P],
                                                     wpj[q][:, b, :], start=b == 0, stop=b == FB - 1)
                        i.then_inc(y_full, 1)

                    def expert(e, q, use, more):
                        c = NC * e
                        pe.wait_ge(w_ld[q], 48 * use + 48)
                        up(c, 0, q, e)
                        up(c + 1, 1, q, e)
                        down(c, 0, q)
                        up(c + 2, 2, q, e)
                        down(c + 1, 1, q)
                        if more:
                            transposes(e + 1, 1 - q, use + q)
                        down(c + 2, 2, q)

                    transposes(0, 0, 0)
                    expert(0, 0, 0, True)
                    expert(1, 1, 0, True)
                    with nc.tensor.Fori(1, E // 2 - 1) as h:
                        expert(2 * h, 0, h, True)
                        expert(2 * h + 1, 1, h, True)
                    expert(E - 2, 0, E // 2 - 1, True)
                    expert(E - 1, 1, E // 2 - 1, False)

                @block.scalar
                def _(act):
                    def gelus(h, q):
                        e = 2 * h + q
                        for cc, (t0, n) in enumerate(CHUNKS):
                            c = NC * e + cc
                            par = (cc + NC * q) % 2
                            if cc == 0:
                                act.wait_ge(e_chain, EXPERT_STEPS * e + 1)
                            wait(act, y_full, c - 1)
                            for b in range(FB):
                                act.wait_ge(h_full, FB * c + b + 1)
                                nc.scalar.activation(hT[par][:, b, 0:n * P], h_bank[b][:, 0:n * P], ACT.Gelu,
                                                     bias=bfc[q][:, b:b + 1]).then_inc(h_done, 1)
                    pairs(nc.scalar, E // 2, gelus)

                @block.vector
                def _(dve):
                    def turned(e, q, g):
                        t0, n = CHUNKS[g]
                        dve.wait_ge(t_full, NC * e + g + 1)
                        if g == 0:
                            wait(dve, y_full, NC * (e - 1))
                        nc.vector.tensor_copy(xbT[q][:, t0 * P:(t0 + n) * P],
                                              t_bank[g % 2 if q == 0 else (g + 1) % 2][:, 0:n * P]).then_inc(t_evac, 1)

                    def numbers(e, q, use):
                        step = Steps(dve, e_chain, e * EXPERT_STEPS, EXPERT_STEPS)
                        wait(dve, h_done, FB * NC * (e - 1))
                        step(nc.vector.tensor_copy(bfc[q][:], bias_up[:, bass.ds(e * FB, FB)]))
                        dve.wait_ge(rows_ld[q], 16 * use + 16)
                        wait(dve, added, 16 * CT * (e - 1))
                        one, used = is_first[:, bass.ds(e, 1), :], is_used[:, bass.ds(e, 1), :]
                        one = one.rearrange("p o t -> p (o t)")
                        used = used.rearrange("p o t -> p (o t)")
                        nc.vector.tensor_tensor(ti[:], xb[q][:, :, C_ID], spare[:], ALU.subtract)
                        step(nc.vector.tensor_tensor(pd[:], xb[q][:, :, C_P0], xb[q][:, :, C_P1], ALU.subtract))
                        step(nc.vector.tensor_tensor(pd[:], pd[:], one, ALU.mult))
                        step(nc.vector.tensor_tensor(pd[:], pd[:], xb[q][:, :, C_P1], ALU.add))
                        step(nc.vector.tensor_tensor(ti[:], ti[:], used, ALU.mult))
                        step(nc.vector.scalar_tensor_tensor(pw[:], pd[:], 0.5, used, ALU.mult, ALU.mult))
                        step(nc.vector.tensor_tensor(ids[q][:], ti[:], spare[:], ALU.add))
                        step.end()

                    def weighted(e, q, cc):
                        t0, n = CHUNKS[cc]
                        c = NC * e + cc
                        par = (cc + NC * q) % 2
                        dve.wait_ge(y_full, c + 1)
                        y = ys[q][:, t0:t0 + n, :]
                        nc.vector.tensor_tensor(y, y_bank[par][:, 0:n * P].rearrange("p (t d) -> p t d", d=D),
                                                bpj[q][:, None, :].broadcast_to([P, n, D]), ALU.add).then_inc(y_done, 1)
                        dve.wait_ge(y_done, c + 1)
                        nc.vector.tensor_tensor(y, y, pw[:, t0:t0 + n, None].broadcast_to([P, n, D]),
                                                ALU.mult).then_inc(y_ready, 1)

                    def expert(e, q, use, more):
                        numbers(e, q, use)
                        dve.wait_ge(w_ld[q], 48 * use + 48)
                        weighted(e, q, 0)
                        weighted(e, q, 1)
                        if more:
                            for g in range(NC):
                                turned(e + 1, 1 - q, g)
                        weighted(e, q, 2)

                    for g in range(NC):
                        turned(0, 0, g)
                    expert(0, 0, 0, True)
                    expert(1, 1, 0, True)
                    with nc.vector.Fori(1, E // 2 - 1) as h:
                        expert(2 * h, 0, h, True)
                        expert(2 * h + 1, 1, h, True)
                    expert(E - 2, 0, E // 2 - 1, True)
                    expert(E - 1, 1, E // 2 - 1, False)

                @block.gpsimd
                def _(pool):
                    def send(h, q):
                        e = 2 * h + q
                        wait_apart(pool, added, e * CT * 16)
                        for cc, (t0, n) in enumerate(CHUNKS):
                            wait_apart(pool, y_ready, NC * e + cc + 1)
                            for t in range(t0, t0 + n):
                                nc.gpsimd.indirect_dma_start(
                                    dest[:, :], bass.IndirectOffsetOnAxis(ap=ids[q][:, t:t + 1], axis=0),
                                    ys[q][:, t, :], None, compute_op=ALU.add).then_inc(added, 16)

                    pairs(nc.gpsimd, E // 2, send)
                    wait_apart(pool, added, E * CT * 16)

        experts(1, mid, False)

        a_full, a_done, masked, pv_done, o_done, c_full, c_evac, parts_ok, v_copied, v_ready = (
            sem(n) for n in ("a_full", "a_done", "masked", "pv_done", "o_done", "c_full", "c_evac", "parts_ok",
                             "v_copied", "v_ready"))
        st_full = [sem(f"st_full{i}") for i in range(2)]
        exp_done = [sem(f"exp_done{i}") for i in range(2)]
        qa_ld = [sem(f"qa_ld{i}") for i in range(2)]
        qb_ld = [sem(f"qb_ld{i}") for i in range(2)]
        kp_ld = [sem(f"kp_ld{i}") for i in range(NG)]
        max_ld = [[sem(f"max_ld{hf}{i}") for i in range(2)] for hf in range(2)]
        max_st, x1_ld, x2_ld, x2_st, x2_bias, stack_st = (
            sem(n) for n in ("max_st", "x1_ld", "x2_ld", "x2_st", "x2_bias", "stack_st"))
        n_stat, n_rstd, n_done, n_chain, part_one, rest_ok, split_ok, cleared, p_chain, v_ones, ctx_chain, win2 = (
            sem(n) for n in ("n_stat", "n_rstd", "n_done", "n_chain", "part_one", "rest_ok", "split_ok", "cleared",
                             "p_chain", "v_ones", "ctx_chain", "win2"))
        half_ok, r_num, n_pow = sem("half_ok"), sem("r_num"), sem("n_pow")
        with ExitStack() as part:
            sba = maker(part)
            qa = [sba(f"qa{i}", [P, HS, S], bf16) for i in range(2)]
            qb = [sba(f"qb{i}", [P, HS, S], bf16) for i in range(2)]
            kp = [sba(f"kp{i}", [P, HS // 2, S], bf16) for i in range(NG)]
            pt = [sba(f"pt{i}", [P, HS, 512]) for i in range(PTS)]
            v_all = sba("v_all", [P, B * T, NH, DH + 1])
            vs = [sba(f"vs{i}", [P, T, HS, VW]) for i in range(2)]
            o_sb = sba("o_sb", [P, S])
            ctx = sba("ctx", [P, T, D])
            ctxT = sba("ctxT", [P, S])
            x1 = sba("x1", [P, T, D])
            xn = sba("xn", [P, T, D])
            xnT = sba("xnT", [P, S])
            x2 = sba("x2", [P, T, D])
            parts = [[sba(f"{n}{j}", [P, S], bf16) for j in range(3)] for n in ("qp", "kq")]
            rest = sba("rest", [P, 2, 512])
            n_st = sba("n_st", [P, T, 6])
            n_mv = sba("n_mv", [P, T, 2])
            n_var = sba("n_var", [P, T])
            n_rs = sba("n_rs", [P, T])
            n_negm = sba("n_negm", [P, T])
            n_shift = sba("n_shift", [P, T])
            m_units = sba("m_units", [P, T, T // 2 + 1, HS])
            m_of = [sba(f"m_of{i}", [P, HS, T // 2]) for i in range(2)]
            m_neg = sba("m_neg", [P, HS, T // 2])
            m_parts = [sba(f"m_parts{i}", [P, 3, HS, T // 2], bf16) for i in range(2)]
            MR = 3 * HS * T // 2
            m_rows = [sba(f"m_rows{i}", [MR, P], bf16) for i in range(2)]
            recip = sba("recip", [P, T // 2, HS])
            block = part.enter_context(nc.Block())
            a_bank, o_bank, c_bank = bank[4:6], bank[6], bank[7]
            m_bank = c_bank.bitcast(bf16)
            two = two_banks[0:2]

            def use_of(uses, base):
                return {name: base + i for i, name in enumerate(uses)}

            class Batch:
                def __init__(self, b, kind):
                    self.b, self.kind = b, kind
                    self.first, self.final = kind == "first", kind == "final"
                    uses = {"first": FIRST_USES, "mid": MID_USES, "final": LAST_USES}[kind]
                    if self.first:
                        base = len(PRO)
                    else:
                        base = len(PRO) + len(FIRST_USES) + (b - 1) * len(MID_USES)
                    self.at = {name: base + i for i, name in enumerate(uses)}

            pro_at = {name: i for i, name in enumerate(PRO)}
            tail_at = {name: TAIL_AT + i for i, name in enumerate(TAIL)}

            def sweep(eng, step):
                for g in range(NG):
                    step(Batch(0, "first"), g)
                with eng.Fori(1, B - 1) as b:
                    for g in range(NG):
                        step(Batch(b, "mid"), g)
                for g in range(NG):
                    step(Batch(B - 1, "final"), g)

            R2_USE = B // 2

            LOADS = 2 * 16
            STORES = 2 * (KS // DH) * 16

            @block.sync
            def _(sp):
                def load_stack(dst, stack, b, g, done):
                    src = stack[bass.ds(b * NH * KS + g * HS * KS, HS * KS), :].rearrange("(i s r) n -> s r i n", s=2, r=KS)
                    for s in range(2):
                        sp.dma_start(dst(s), src[s]).then_inc(done, 16)

                def load_q(dst, b, g, done):
                    load_stack(lambda s: dst[64 * s:64 * s + KS].rearrange("p (i s) n -> p s i n", s=2)[:, s],
                               q_stack, b, g, done)

                def load_k(b, g):
                    load_stack(lambda s: kp[g][64 * s:64 * s + KS], k_stack, b, g, kp_ld[g])

                def step(bt, g):
                    b, at = bt.b, bt.at
                    n, p = NG * b + g, g % 2
                    more = not (bt.final and g == NG - 1)
                    if g == 0:
                        if not bt.final:
                            wait_apart(sp, n_done, b + 1)
                            sp.dma_start(x1[:], mid[bass.ds((b + 1) * S, S), :].rearrange("(t p) d -> p t d", p=P)
                                         ).then_inc(x1_ld, 16)
                        if not bt.first:
                            wait_apart(sp, r_rows, B + b - 1)
                            sp.dma_start(x2[:], mid[bass.ds((b - 1) * S, S), :].rearrange("(t p) d -> p t d", p=P)
                                         ).then_inc(x2_ld, 16)
                    if more:
                        wait_apart(sp, st_full[1], NU * n)
                        nb, ng = (b, g + 1) if g < NG - 1 else (b + 1, 0)
                        load_q(qb[1 - p], nb, ng, qb_ld[1 - p])
                    move(at[("max0", g)], 0, b, g, 2 * n + 1)
                    if g == 1 and not bt.first:
                        store_x2(at, b - 1)
                    if g == 2 and not bt.first:
                        wait_apart(sp, x2_st, 16 * b)
                    if g == 2 and not bt.final:
                        store_stacks(b + 1)
                    if not (bt.final and g >= 2):
                        nb, ng = (b, g + 2) if g < 2 else (b + 1, g - 2)
                        if g >= 2:
                            wait_apart(sp, stack_st, STORES * (b + 2))
                        load_q(qa[p], nb, ng, qa_ld[p])
                        load_k(nb, ng)
                    if more:
                        nb, ng = (b, g + 1) if g < NG - 1 else (b + 1, 0)
                        move(at[("max1", g + 1)], 1, nb, ng, 2 * n + 2)

                def move(use, hf, b, g, k):
                    par = g % 2
                    wait_apart(sp, c_evac, use + 1)
                    wait_apart(sp, max_ld[hf][1 - par], 32 * (2 * b + (g + 1) // 2))
                    flat = max_rows.rearrange("r (t q) -> (r t) q", q=P)
                    sp.dma_start(flat[hf * MR:(hf + 1) * MR, :], m_rows[hf][:]).then_inc(max_st, 16)
                    wait_apart(sp, max_st, 16 * (k + 1))
                    for s in range(2):
                        src = max_rows[hf * 3 * HS:(hf + 1) * 3 * HS, :].rearrange("(c i s) n -> s c i n", c=3, s=2)[s]
                        dst = qb[par][64 * s + KS:64 * s + KS + 3].rearrange("p (i s) n -> p s i n", s=2)[:, s, :,
                                                                            hf * HALF:(hf + 1) * HALF]
                        sp.dma_start(dst, src).then_inc(max_ld[hf][par], 16)

                def store_stacks(b):
                    wait_apart(sp, split_ok, 4 * (b + 1))
                    for stack, tiles, order in ((q_stack, parts[0], Q_PART), (k_stack, parts[1], K_PART)):
                        for c, j in enumerate(order):
                            dst = stack[bass.ds(b * NH * KS, NH * KS), :].rearrange("(h c d) n -> c h d n", h=NH, d=DH)[c]
                            sp.dma_start(dst, tiles[j][:]).then_inc(stack_st, 16)

                def store_x2(at, b):
                    wait_apart(sp, c_evac, at["o_p1"] + 1)
                    sp.dma_start(last[bass.ds(b * S, S), :].rearrange("(t p) d -> p t d", p=P), x2[:]).then_inc(x2_st, 16)

                sp.dma_start(x1[:], mid[0:S, :].rearrange("(t p) d -> p t d", p=P)).then_inc(x1_ld, 16)
                store_stacks(0)
                wait_apart(sp, stack_st, STORES)
                wait_apart(sp, cleared, 2)
                load_q(qa[0], 0, 0, qa_ld[0])
                load_k(0, 0)
                load_q(qb[0], 0, 0, qb_ld[0])
                load_q(qa[1], 0, 1, qa_ld[1])
                load_k(0, 1)
                move(pro_at[("max1", 0)], 1, 0, 0, 0)
                sweep(nc.sync, step)
                b = B - 1
                wait_apart(sp, r_rows, B + b)
                sp.dma_start(x2[:], mid[b * S:(b + 1) * S, :].rearrange("(t p) d -> p t d", p=P)).then_inc(x2_ld, 16)
                store_x2(tail_at, b)
                wait_apart(sp, x2_st, 16 * B)

            @block.tensor
            def _(pe):
                def score(par, g, b, n, u, pair):
                    hf, kb = UNITS[u]
                    q0, w = unit_queries(u)
                    wait(pe, exp_done[pair], NU * n + u)
                    for s in range(2):
                        i = nc.tensor.matmul(two[pair][:, s, 0:w], kp[g][:, pair, kb * P:(kb + 1) * P],
                                             qb[par][:, 2 * pair + s, q0:q0 + w], start=True, stop=True)
                    i.then_inc(st_full[pair], 1)

                def maxima(n, g, b, a0, a1):
                    par = g % 2
                    for a in range(a0, a1):
                        qt, heads, k0, w, diag, _ = AUNITS[a]
                        if a == 0:
                            pe.wait_ge(qa_ld[par], LOADS * uses_of(b, g))
                            pe.wait_ge(kp_ld[g], LOADS * (b + 1))
                        wait(pe, a_done, NA * n + a - 1)
                        if diag:
                            nc.tensor.matmul(a_bank[a % 2], identb[:], causal[:].rearrange("p h k -> p (h k)"),
                                             start=True, stop=False)
                        for j, h in enumerate(heads):
                            i = nc.tensor.matmul(a_bank[a % 2][:, j * w:(j + 1) * w], qa[par][:, h, qt * P:(qt + 1) * P],
                                                 kp[g][:, h // 2, k0:k0 + w], start=not diag,
                                                 stop=not diag or j == len(heads) - 1)
                        i.then_inc(a_full, 1)

                def uses_of(b, g):
                    return 2 * b + g // 2 + 1

                def values(par, n, u):
                    hf, kb = UNITS[u]
                    q0, w = unit_queries(u)
                    if u in (0, T):
                        wait(pe, o_done, 2 * n + u // T)
                        if u == 0:
                            pe.wait_ge(v_copied, n + 1)
                    if u in MASKED:
                        pe.wait_ge(masked, len(MASKED) * n + MASKED.index(u) + 1)
                    else:
                        pe.wait_ge(exp_done[1], NU * n + u + 1)
                    for h in range(HS):
                        i = nc.tensor.matmul(o_bank[VW * h:VW * h + VW, q0 - hf * HALF:q0 - hf * HALF + w],
                                             vs[par][:, kb, h, :], pt[u % PTS][:, h, 0:w],
                                             start=u in (0, T), stop=u in (T - 1, NU - 1))
                    i.then_inc(pv_done, 1)

                def bank_free(use):
                    wait(pe, c_evac, use)

                def max_rows_of(use, n, hf):
                    bank_free(use)
                    wait_apart(pe, parts_ok, 2 * n + (1 if hf else 2))
                    nc.tensor.transpose(m_bank[0:MR, 0:P], m_parts[hf][:].rearrange("p c h t -> p (c h t)"),
                                        identb[:]).then_inc(c_full, 1)

                def turn(use, src, half):
                    bank_free(use)
                    for t in range(4):
                        i = nc.tensor.transpose(c_bank[:, t * P:(t + 1) * P], src(4 * half + t), ident[:])
                    i.then_inc(c_full, 1)

                def context(use, n, hf):
                    pe.wait_ge(o_done, 2 * n + (1 if hf else 2))
                    turn(use, lambda t: o_sb[:, t * P:(t + 1) * P], hf)

                def project(use, w, half):
                    bank_free(use)
                    nc.tensor.matmul(c_bank, w[:], xnT[:, half * 512:half * 512 + 512], start=True,
                                     stop=True).then_inc(c_full, 1)

                def by_token(use, srcT, w, half):
                    bank_free(use)
                    for t in range(4):
                        c = (4 * half + t) * P
                        i = nc.tensor.matmul(c_bank[:, t * P:(t + 1) * P], srcT[:, c:c + P], w[:], start=True, stop=True)
                    i.then_inc(c_full, 1)

                def norm_task(at, name, b):
                    if name == "x_t0":
                        pe.wait_ge(n_done, b + 1)
                    if name in ("x_t0", "x_t1"):
                        turn(at[name], lambda t: xn[:, t, :], int(name[-1]))
                    elif name[0] in "qk":
                        project(at[name], wqT if name[0] == "q" else wkT, int(name[-1]))
                    else:
                        by_token(at[name], xnT, wvT, int(name[-1]))

                def out_task(at, name, call):
                    if name in ("o_t0", "o_t1"):
                        turn(at[name], lambda t: ctx[:, t, :], int(name[-1]))
                    elif name in ("o_p0", "o_p1"):
                        by_token(at[name], ctxT, woT, int(name[-1]))
                    elif name in ("r_t0", "r_t1"):
                        bank_free(at[name])
                        router_transpose(pe, call, 0, int(name[-1]), c_bank, c_full)
                    elif name == "r_lg":
                        bank_free(at[name])
                        router_logits(pe, c_bank, c_full)
                    else:
                        bank_free(at[name])
                        router_ranks(pe, call, c_bank, c_full)

                def step(bt, g):
                    b, at = bt.b, bt.at
                    n, par = NG * b + g, g % 2
                    more = not (bt.final and g == NG - 1)
                    nb, ng = (b, g + 1) if g < NG - 1 else (b + 1, 0)
                    pe.wait_ge(qb_ld[par], LOADS * uses_of(b, g))
                    for u in range(NU):
                        if u == 0:
                            pe.wait_ge(max_ld[1][par], 32 * uses_of(b, g))
                        if u == T:
                            pe.wait_ge(max_ld[0][par], 32 * uses_of(b, g))
                        a0, a3 = A_FROM[u], A_FROM[u + 1]
                        a1, a2 = min(a0 + 1, a3), min(a0 + 1 + max(1, (a3 - a0) // 2), a3)
                        score(par, g, b, n, u, 0)
                        if more:
                            maxima(n + 1, ng, nb, a0, a1)
                        score(par, g, b, n, u, 1)
                        if more:
                            maxima(n + 1, ng, nb, a1, a2)
                        if u >= LAG:
                            values(par, n, u - LAG)
                        elif not (bt.first and g == 0):
                            values(1 - par, n - 1, NU - LAG + u)
                        if more:
                            maxima(n + 1, ng, nb, a2, a3)
                        if u == 1:
                            max_rows_of(at[("max0", g)], n, 0)
                        if u == 2 and ("ctx0", g - 1) in at:
                            context(at[("ctx0", g - 1)], n - 1, 0)
                        if g == 0 and not bt.first and 3 <= u <= 6:
                            out_task(at, ("o_t0", "o_t1", "o_p0", "o_p1")[u - 3], B + b - 1)
                        if g == 1 and not bt.final and 3 <= u <= 7:
                            norm_task(at, ("x_t0", "x_t1", "q0", "q1", "k0")[u - 3], b + 1)
                        if g == 2 and not bt.first and 3 <= u <= 5:
                            out_task(at, ("r_t0", "r_t1", "r_lg")[u - 3], B + b - 1)
                        if g == 2 and not bt.final and 6 <= u <= 7:
                            norm_task(at, ("v0", "v1")[u - 6], b + 1)
                        if u == U_MA and more:
                            max_rows_of(at[("max1", g + 1)], n + 1, 1)
                        if u == 9 and g == 1 and not bt.final:
                            norm_task(at, "k1", b + 1)
                        if u == 9 and g == 2 and not bt.first:
                            out_task(at, "r_rk", B + b - 1)
                        if u == NU - 1:
                            context(at[("ctx1", g)], n, 1)

                for name in PRO[:-1]:
                    norm_task(pro_at, name, 0)
                pe.wait_ge(cleared, 2)
                maxima(0, 0, 0, 0, NA)
                max_rows_of(pro_at[("max1", 0)], 0, 1)
                sweep(nc.tensor, step)
                for u in range(NU - LAG, NU):
                    values((NG * B - 1) % 2, NG * B - 1, u)
                context(tail_at[("ctx0", NG - 1)], NG * B - 1, 0)
                for name in TAIL[1:]:
                    out_task(tail_at, name, 2 * B - 1)

            @block.scalar
            def _(act):
                def take(use, dst, src=None):
                    act.wait_ge(c_full, use + 1)
                    nc.scalar.copy(dst, c_bank if src is None else src).then_inc(c_evac, 1)

                def take_max(use, k, hf):
                    wait(act, max_st, 16 * k)
                    take(use, m_rows[hf][:], m_bank[0:MR, 0:P])

                def take_o(n, hf, read):
                    act.wait_ge(pv_done, NU * n + (T if hf else NU))
                    wait(act, c_full, read)
                    nc.scalar.copy(o_sb[:, hf * HALF:(hf + 1) * HALF], o_bank).then_inc(o_done, 1)

                def first_part(use, b, which, half):
                    act.wait_ge(c_full, use + 1)
                    if half == 0:
                        wait(act, stack_st, STORES * b)
                    nc.scalar.activation(parts[which][0][:, half * 512:half * 512 + 512], c_bank, ACT.Identity,
                                         bias=(bq_c, bk_c)[which][:]).then_inc(part_one, 1)

                def norm_task(at, name, b):
                    half = int(name[-1])
                    if name[0] == "x":
                        take(at[name], xnT[:, half * 512:half * 512 + 512])
                    elif name[0] in "qk":
                        first_part(at[name], b, "qk".index(name[0]), half)

                def out_take(at, name):
                    half = int(name[-1])
                    dst = ctxT if name[0] == "o" else xT
                    take(at[name], dst[:, half * 512:half * 512 + 512])

                def norm(b, t0, t1):
                    act.wait_ge(n_rstd, b + 1)
                    for t in range(t0, t1):
                        i = nc.scalar.activation(xn[:, t, :], x1[:, t, :], ACT.Identity, scale=n_rs[:, t:t + 1],
                                                 bias=n_shift[:, t:t + 1])
                    if t1 == T:
                        i.then_inc(n_done, 1)

                def norm_out(k, t0, t1):
                    if t0 == 0:
                        act.wait_ge(r_shift, k + 1)
                        act.wait_ge(r_num, k + 1)
                    for t in range(t0, t1):
                        i = nc.scalar.activation(rows[0][:, t, 0:D], x2[:, t, :], ACT.Identity, scale=rstd[:, t:t + 1],
                                                 bias=shift[:, t:t + 1])
                    if t1 == T:
                        i.then_inc(r_rows, 1)

                def step(bt, g):
                    b, at = bt.b, bt.at
                    n = NG * b + g
                    more = not (bt.final and g == NG - 1)
                    for u in range(NU):
                        q0, w = unit_queries(u)
                        for pair in range(2):
                            if pair == 0:
                                wait(act, pv_done, NU * n + u - PTS + 1)
                            act.wait_ge(st_full[pair], NU * n + u + 1)
                            nc.scalar.activation(pt[u % PTS][:, 2 * pair:2 * pair + 2, 0:w], two[pair][:, :, 0:w], ACT.Exp,
                                                 scale=SCALE).then_inc(exp_done[pair], 1)
                        if u == LAG - 1 and not (bt.first and g == 0):
                            take_o(n - 1, 0, at[("max0", g)])
                        if u == 1:
                            take_max(at[("max0", g)], 2 * n + 1, 0)
                        if g == 0 and not bt.first and 3 <= u <= 4:
                            out_take(at, ("o_t0", "o_t1")[u - 3])
                        if g == 1 and not bt.final and 3 <= u <= 7:
                            norm_task(at, ("x_t0", "x_t1", "q0", "q1", "k0")[u - 3], b + 1)
                        if g == 2 and not bt.first and 3 <= u <= 4:
                            out_take(at, ("r_t0", "r_t1")[u - 3])
                        if g == 0 and not bt.final and u >= 10:
                            norm(b + 1, (u - 10) * T // 2, (u - 9) * T // 2)
                        if g == 1 and not bt.first and 1 <= u <= 2:
                            norm_out(b - 1, (u - 1) * T // 2, u * T // 2)
                        if u == T + LAG - 1:
                            take_o(n, 1, at[("max0", g)] + 1)
                        if u == U_MA and more:
                            take_max(at[("max1", g + 1)], 2 * n + 2, 1)
                        if u == 9 and g == 1 and not bt.final:
                            norm_task(at, "k1", b + 1)
                        if u == 9 and g == 2 and not bt.first:
                            router_exp(act, B + b - 1)

                norm(0, 0, T)
                for name in PRO[:6]:
                    norm_task(pro_at, name, 0)
                take_max(pro_at[("max1", 0)], 0, 1)
                sweep(nc.scalar, step)
                take_o(NG * B - 1, 0, tail_at[("ctx0", NG - 1)])
                for name in ("o_t0", "o_t1"):
                    out_take(tail_at, name)
                norm_out(B - 1, 0, T)
                for name in ("r_t0", "r_t1"):
                    out_take(tail_at, name)
                router_exp(act, 2 * B - 1)

            @block.vector
            def _(dve):
                def reduce(n, a0, a1):
                    for a in range(a0, a1):
                        qt, heads, k0, w, diag, at = AUNITS[a]
                        dve.wait_ge(a_full, NA * n + a + 1)
                        nc.vector.tensor_reduce(m_units[:, qt, at, heads[0]:heads[-1] + 1],
                                                a_bank[a % 2].rearrange("p (h k) -> p h k", k=w), AX.X,
                                                ALU.max).then_inc(a_done, 1)
                        if a in (NA1 - 1, NA - 1):
                            hf = int(a < NA1)
                            wait(dve, parts_ok, 2 * n - hf)
                            dve.wait_ge(a_done, NA * n + a + 1)
                            nc.vector.tensor_reduce(m_of[hf][:], m_units[:, hf * T // 2:(hf + 1) * T // 2, :, :]
                                                    .rearrange("p t c h -> p h t c"), AX.X, ALU.max).then_inc(half_ok, 1)

                def context(use, n, g, hf):
                    dve.wait_ge(c_full, use + 1)
                    v = c_bank.rearrange("p (t h w) -> p t h w", t=4, h=HS)
                    nc.vector.reciprocal(recip[:], v[:, :, :, DH]).then_inc(ctx_chain, 1)
                    dve.wait_ge(ctx_chain, 2 * n + (1 if hf else 2))
                    nc.vector.tensor_tensor(
                        ctx[:, 4 * hf:4 * hf + 4, g * HS * DH:(g + 1) * HS * DH].rearrange("p t (h d) -> p t h d", h=HS),
                        v[:, :, :, 0:DH], recip[:, :, :, None].broadcast_to([P, 4, HS, DH]), ALU.mult).then_inc(c_evac, 1)

                def sums(b):
                    dve.wait_ge(x1_ld, 16 * (b + 1))
                    for t in range(T):
                        i = nc.vector.bn_stats(n_st[:, t, :], x1[:, t, :])
                    i.then_inc(n_chain, 1)

                def moments(b):
                    wait_apart(dve, n_chain, 2 * b + 1)
                    for t in range(T):
                        i = nc.vector.bn_aggr(n_mv[:, t, :], n_st[:, t, :])
                    i.then_inc(n_chain, 1)
                    dve.wait_ge(n_chain, 2 * b + 2)
                    nc.vector.tensor_scalar(n_negm[:], n_mv[:, :, 0], -1.0, None, ALU.mult)
                    nc.vector.tensor_scalar(n_var[:], n_mv[:, :, 1], EPS, None, ALU.add).then_inc(n_stat, 1)

                def remainder(use, b, which, half):
                    k = 4 * b + 2 * which + half
                    dve.wait_ge(part_one, k + 1)
                    wait(dve, split_ok, k - 1)
                    nc.vector.scalar_tensor_tensor(rest[:, half, :], c_bank, (bq_c, bk_c)[which][:],
                                                   parts[which][0][:, half * 512:half * 512 + 512],
                                                   ALU.add, ALU.subtract).then_inc(c_evac, 1)

                def norm_task(at, name, b):
                    half = int(name[-1])
                    if name[0] in "qk":
                        remainder(at[name], b, "qk".index(name[0]), half)
                    elif name[0] == "v":
                        dve.wait_ge(c_full, at[name] + 1)
                        nc.vector.tensor_tensor(
                            v_all[:, bass.ds(b * T + 4 * half, 4), :, 0:DH],
                            c_bank.rearrange("p (t h d) -> p t h d", t=4, d=DH),
                            bv_r[:].rearrange("p (h d) -> p h d", d=DH)[:, None, :, :].broadcast_to([P, 4, NH, DH]),
                            ALU.add).then_inc(c_evac, 1)

                def add_out(at, name, b):
                    half = int(name[-1])
                    dve.wait_ge(c_full, at[name] + 1)
                    dve.wait_ge(x2_bias, b + 1)
                    v = x2[:, 4 * half:4 * half + 4, :]
                    nc.vector.tensor_tensor(v, c_bank.rearrange("p (t d) -> p t d", t=4), v, ALU.add).then_inc(c_evac, 1)

                held = {}

                def out_task(at, name, b):
                    call = B + b
                    if name in ("o_p0", "o_p1"):
                        add_out(at, name, b)
                    elif name == "r_lg":
                        dve.wait_ge(c_full, at[name] + 1)
                        held["step"] = router_top2(dve, c_bank, call, c_evac, at[name] + 1)
                    elif name == "r_rk":
                        dve.wait_ge(c_full, at[name] + 1)
                        router_rank(c_bank, c_evac, held["step"])

                def step(bt, g):
                    b, at = bt.b, bt.at
                    n = NG * b + g
                    more = not (bt.final and g == NG - 1)
                    for u in range(NU):
                        if more:
                            reduce(n + 1, A_FROM[u], A_FROM[u + 1])
                        if u == 2 and ("ctx0", g - 1) in at:
                            context(at[("ctx0", g - 1)], n - 1, (g - 1) % NG, 0)
                        if g == 0 and not bt.first and 5 <= u <= 6:
                            out_task(at, ("o_p0", "o_p1")[u - 5], b - 1)
                        if g == 0 and not bt.final and u == 6:
                            sums(b + 1)
                        if g == 0 and not bt.final and u == 7:
                            moments(b + 1)
                        if g == 0 and not bt.first:
                            if u == 9:
                                dve.wait_ge(c_evac, at["o_p1"] + 1)
                                router_sums(x2, 0, T // 2)
                            if u == 10:
                                router_sums(x2, T // 2, T)
                            if u == 11:
                                router_moments(dve, B + b - 1)
                        if g == 1 and not bt.first and u == 0:
                            router_numbers(dve, 0, b - 1 + R2_USE).then_inc(r_num, 1)
                        if g == 1 and not bt.final and 5 <= u <= 7:
                            norm_task(at, ("q0", "q1", "k0")[u - 5], b + 1)
                        if g == 1 and not bt.final and u == 9:
                            norm_task(at, "k1", b + 1)
                        if g == 2 and not bt.first and u == 5:
                            out_task(at, "r_lg", b - 1)
                        if g == 2 and not bt.final and 6 <= u <= 7:
                            norm_task(at, ("v0", "v1")[u - 6], b + 1)
                        if g == 2 and not bt.first and u == 9:
                            out_task(at, "r_rk", b - 1)
                        if g == 2 and not bt.first and u == 10:
                            router_rows(dve, B + b - 1, 0, held["step"])
                        if u == NU - 1:
                            context(at[("ctx1", g)], n, g, 1)

                nc.vector.memset(m_units[:], NEG)
                for t_ in qa + qb:
                    i = nc.vector.memset(t_[:], 0.0)
                i.then_inc(cleared, 1)
                nc.vector.tensor_copy(tok_id[:], tok_id0[:])
                nc.vector.memset(taken[:], 0.0)
                sums(0)
                moments(0)
                for name in PRO[2:8]:
                    norm_task(pro_at, name, 0)
                reduce(0, 0, NA)
                sweep(nc.vector, step)
                b = B - 1
                context(tail_at[("ctx0", NG - 1)], NG * B - 1, NG - 1, 0)
                out_task(tail_at, "o_p0", b)
                out_task(tail_at, "o_p1", b)
                dve.wait_ge(c_evac, tail_at["o_p1"] + 1)
                router_sums(x2, 0, T)
                router_moments(dve, B + b)
                router_numbers(dve, 0, b + R2_USE).then_inc(r_num, 1)
                out_task(tail_at, "r_lg", b)
                out_task(tail_at, "r_rk", b)
                router_rows(dve, B + b, 0, held["step"])
                dve.wait_ge(r_chain, 2 * B * ROUTER_STEPS)
                router_windows(dve, win2, 0)

            @block.gpsimd
            def _(pool):
                PART_STEPS = 4

                def split_max(n, hf, k, used):
                    wait_apart(pool, half_ok, 2 * n + (1 if hf else 2))
                    wait_apart(pool, c_full, used)
                    wait_apart(pool, parts_ok, k)
                    base, c = PART_STEPS * k, [0]

                    def step(i):
                        c[0] += 1
                        i.then_inc(p_chain, 1)
                        wait_apart(pool, p_chain, base + c[0])

                    mp = m_parts[hf]
                    step(nc.gpsimd.tensor_scalar(m_neg[:], m_of[hf][:], -1.0, None, ALU.mult))
                    step(nc.gpsimd.tensor_copy(mp[:, 0], m_neg[:]))
                    step(nc.gpsimd.tensor_tensor(m_neg[:], m_neg[:], mp[:, 0], ALU.subtract))
                    step(nc.gpsimd.tensor_copy(mp[:, 1], m_neg[:]))
                    nc.gpsimd.tensor_tensor(mp[:, 2], m_neg[:], mp[:, 1], ALU.subtract).then_inc(parts_ok, 1)

                def split(use, b, which, half):
                    k = 4 * b + 2 * which + half
                    s = slice(half * 512, half * 512 + 512)
                    wait_apart(pool, c_evac, use + 1)
                    nc.gpsimd.tensor_copy(parts[which][1][:, s], rest[:, half, :]).then_inc(rest_ok, 1)
                    wait_apart(pool, rest_ok, k + 1)
                    nc.gpsimd.tensor_tensor(parts[which][2][:, s], rest[:, half, :], parts[which][1][:, s],
                                            ALU.subtract).then_inc(split_ok, 1)

                def copy_v(b, g, n, ready):
                    wait_apart(pool, pv_done, NU * (n - 1))
                    if g == 0:
                        wait_apart(pool, c_evac, ready)
                    nc.gpsimd.tensor_copy(vs[g % 2][:, :, :, 0:DH + 1],
                                          v_all[:, bass.ds(b * T, T), g * HS:(g + 1) * HS, :]).then_inc(v_copied, 1)

                def mask(n, u):
                    wait_apart(pool, exp_done[1], NU * n + u + 1)
                    v = pt[u % PTS][:, :, 0:P]
                    nc.gpsimd.affine_select(out=v, in_=v, compare_op=ALU.is_ge, fill=0.0, base=0,
                                            pattern=[[0, HS], [1, P]], channel_multiplier=-1).then_inc(masked, 1)

                def rstd1(b):
                    wait_apart(pool, n_stat, b + 1)
                    nc.gpsimd.tensor_tensor(n_rs[:], n_var[:], half_neg[:], ALU.pow).then_inc(n_pow, 1)
                    wait_apart(pool, n_pow, b + 1)
                    nc.gpsimd.tensor_tensor(n_shift[:], n_negm[:], n_rs[:], ALU.mult).then_inc(n_rstd, 1)

                def bias_x2(b):
                    wait_apart(pool, x2_ld, 16 * (b + 1))
                    nc.gpsimd.tensor_tensor(x2[:], x2[:], bo_r[:, None, :].broadcast_to([P, T, D]), ALU.add).then_inc(x2_bias, 1)

                def step(bt, g):
                    b, at = bt.b, bt.at
                    n = NG * b + g
                    more = not (bt.final and g == NG - 1)
                    nb, ng = (b, g + 1) if g < NG - 1 else (b + 1, 0)
                    for u in range(NU):
                        if u == LAG and more:
                            copy_v(nb, ng, n + 1, at[("max0", g)])
                        if u in MASKED:
                            mask(n, u)
                        if g == 0 and not bt.first and u == 3:
                            bias_x2(b - 1)
                        if g == 0 and not bt.final and u == 8:
                            rstd1(b + 1)
                        if g == 1 and not bt.final and u in (6, 7, 8, 10):
                            k = (6, 7, 8, 10).index(u)
                            split(at[("q0", "q1", "k0", "k1")[k]], b + 1, k // 2, k % 2)
                        if g == 1 and not bt.first and u == 0:
                            router_rstd(pool, B + b - 1)
                            router_shift(pool, b - 1)
                        if g == 3 and not bt.first:
                            if u == 0:
                                wait_apart(pool, r_idx, B + b)
                            for k in (range(3 * u, 3 * u + 3) if u < 4 else range(u + 8, min(u + 9, TOPK * T))):
                                router_scatter(pool, 0, k)
                        if u == 7 and more:
                            split_max(n + 1, 1, 2 * n + 2, at[("max0", g)] + 1)
                        if u == NU - 1 and more:
                            split_max(n + 1, 0, 2 * n + 3, at[("max1", g + 1)] + 1)

                for t_ in kp:
                    i = nc.gpsimd.memset(t_[:], 1.0)
                i.then_inc(cleared, 1)
                for t_ in vs:
                    nc.gpsimd.memset(t_[:], 0.0)
                nc.gpsimd.memset(v_all[:, :, :, DH], 1.0).then_inc(v_ones, 1)
                rstd1(0)
                for k in range(4):
                    split(pro_at[("q0", "q1", "k0", "k1")[k]], 0, k // 2, k % 2)
                wait_apart(pool, v_ones, 1)
                copy_v(0, 0, 0, pro_at["v1"] + 1)
                split_max(0, 1, 0, 0)
                split_max(0, 0, 1, 0)
                sweep(nc.gpsimd, step)
                b = B - 1
                bias_x2(b)
                router_rstd(pool, B + b)
                router_shift(pool, b)
                wait_apart(pool, r_idx, 2 * B)
                for k in range(TOPK * T):
                    router_scatter(pool, 0, k)
                wait_apart(pool, scattered[0], (R2_USE + B) * 16 * TOPK * T)

        experts(2, last, True)


_INS = ["L0_attn_x", "L0_attn_wq", "L0_attn_bq", "L0_attn_wk", "L0_attn_bk", "L0_attn_wv", "L0_attn_bv", "L0_attn_wo",
        "L0_attn_bo", "L0_ffn_gate_w", "L0_ffn_c_fc", "L0_ffn_fc_bias", "L0_ffn_c_proj", "L0_ffn_proj_bias"]
_OUTS = [((4, 1024, 128), "float32")]


def kernel(**inputs):
    import numpy as _np
    import concourse.bacc as _bacc
    from concourse import mybir as _mybir
    from concourse.bass_utils import run_bass_kernel_spmd as _run

    nc = _bacc.Bacc("TRN2", target_bir_lowering=False, num_devices=1)
    arrays, args = {}, []
    for name in _INS:
        a = _np.ascontiguousarray(inputs[name])
        arrays[f"in_{name}_dram"] = a
        args.append(nc.dram_tensor(f"in_{name}_dram", a.shape, _mybir.dt.from_np(a.dtype), kind="ExternalInput").ap())
    for i, (shape, dtype) in enumerate(_OUTS):
        dt = _mybir.dt.from_np(_np.dtype(dtype))
        args.append(nc.dram_tensor(f"out_{i}_dram", shape, dt, kind="ExternalOutput").ap())
    macaron_block_kernel(nc, *args)
    r = _run(nc, [arrays], core_ids=[0])
    got = tuple(r.results[0][f"out_{i}_dram"] for i in range(len(_OUTS)))
    return got[0]
```

```python
import concourse.bass as bass
from concourse import mybir
from contextlib import ExitStack


def macaron_block_kernel(nc, x, wq, bq, wk, bk, wv, bv, wo, bo, gate_w, c_fc, fc_bias, c_proj, proj_bias, out):
    f32, bf16, i32 = mybir.dt.float32, mybir.dt.bfloat16, mybir.dt.int32
    ALU, ACT, AX = mybir.AluOpType, mybir.ActivationFunctionType, mybir.AxisListType

    P = 128
    B, S, D = x.shape
    N = B * S
    E, _, F = c_fc.shape
    FB = F // P
    T = S // P
    NH, DH = 16, D // 16
    TOPK = 2
    CAP = int(1.25 * N * TOPK / E)
    CT = CAP // P
    EPS = 1e-5
    NEG = -3.0e38
    ROW = D + 4
    C_ID, C_P0, C_P1 = D, D + 1, D + 2
    SKIP = 1.0e6

    HS = 4
    NG = NH // HS
    Q_PART = [0, 0, 0, 1, 1, 2]
    K_PART = [0, 1, 2, 0, 1, 0]
    KS = len(Q_PART) * DH
    HALF = S // 2
    SCALE = float(DH) ** -0.5
    VW = 32

    UNITS = [(1, k) for k in range(T)] + [(0, k) for k in range(T // 2)]
    NU = len(UNITS)

    def unit_queries(u):
        hf, kb = UNITS[u]
        q0 = max(hf * HALF, kb * P)
        return q0, (hf + 1) * HALF - q0

    MASKED = [u for u in range(NU) if UNITS[u][1] * P >= UNITS[u][0] * HALF]
    AUNITS = []
    for hf in (1, 0):
        for qt in range(hf * T // 2, (hf + 1) * T // 2):
            for j in range(qt // 2):
                AUNITS += [(qt, (0, 1), 2 * j * P, 2 * P, False, j), (qt, (2, 3), 2 * j * P, 2 * P, False, j)]
            if qt % 2:
                AUNITS.append((qt, range(HS), (qt - 1) * P, P, False, T // 2 - 1))
            AUNITS.append((qt, range(HS), qt * P, P, True, T // 2))
        if hf:
            NA1 = len(AUNITS)
    NA = len(AUNITS)
    A_IN_SLOT = [3, 3, 4, 4, 4, 4, 2, 2, 3, 3, 2, 2]
    assert sum(A_IN_SLOT) == NA and sum(A_IN_SLOT[:8]) >= NA1
    A_FROM = [sum(A_IN_SLOT[:u]) for u in range(NU + 1)]
    LAG = 2
    PTS = LAG + 2
    U_MA = 8

    def bank_uses(first, final):
        uses = []
        for g in range(NG):
            uses.append(("max0", g))
            if not (first and g == 0):
                uses.append(("ctx0", g - 1))
            if g == 0 and not first:
                uses += ["o_t0", "o_t1", "o_p0", "o_p1"]
            if g == 1 and not final:
                uses += ["x_t0", "x_t1", "q0", "q1", "k0"]
            if g == 2:
                if not first:
                    uses += ["r_t0", "r_t1", "r_lg"]
            if g == 3 and not final:
                uses += ["v0", "v1"]
            if not (final and g == NG - 1):
                uses.append(("max1", g + 1))
            if g == 1 and not final:
                uses.append("k1")
            if g == 2 and not first:
                uses.append("r_rk")
            uses.append(("ctx1", g))
        return uses

    PRO = ["x_t0", "x_t1", "q0", "q1", "k0", "k1", "v0", "v1", ("max1", 0)]
    FIRST_USES, MID_USES, LAST_USES = bank_uses(True, False), bank_uses(False, False), bank_uses(False, True)
    TAIL = [("ctx0", NG - 1), "o_t0", "o_t1", "o_p0", "o_p1", "r_t0", "r_t1", "r_lg", "r_rk"]
    TAIL_AT = len(PRO) + len(FIRST_USES) + (B - 2) * len(MID_USES) + len(LAST_USES)

    xf = x.rearrange("b s d -> (b s) d")
    bucket = nc.dram_tensor("bucket", [E * 4 * CAP, ROW], f32, kind="Internal").ap()
    mid = nc.dram_tensor("mid", [N, D], f32, kind="Internal").ap()
    last = out.rearrange("b s d -> (b s) d")
    q_stack = nc.dram_tensor("q_stack", [B * NH * KS, S], bf16, kind="Internal").ap()
    k_stack = nc.dram_tensor("k_stack", [B * NH * KS, S], bf16, kind="Internal").ap()
    max_rows = nc.dram_tensor("max_rows", [2 * 3 * HS, HALF], bf16, kind="Internal").ap()

    whole = ExitStack()
    with whole:
        def maker(stack):
            def make(name, shape, dt=f32):
                return stack.enter_context(nc.sbuf_tensor(name, shape, dt))
            return make

        def sem(name):
            return whole.enter_context(nc.semaphore(name))

        sb = maker(whole)
        two_banks = [whole.enter_context(nc.psum_tensor(f"banks{i}", [P, 2, 512], f32)) for i in range(4)]
        bank = [two_banks[i // 2][:, i % 2, :] for i in range(8)]

        ident = sb("ident", [P, P])
        identb = sb("identb", [P, P], bf16)
        before = sb("before", [P, P], bf16)
        onesb = sb("onesb", [P, P], bf16)
        zero = sb("zero", [P, CT * ROW])
        gate = sb("gate", [P, E])
        place = sb("place", [P, T, E])
        half_neg = sb("half_neg", [P, T])
        tok_id0 = sb("tok_id0", [P, T])
        tok_id = sb("tok_id", [P, T])
        slot_of = sb("slot_of", [P, CT])
        sign = sb("sign", [P, T, TOPK])
        slot0 = sb("slot0", [P, T, TOPK])
        taken = sb("taken", [P, TOPK, E])
        firsts = sb("firsts", [P, E])
        seconds = sb("seconds", [P, E])
        total = sb("total", [P, E])
        is_first = sb("is_first", [P, E, CT])
        is_used = sb("is_used", [P, E, CT])
        window = sb("window", [P, E], i32)
        low_at = sb("low_at", [P, E], i32)
        fill_at = sb("fill_at", [P, E], i32)
        e_base = sb("e_base", [P, E])
        iota_i = sb("iota_i", [P, 64], i32)
        wqT, wkT, wvT, woT = (sb(n, [P, P]) for n in ("wqT", "wkT", "wvT", "woT"))
        bq_c, bk_c = sb("bq_c", [P, 1]), sb("bk_c", [P, 1])
        bv_r, bo_r = sb("bv_r", [P, P]), sb("bo_r", [P, P])
        bias_up = sb("bias_up", [P, E * FB])
        causal = sb("causal", [P, HS, P], bf16)
        rows = [sb(f"rows{i}", [P, T, ROW]) for i in range(2)]
        stat = sb("stat", [P, T, 6])
        mv = sb("mv", [P, T, 2])
        var_e = sb("var_e", [P, T])
        rstd = sb("rstd", [P, T])
        neg_mean = sb("neg_mean", [P, T])
        shift = sb("shift", [P, T])
        xT = sb("xT", [P, S])
        lg = sb("lg", [P, T, E])
        lg2 = sb("lg2", [P, T, E])
        eq = sb("eq", [P, T, E])
        cand = sb("cand", [P, T, E])
        top = sb("top", [P, T, TOPK])
        chosen = sb("chosen", [P, T, TOPK])
        hot = sb("hot", [P, T, TOPK, E], bf16)
        gap = sb("gap", [P, T])
        eg = sb("eg", [P, T])
        es = sb("es", [P, T])
        ranks = sb("ranks", [P, T, TOPK, E])
        rank = sb("rank", [P, T, TOPK])
        over = sb("over", [P, T, TOPK])
        place_in = sb("place_in", [P, T, TOPK])
        row_ix = [sb(f"row_ix{i}", [P, TOPK, T], i32) for i in range(2)]

        scattered = [sem(f"scattered{i}") for i in range(2)]
        r_stat, r_rstd, r_shift, r_rows, r_hot, r_exp, r_idx, r_chain = (
            sem(n) for n in ("r_stat", "r_rstd", "r_shift", "r_rows", "r_hot", "r_exp", "r_idx", "r_chain"))

        passed = sem("passed")

        def wait(eng, s, n):
            if not (isinstance(n, int) and n <= 0):
                eng.wait_ge(s, n)

        def wait_apart(eng, s, n):
            wait(eng, s, n)
            if not isinstance(n, int):
                eng.sem_inc(passed, 1)

        def pairs(eng, count, body):
            body(0, 0)
            body(0, 1)
            if count > 1:
                with eng.Fori(1, count) as h:
                    body(h, 0)
                    body(h, 1)

        class Steps:
            def __init__(self, eng, s, base, total):
                self.eng, self.s, self.base, self.total, self.k = eng, s, base, total, 0

            def __call__(self, ins):
                ins.then_inc(self.s, 1)
                self.k += 1
                self.eng.wait_ge(self.s, self.base + self.k)

            def end(self):
                assert self.k == self.total, (self.k, self.total)

        ROUTER_STEPS = 20

        def router_sums(xin, t0, t1):
            for t in range(t0, t1):
                i = nc.vector.bn_stats(stat[:, t, :], xin[:, t, :])
            if t1 == T:
                i.then_inc(r_chain, 1)

        def router_moments(dve, base):
            wait_apart(dve, r_chain, base + 1)
            for t in range(T):
                i = nc.vector.bn_aggr(mv[:, t, :], stat[:, t, :])
            i.then_inc(r_chain, 1)
            dve.wait_ge(r_chain, base + 2)
            nc.vector.tensor_scalar(neg_mean[:], mv[:, :, 0], -1.0, None, ALU.mult)
            nc.vector.tensor_scalar(var_e[:], mv[:, :, 1], EPS, None, ALU.add).then_inc(r_stat, 1)

        def router_rstd(pool, call):
            wait_apart(pool, r_stat, call + 1)
            nc.gpsimd.tensor_tensor(rstd[:], var_e[:], half_neg[:], ALU.pow).then_inc(r_rstd, 1)

        def router_shift(pool, k):
            wait_apart(pool, r_rstd, B + k + 1)
            nc.gpsimd.tensor_tensor(shift[:], neg_mean[:], rstd[:], ALU.mult).then_inc(r_shift, 1)

        def router_numbers(dve, buf, use):
            wait(dve, scattered[buf], use * 16 * TOPK * T)
            return nc.vector.tensor_copy(rows[buf][:, :, C_ID], tok_id[:])

        def router_norm(dve, xin, call, buf, use):
            dve.wait_ge(r_rstd, call + 1)
            router_numbers(dve, buf, use)
            for t in range(T):
                i = nc.vector.tensor_scalar(rows[buf][:, t, 0:D], xin[:, t, :], mv[:, t, 0:1], rstd[:, t:t + 1],
                                            ALU.subtract, ALU.mult)
            i.then_inc(r_rows, 1)

        def router_transpose(pe, call, buf, half, tb, full):
            if half == 0:
                pe.wait_ge(r_rows, call + 1)
            for t in range(4):
                i = nc.tensor.transpose(tb[:, t * P:(t + 1) * P], rows[buf][:, 4 * half + t, 0:D], ident[:])
            i.then_inc(full, 1)

        def router_logits(pe, lb, full):
            for t in range(T):
                i = nc.tensor.matmul(lb[:, t * E:(t + 1) * E], xT[:, t * P:(t + 1) * P], gate[:], start=True, stop=True)
            i.then_inc(full, 1)

        def router_top2(dve, lb, base, evac, evac_n):
            step = Steps(dve, r_chain, base, ROUTER_STEPS - 2)
            nc.vector.tensor_scalar(tok_id[:], tok_id[:], float(S), None, ALU.add)
            i = nc.vector.tensor_copy(lg[:].rearrange("p t e -> p (t e)"), lb[:, 0:T * E])
            i.then_inc(evac, 1)
            dve.wait_ge(evac, evac_n)
            step(nc.vector.tensor_reduce(top[:, :, 0], lg[:], AX.X, ALU.max))

            def one_hot(l, k):
                wide = top[:, :, k:k + 1].broadcast_to([P, T, E])
                step(nc.vector.tensor_tensor(eq[:], l[:], wide, ALU.is_equal))
                step(nc.vector.tensor_tensor(cand[:], eq[:], place[:], ALU.mult))
                step(nc.vector.tensor_reduce(chosen[:, :, k], cand[:], AX.X, ALU.max))
                return nc.vector.tensor_tensor(hot[:, :, k, :], place[:], chosen[:, :, k:k + 1].broadcast_to([P, T, E]),
                                               ALU.is_equal)
            step(one_hot(lg, 0))
            step(nc.vector.scalar_tensor_tensor(lg2[:], hot[:, :, 0, :], NEG, lg[:], ALU.mult, ALU.add))
            step(nc.vector.tensor_reduce(top[:, :, 1], lg2[:], AX.X, ALU.max))
            one_hot(lg2, 1).then_inc(r_hot, 1)
            nc.vector.tensor_tensor(gap[:], top[:, :, 1], top[:, :, 0], ALU.subtract).then_inc(r_hot, 1)
            return step

        def router_exp(act, call):
            act.wait_ge(r_hot, 2 * call + 2)
            nc.scalar.activation(eg[:], gap[:], ACT.Exp).then_inc(r_exp, 1)

        def router_ranks(pe, call, rb, full):
            pe.wait_ge(r_hot, 2 * call + 1)
            W = TOPK * E
            h = hot[:].rearrange("p t k e -> p (t k e)")
            nc.tensor.matmul(rb[:, 0:T * W], before[:], h, start=True, stop=False)
            for s in range(1, T):
                nc.tensor.matmul(rb[:, s * W:T * W], onesb[:], h[:, 0:(T - s) * W], start=False, stop=s == T - 1)
            for t in range(T):
                i = nc.tensor.matmul(rb[:, T * W:T * W + W], onesb[:], h[:, t * W:(t + 1) * W], start=t == 0, stop=t == T - 1)
            i.then_inc(full, 1)

        def router_rank(rb, evac, step):
            W = TOPK * E
            tk = taken[:].rearrange("p k e -> p (k e)")
            step(nc.vector.tensor_tensor(ranks[:].rearrange("p t k e -> p t (k e)"),
                                         rb[:, 0:T * W].rearrange("p (t w) -> p t w", w=W),
                                         tk[:, None, :].broadcast_to([P, T, W]), ALU.add))
            nc.vector.tensor_tensor(tk, tk, rb[:, T * W:T * W + W], ALU.add).then_inc(evac, 1)
            step(nc.vector.tensor_tensor(ranks[:], ranks[:], hot[:], ALU.mult))
            step(nc.vector.tensor_reduce(rank[:], ranks[:], AX.X, ALU.add))

        def router_rows(dve, call, buf, step):
            nc.vector.tensor_scalar(over[:], rank[:], float(CAP), SKIP, ALU.is_ge, ALU.mult)
            step(nc.vector.tensor_tensor(place_in[:], rank[:], sign[:], ALU.mult))
            step(nc.vector.scalar_tensor_tensor(place_in[:], chosen[:], -4.0 * CAP, place_in[:], ALU.mult, ALU.add))
            step(nc.vector.tensor_tensor(place_in[:], place_in[:], over[:], ALU.add))
            dve.wait_ge(r_exp, call + 1)
            step(nc.vector.tensor_scalar(es[:], eg[:], 1.0, None, ALU.add))
            step(nc.vector.reciprocal(gap[:], es[:]))
            nc.vector.tensor_copy(rows[buf][:, :, C_P0], gap[:])
            nc.vector.tensor_tensor(rows[buf][:, :, C_P1], gap[:], eg[:], ALU.mult)
            nc.vector.tensor_tensor(row_ix[buf][:].rearrange("p k t -> p t k"), place_in[:], slot0[:],
                                    ALU.add).then_inc(r_idx, 1)
            step.end()

        def router_scatter(pool, buf, n):
            k, t = divmod(n, T)
            nc.gpsimd.indirect_dma_start(bucket[:, :], bass.IndirectOffsetOnAxis(ap=row_ix[buf][:, k, t:t + 1], axis=0),
                                         rows[buf][:, t, :], None, bounds_check=E * 4 * CAP - 1,
                                         oob_is_err=False).then_inc(scattered[buf], 16)

        WINDOW_STEPS = 3

        def router_windows(dve, s, at):
            nc.vector.tensor_scalar(seconds[:], taken[:, 1, :], float(CAP), None, ALU.min)
            nc.vector.tensor_scalar(firsts[:], taken[:, 0, :], float(CAP), None, ALU.min).then_inc(s, 1)
            dve.wait_ge(s, at + 1)
            nc.vector.tensor_tensor(fill_at[:], e_base[:], seconds[:], ALU.add)
            nc.vector.tensor_tensor(total[:], firsts[:], taken[:, 1, :], ALU.add)
            nc.vector.tensor_tensor(window[:], e_base[:], firsts[:], ALU.subtract)
            nc.vector.tensor_tensor(is_first[:], slot_of[:, None, :].broadcast_to([P, E, CT]),
                                    firsts[:, :, None].broadcast_to([P, E, CT]), ALU.is_lt).then_inc(s, 1)
            dve.wait_ge(s, at + 2)
            nc.vector.tensor_scalar(low_at[:], window[:], -float(CAP), None, ALU.add)
            nc.vector.tensor_tensor(is_used[:], slot_of[:, None, :].broadcast_to([P, E, CT]),
                                    total[:, :, None].broadcast_to([P, E, CT]), ALU.is_lt).then_inc(s, 1)

        def row_of(table, e):
            return nc.sync.value_load(table[0:1, bass.ds(e, 1)], min_val=0, max_val=(4 * E - 1) * CAP)

        def clear(sp, at):
            return sp.dma_start(bucket[bass.ds(at, CAP), :].rearrange("(p r) c -> p (r c)", p=P), zero[:])

        s_w, s_gate, s_zero, s_copy = (sem(n) for n in ("s_w", "s_gate", "s_zero", "s_copy"))
        s_iota, s_const, s_cdve, s_wt = (sem(n) for n in ("s_iota", "s_const", "s_cdve", "s_wt"))
        r1_ld = [sem(f"r1_ld{i}") for i in range(2)]
        r1_full, r1_evac, win1, cleared1 = sem("r1_full"), sem("r1_evac"), sem("win1"), sem("cleared1")
        with ExitStack() as part:
            sb1 = maker(part)
            wraw = sb1("wraw", [P, 4, P])
            braw = sb1("braw", [E * FB, P])
            xin = [sb1(f"xin{i}", [P, T, D]) for i in range(2)]
            block = part.enter_context(nc.Block())

            @block.sync
            def _(sp):
                def load(h, buf):
                    wait_apart(sp, r_rows, 2 * h - 1 + buf)
                    sp.dma_start(xin[buf][:], xf[bass.ds((2 * h + buf) * S, S), :].rearrange("(t p) d -> p t d", p=P)
                                 ).then_inc(r1_ld[buf], 16)

                pairs(nc.sync, B // 2, load)
                sp.wait_ge(win1, WINDOW_STEPS)
                sp.wait_ge(s_zero, 1)
                for e in range(2):
                    clear(sp, row_of(fill_at, e)).then_inc(cleared1, 16)
                sp.wait_ge(cleared1, 2 * 16)

            @block.gpsimd
            def _(pool):
                nc.gpsimd.iota(iota_i[:, 0:CT], pattern=[[P, CT]], base=0, channel_multiplier=1)
                nc.gpsimd.iota(iota_i[:, 32:32 + T], pattern=[[P, T]], base=0, channel_multiplier=1)
                nc.gpsimd.iota(iota_i[:, 48:48 + E], pattern=[[-1, E]], base=E, channel_multiplier=0).then_inc(s_iota, 1)
                wait_apart(pool, s_cdve, 1)
                for tile_ in (ident, identb):
                    nc.gpsimd.affine_select(out=tile_[:], in_=tile_[:], compare_op=ALU.not_equal, fill=1.0, base=0,
                                            pattern=[[-1, P]], channel_multiplier=1).then_inc(s_const, 1)
                nc.gpsimd.affine_select(out=before[:], in_=before[:], compare_op=ALU.is_gt, fill=0.0, base=0,
                                        pattern=[[1, P]], channel_multiplier=-1).then_inc(s_const, 1)
                nc.gpsimd.affine_select(out=causal[:], in_=causal[:], compare_op=ALU.is_ge, fill=NEG, base=0,
                                        pattern=[[0, HS], [-1, P]], channel_multiplier=1).then_inc(s_const, 1)

                def scatter(call, buf, more):
                    if more:
                        router_rstd(pool, call + 1)
                    wait_apart(pool, r_idx, call + 1)
                    for n in range(TOPK * T):
                        router_scatter(pool, buf, n)

                router_rstd(pool, 0)
                pairs(nc.gpsimd, B // 2 - 1, lambda h, buf: scatter(2 * h + buf, buf, True))
                scatter(B - 2, 0, True)
                scatter(B - 1, 1, False)
                for buf in range(2):
                    wait_apart(pool, scattered[buf], B // 2 * 16 * TOPK * T)

            @block.vector
            def _(dve):
                nc.vector.memset(ident[:], 0.0)
                nc.vector.memset(identb[:], 0.0)
                nc.vector.memset(before[:], 1.0)
                nc.vector.memset(causal[:], 0.0).then_inc(s_cdve, 1)
                nc.vector.memset(zero[:], 0.0).then_inc(s_zero, 1)
                nc.vector.memset(onesb[:], 1.0)
                nc.vector.memset(half_neg[:], -0.5)
                nc.vector.memset(taken[:], 0.0)
                for buf in range(2):
                    nc.vector.memset(rows[buf][:, :, D:ROW], 0.0)
                nc.vector.memset(sign[:, :, 0], -1.0)
                nc.vector.memset(sign[:, :, 1], 1.0)
                nc.vector.memset(slot0[:, :, 0], 4.0 * CAP * E + 2 * CAP - 1)
                nc.vector.memset(slot0[:, :, 1], 4.0 * CAP * E + 2 * CAP)
                dve.wait_ge(s_iota, 1)
                nc.vector.tensor_copy(slot_of[:], iota_i[:, 0:CT])
                nc.vector.tensor_copy(tok_id0[:], iota_i[:, 32:32 + T])
                nc.vector.tensor_copy(tok_id[:], iota_i[:, 32:32 + T])
                nc.vector.tensor_copy(place[:], iota_i[:, None, 48:48 + E].broadcast_to([P, T, E]))
                nc.vector.tensor_scalar(e_base[:], iota_i[:, 48:48 + E], -4.0 * CAP, 4.0 * CAP * E + 2 * CAP, ALU.mult,
                                        ALU.add).then_inc(s_cdve, 1)
                dve.wait_ge(s_cdve, 2)

                def moments(h, buf, base):
                    dve.wait_ge(r1_ld[buf], 16 * h + 16)
                    router_sums(xin[buf], 0, T)
                    router_moments(dve, base)

                def route(h, buf, more):
                    call = 2 * h + buf
                    router_norm(dve, xin[buf], call, buf, h)
                    if more:
                        moments(h + buf, 1 - buf, call * ROUTER_STEPS + 2)
                    dve.wait_ge(r1_full, 4 * call + 3)
                    step = router_top2(dve, bank[6], call * ROUTER_STEPS + (4 if more else 2), r1_evac, 4 * call + 3)
                    dve.wait_ge(r1_full, 4 * call + 4)
                    router_rank(bank[7], r1_evac, step)
                    router_rows(dve, call, buf, step)

                moments(0, 0, 0)
                pairs(nc.vector, B // 2 - 1, lambda h, buf: route(h, buf, True))
                route(B // 2 - 1, 0, True)
                route(B // 2 - 1, 1, False)
                dve.wait_ge(r_chain, B * ROUTER_STEPS)
                dve.wait_ge(r1_evac, 4 * B)
                router_windows(dve, win1, 0)
                for n, w in enumerate((wqT, wkT, wvT, woT)):
                    dve.wait_ge(s_wt, n + 1)
                    nc.vector.tensor_copy(w[:], bank[1 + n][:, 0:P])
                dve.wait_ge(s_wt, 5)
                nc.vector.tensor_copy(bias_up[:], bank[5][:, 0:E * FB])

            @block.scalar
            def _(act):
                act.dma_start(gate[:], gate_w).then_inc(s_gate, 16)
                for n, w in enumerate((wq, wk, wv, wo)):
                    act.dma_start(wraw[:, n, :], w).then_inc(s_w, 16)
                act.dma_start(braw[:], fc_bias.rearrange("e o (b p) -> (e o b) p", p=P)).then_inc(s_w, 16)
                act.dma_start(bq_c[:], bq.rearrange("(p o) -> p o", o=1)).then_inc(s_w, 16)
                act.dma_start(bk_c[:], bk.rearrange("(p o) -> p o", o=1)).then_inc(s_w, 16)
                act.dma_start(bv_r[:], bv.rearrange("(o n) -> o n", o=1).broadcast_to([P, D])).then_inc(s_w, 16)
                act.dma_start(bo_r[:], bo.rearrange("(o n) -> o n", o=1).broadcast_to([P, D])).then_inc(s_w, 16)
                act.dma_start(mid[0:N, :], xf).then_inc(s_copy, 16)
                with nc.scalar.Fori(0, B) as call:
                    for half in range(2):
                        act.wait_ge(r1_full, 4 * call + half + 1)
                        nc.scalar.copy(xT[:, half * 512:half * 512 + 512], bank[half][:]).then_inc(r1_evac, 1)
                    router_exp(act, call)
                act.wait_ge(s_copy, 16)
                act.wait_ge(s_w, 16 * 9)

            @block.tensor
            def _(pe):
                pe.wait_ge(s_const, 4)
                pe.wait_ge(s_gate, 16)
                def route(h, buf):
                    call = 2 * h + buf
                    wait(pe, r1_evac, 4 * call)
                    for half in range(2):
                        router_transpose(pe, call, buf, half, bank[half], r1_full)
                    wait(pe, r1_evac, 4 * call + 2)
                    router_logits(pe, bank[6], r1_full)
                    router_ranks(pe, call, bank[7], r1_full)

                pairs(nc.tensor, B // 2, route)
                pe.wait_ge(s_w, 16 * 9)
                for n in range(4):
                    nc.tensor.transpose(bank[1 + n][:, 0:P], wraw[:, n, :], ident[:]).then_inc(s_wt, 1)
                nc.tensor.transpose(bank[5][:, 0:E * FB], braw[:], ident[0:E * FB, 0:E * FB]).then_inc(s_wt, 1)

        CHUNKS = [(0, 4), (4, 4), (8, CT - 8)]
        NC = len(CHUNKS)
        EXPERT_STEPS = 7

        def experts(tag, dest, final):
            cleared_rows, cleared_low = sem(f"cleared_rows{tag}"), sem(f"cleared_low{tag}")
            rows_ld = [sem(f"rows_ld{tag}{i}") for i in range(2)]
            w_ld = [sem(f"w_ld{tag}{i}") for i in range(2)]
            t_full, t_evac, h_full, h_done, y_full, y_done, y_ready, added, e_chain = (
                sem(f"{n}{tag}") for n in ("t_full", "t_evac", "h_full", "h_done", "y_full", "y_done", "y_ready",
                                           "added", "e_chain"))
            with ExitStack() as part:
                sbe = maker(part)
                xb = [sbe(f"xb{tag}{i}", [P, CT, ROW]) for i in range(2)]
                wfc = [sbe(f"wfc{tag}{i}", [P, F]) for i in range(2)]
                wpj = [sbe(f"wpj{tag}{i}", [P, FB, D]) for i in range(2)]
                bfc = [sbe(f"bfc{tag}{i}", [P, FB]) for i in range(2)]
                bpj = [sbe(f"bpj{tag}{i}", [P, D]) for i in range(2)]
                xbT = [sbe(f"xbT{tag}{i}", [P, CAP]) for i in range(2)]
                hT = [sbe(f"hT{tag}{i}", [P, FB, 512]) for i in range(2)]
                ys = [sbe(f"ys{tag}{i}", [P, CT, D]) for i in range(2)]
                pw = sbe(f"pw{tag}", [P, CT])
                pd = sbe(f"pd{tag}", [P, CT])
                ti = sbe(f"ti{tag}", [P, CT])
                ids = [sbe(f"ids{tag}{i}", [P, CT], i32) for i in range(2)]
                block = part.enter_context(nc.Block())
                t_bank, y_bank, h_bank = bank[0:2], bank[2:4], bank[4:8]

                @block.sync
                def _(sp):
                    def load_rows(e, q, at):
                        wait_apart(sp, t_full, NC * (e - 1))
                        wait_apart(sp, e_chain, EXPERT_STEPS * (e - 1))
                        sp.dma_start(xb[q][:], bucket[bass.ds(at, CAP), :].rearrange("(t p) c -> p t c", p=P)
                                     ).then_inc(rows_ld[q], 16)

                    def load_weights(e, q):
                        wait_apart(sp, y_done, NC * (e - 1))
                        sp.dma_start(wfc[q][:], c_fc.rearrange("e d f -> (e d) f")[bass.ds(e * D, D), :]
                                     ).then_inc(w_ld[q], 16)
                        sp.dma_start(wpj[q][:], c_proj.rearrange("e f d -> (e f) d")[bass.ds(e * F, F), :]
                                     .rearrange("(b p) d -> p b d", p=P)).then_inc(w_ld[q], 16)
                        sp.dma_start(bpj[q][:], proj_bias.rearrange("e o d -> (e o) d")[bass.ds(e, 1), :]
                                     .broadcast_to([P, D])).then_inc(w_ld[q], 16)

                    def load(h, q):
                        e = 2 * h + q
                        at = row_of(window, e)
                        if not final and not isinstance(h, int):
                            clear(sp, row_of(fill_at, e)).then_inc(cleared_rows, 16)
                            wait_apart(sp, cleared_rows, 16 * (e - 1))
                        load_rows(e, q, at)
                        load_weights(e, q)
                        if not final:
                            clear(sp, row_of(low_at, e)).then_inc(cleared_low, 16)

                    pairs(nc.sync, E // 2, load)
                    if not final:
                        sp.wait_ge(cleared_low, 16 * E)

                @block.tensor
                def _(pe):
                    def transposes(e, q, use, g):
                        t0, n = CHUNKS[g]
                        if g == 0:
                            pe.wait_ge(rows_ld[q], 16 * use + 16)
                        wait(pe, t_evac, NC * e + g - 1)
                        for t in range(n):
                            i = nc.tensor.transpose(t_bank[(g + NC * q) % 2][:, t * P:(t + 1) * P],
                                                    xb[q][:, t0 + t, 0:D], ident[:])
                        i.then_inc(t_full, 1)

                    def up(c, cc, q, e):
                        t0, n = CHUNKS[cc]
                        pe.wait_ge(t_evac, NC * e + cc + 1)
                        for b in range(FB):
                            wait(pe, h_done, FB * (c - 1) + b + 1)
                            nc.tensor.matmul(h_bank[b][:, 0:n * P], wfc[q][:, b * P:(b + 1) * P],
                                             xbT[q][:, t0 * P:(t0 + n) * P], start=True, stop=True).then_inc(h_full, 1)

                    def down(c, cc, q):
                        t0, n = CHUNKS[cc]
                        par = (cc + NC * q) % 2
                        pe.wait_ge(h_done, FB * (c + 1))
                        wait(pe, y_done, c - 1)
                        for t in range(n):
                            for b in range(FB):
                                i = nc.tensor.matmul(y_bank[par][:, t * P:(t + 1) * P], hT[par][:, b, t * P:(t + 1) * P],
                                                     wpj[q][:, b, :], start=b == 0, stop=b == FB - 1)
                        i.then_inc(y_full, 1)

                    def expert(e, q, use, more):
                        c = NC * e
                        pe.wait_ge(w_ld[q], 48 * use + 48)
                        up(c, 0, q, e)
                        up(c + 1, 1, q, e)
                        down(c, 0, q)
                        if more:
                            transposes(e + 1, 1 - q, use + q, 0)
                        up(c + 2, 2, q, e)
                        if more:
                            transposes(e + 1, 1 - q, use + q, 1)
                        down(c + 1, 1, q)
                        if more:
                            transposes(e + 1, 1 - q, use + q, 2)
                        down(c + 2, 2, q)

                    for g in range(NC):
                        transposes(0, 0, 0, g)
                    expert(0, 0, 0, True)
                    expert(1, 1, 0, True)
                    with nc.tensor.Fori(1, E // 2 - 1) as h:
                        expert(2 * h, 0, h, True)
                        expert(2 * h + 1, 1, h, True)
                    expert(E - 2, 0, E // 2 - 1, True)
                    expert(E - 1, 1, E // 2 - 1, False)

                @block.scalar
                def _(act):
                    def gelus(h, q):
                        e = 2 * h + q
                        for cc, (t0, n) in enumerate(CHUNKS):
                            c = NC * e + cc
                            par = (cc + NC * q) % 2
                            if cc == 0:
                                act.wait_ge(e_chain, EXPERT_STEPS * e + 1)
                            wait(act, y_full, c - 1)
                            for b in range(FB):
                                act.wait_ge(h_full, FB * c + b + 1)
                                nc.scalar.activation(hT[par][:, b, 0:n * P], h_bank[b][:, 0:n * P], ACT.Gelu,
                                                     bias=bfc[q][:, b:b + 1]).then_inc(h_done, 1)
                    pairs(nc.scalar, E // 2, gelus)

                @block.vector
                def _(dve):
                    def turned(e, q, g):
                        t0, n = CHUNKS[g]
                        dve.wait_ge(t_full, NC * e + g + 1)
                        if g == 0:
                            wait(dve, y_full, NC * (e - 1))
                        nc.vector.tensor_copy(xbT[q][:, t0 * P:(t0 + n) * P],
                                              t_bank[(g + NC * q) % 2][:, 0:n * P]).then_inc(t_evac, 1)

                    def numbers(e, q, use):
                        step = Steps(dve, e_chain, e * EXPERT_STEPS, EXPERT_STEPS)
                        wait(dve, h_done, FB * NC * (e - 1))
                        step(nc.vector.tensor_copy(bfc[q][:], bias_up[:, bass.ds(e * FB, FB)]))
                        dve.wait_ge(rows_ld[q], 16 * use + 16)
                        wait(dve, added, 16 * CT * (e - 1))
                        one, used = is_first[:, bass.ds(e, 1), :], is_used[:, bass.ds(e, 1), :]
                        one = one.rearrange("p o t -> p (o t)")
                        used = used.rearrange("p o t -> p (o t)")
                        nc.vector.tensor_scalar(ti[:], xb[q][:, :, C_ID], SKIP, None, ALU.subtract)
                        step(nc.vector.tensor_tensor(pd[:], xb[q][:, :, C_P0], xb[q][:, :, C_P1], ALU.subtract))
                        step(nc.vector.tensor_tensor(pd[:], pd[:], one, ALU.mult))
                        step(nc.vector.tensor_tensor(pd[:], pd[:], xb[q][:, :, C_P1], ALU.add))
                        step(nc.vector.tensor_tensor(ti[:], ti[:], used, ALU.mult))
                        step(nc.vector.scalar_tensor_tensor(pw[:], pd[:], 0.5, used, ALU.mult, ALU.mult))
                        step(nc.vector.tensor_scalar(ids[q][:], ti[:], SKIP, None, ALU.add))
                        step.end()

                    def weighted(e, q, cc):
                        t0, n = CHUNKS[cc]
                        c = NC * e + cc
                        par = (cc + NC * q) % 2
                        dve.wait_ge(y_full, c + 1)
                        y = ys[q][:, t0:t0 + n, :]
                        nc.vector.tensor_tensor(y, y_bank[par][:, 0:n * P].rearrange("p (t d) -> p t d", d=D),
                                                bpj[q][:, None, :].broadcast_to([P, n, D]), ALU.add).then_inc(y_done, 1)
                        dve.wait_ge(y_done, c + 1)
                        nc.vector.tensor_tensor(y, y, pw[:, t0:t0 + n, None].broadcast_to([P, n, D]),
                                                ALU.mult).then_inc(y_ready, 1)

                    def expert(e, q, use, more):
                        numbers(e, q, use)
                        dve.wait_ge(w_ld[q], 48 * use + 48)
                        weighted(e, q, 0)
                        for g in range(NC):
                            if more:
                                turned(e + 1, 1 - q, g)
                            if g > 0:
                                weighted(e, q, g)

                    for g in range(NC):
                        turned(0, 0, g)
                    expert(0, 0, 0, True)
                    expert(1, 1, 0, True)
                    with nc.vector.Fori(1, E // 2 - 1) as h:
                        expert(2 * h, 0, h, True)
                        expert(2 * h + 1, 1, h, True)
                    expert(E - 2, 0, E // 2 - 1, True)
                    expert(E - 1, 1, E // 2 - 1, False)

                @block.gpsimd
                def _(pool):
                    def send(h, q):
                        e = 2 * h + q
                        wait_apart(pool, added, e * CT * 16)
                        for cc, (t0, n) in enumerate(CHUNKS):
                            wait_apart(pool, y_ready, NC * e + cc + 1)
                            for t in range(t0, t0 + n):
                                nc.gpsimd.indirect_dma_start(
                                    dest, bass.IndirectOffsetOnAxis(ap=ids[q][:, t:t + 1], axis=0), ys[q][:, t, :],
                                    None, bounds_check=N - 1, oob_is_err=False, compute_op=ALU.add).then_inc(added, 16)

                    pairs(nc.gpsimd, E // 2, send)
                    wait_apart(pool, added, E * CT * 16)

        experts(1, mid, False)

        a_full, a_done, masked, pv_done, o_done, c_full, c_evac, parts_ok, v_copied = (
            sem(n) for n in ("a_full", "a_done", "masked", "pv_done", "o_done", "c_full", "c_evac", "parts_ok",
                             "v_copied"))
        st_full = [sem(f"st_full{i}") for i in range(2)]
        exp_done = [sem(f"exp_done{i}") for i in range(2)]
        qa_ld = [sem(f"qa_ld{i}") for i in range(2)]
        qb_ld = [sem(f"qb_ld{i}") for i in range(2)]
        kp_ld = [sem(f"kp_ld{i}") for i in range(NG)]
        max_ld = [[sem(f"max_ld{hf}{i}") for i in range(2)] for hf in range(2)]
        max_st, x1_ld, x2_ld, x2_st, x2_bias, stack_st = (
            sem(n) for n in ("max_st", "x1_ld", "x2_ld", "x2_st", "x2_bias", "stack_st"))
        n_stat, n_rstd, n_done, n_chain, part_one, rest_ok, split_ok, cleared, p_chain, v_ones, ctx_chain, win2 = (
            sem(n) for n in ("n_stat", "n_rstd", "n_done", "n_chain", "part_one", "rest_ok", "split_ok", "cleared",
                             "p_chain", "v_ones", "ctx_chain", "win2"))
        half_ok, r_num, n_pow = (sem(n) for n in ("half_ok", "r_num", "n_pow"))
        with ExitStack() as part:
            sba = maker(part)
            qa = [sba(f"qa{i}", [P, HS, S], bf16) for i in range(2)]
            qb = [sba(f"qb{i}", [P, HS, S], bf16) for i in range(2)]
            kp = [sba(f"kp{i}", [P, HS // 2, S], bf16) for i in range(NG)]
            pt = [sba(f"pt{i}", [P, HS, 512]) for i in range(PTS)]
            v_all = sba("v_all", [P, B * T, NH, DH + 1])
            vs = [sba(f"vs{i}", [P, T, HS, VW]) for i in range(2)]
            o_sb = sba("o_sb", [P, S])
            ctx = sba("ctx", [P, T, D])
            ctxT = sba("ctxT", [P, S])
            x1 = sba("x1", [P, T, D])
            xn = sba("xn", [P, T, D])
            xnT = sba("xnT", [P, S])
            x2 = sba("x2", [P, T, D])
            parts = [[sba(f"{n}{j}", [P, S], bf16) for j in range(3)] for n in ("qp", "kq")]
            rest = sba("rest", [P, 2, 512])
            n_st = sba("n_st", [P, T, 6])
            n_mv = sba("n_mv", [P, T, 2])
            n_var = sba("n_var", [P, T])
            n_rs = sba("n_rs", [P, T])
            n_negm = sba("n_negm", [P, T])
            n_shift = sba("n_shift", [P, T])
            m_units = sba("m_units", [P, T, T // 2 + 1, HS])
            m_of = [sba(f"m_of{i}", [P, HS, T // 2]) for i in range(2)]
            m_neg = sba("m_neg", [P, HS, T // 2])
            m_parts = [sba(f"m_parts{i}", [P, 3, HS, T // 2], bf16) for i in range(2)]
            MR = 3 * HS * T // 2
            m_rows = [sba(f"m_rows{i}", [MR, P], bf16) for i in range(2)]
            recip = sba("recip", [P, T // 2, HS])
            block = part.enter_context(nc.Block())
            a_bank, o_bank, c_bank = bank[4:6], bank[6], bank[7]
            m_bank = c_bank.bitcast(bf16)
            PRO_BANK = {name: bank[i] for i, name in enumerate(PRO[:8])}
            TAIL_BANK = {name: bank[i % 4] for i, name in enumerate(TAIL[1:])}
            two = two_banks[0:2]

            class Batch:
                def __init__(self, b, kind):
                    self.b, self.kind = b, kind
                    self.first, self.final = kind == "first", kind == "final"
                    uses = {"first": FIRST_USES, "mid": MID_USES, "final": LAST_USES}[kind]
                    if self.first:
                        base = len(PRO)
                    else:
                        base = len(PRO) + len(FIRST_USES) + (b - 1) * len(MID_USES)
                    self.at = {name: base + i for i, name in enumerate(uses)}

            pro_at = {name: i for i, name in enumerate(PRO)}
            tail_at = {name: TAIL_AT + i for i, name in enumerate(TAIL)}

            def bank_of(at, name):
                if at is pro_at:
                    return PRO_BANK[name]
                return TAIL_BANK[name] if at is tail_at else c_bank

            def sweep(eng, step):
                for g in range(NG):
                    step(Batch(0, "first"), g)
                with eng.Fori(1, B - 1) as b:
                    for g in range(NG):
                        step(Batch(b, "mid"), g)
                for g in range(NG):
                    step(Batch(B - 1, "final"), g)

            R2_USE = B // 2

            LOADS = 2 * 16
            STORES = 2 * (KS // DH) * 16

            @block.sync
            def _(sp):
                def load_stack(dst, stack, b, g, done):
                    src = stack[bass.ds(b * NH * KS + g * HS * KS, HS * KS), :].rearrange("(i s r) n -> s r i n", s=2, r=KS)
                    for s in range(2):
                        sp.dma_start(dst(s), src[s]).then_inc(done, 16)

                def load_q(dst, b, g, done):
                    load_stack(lambda s: dst[64 * s:64 * s + KS].rearrange("p (i s) n -> p s i n", s=2)[:, s],
                               q_stack, b, g, done)

                def load_k(b, g):
                    load_stack(lambda s: kp[g][64 * s:64 * s + KS], k_stack, b, g, kp_ld[g])

                def step(bt, g):
                    b, at = bt.b, bt.at
                    n, p = NG * b + g, g % 2
                    more = not (bt.final and g == NG - 1)
                    if g == 0:
                        if not bt.final:
                            wait_apart(sp, n_done, b + 1)
                            sp.dma_start(x1[:], mid[bass.ds((b + 1) * S, S), :].rearrange("(t p) d -> p t d", p=P)
                                         ).then_inc(x1_ld, 16)
                        if not bt.first:
                            wait_apart(sp, r_rows, B + b - 1)
                            sp.dma_start(x2[:], mid[bass.ds((b - 1) * S, S), :].rearrange("(t p) d -> p t d", p=P)
                                         ).then_inc(x2_ld, 16)
                    if more:
                        wait_apart(sp, st_full[1], NU * n)
                        nb, ng = (b, g + 1) if g < NG - 1 else (b + 1, 0)
                        load_q(qb[1 - p], nb, ng, qb_ld[1 - p])
                    move(at[("max0", g)], 0, b, g, 2 * n + 1)
                    if g == 1 and not bt.first:
                        store_x2(at, b - 1)
                    if g == 2 and not bt.first:
                        wait_apart(sp, x2_st, 16 * b)
                    if g == 2 and not bt.final:
                        store_stacks(b + 1)
                    if not (bt.final and g >= 2):
                        nb, ng = (b, g + 2) if g < 2 else (b + 1, g - 2)
                        if g >= 2:
                            wait_apart(sp, stack_st, STORES * (b + 2))
                        load_q(qa[p], nb, ng, qa_ld[p])
                        load_k(nb, ng)
                    if more:
                        nb, ng = (b, g + 1) if g < NG - 1 else (b + 1, 0)
                        move(at[("max1", g + 1)], 1, nb, ng, 2 * n + 2)

                def move(use, hf, b, g, k):
                    par = g % 2
                    wait_apart(sp, c_evac, use + 1)
                    wait_apart(sp, max_ld[hf][1 - par], 32 * (2 * b + (g + 1) // 2))
                    flat = max_rows.rearrange("r (t q) -> (r t) q", q=P)
                    sp.dma_start(flat[hf * MR:(hf + 1) * MR, :], m_rows[hf][:]).then_inc(max_st, 16)
                    wait_apart(sp, max_st, 16 * (k + 1))
                    for s in range(2):
                        src = max_rows[hf * 3 * HS:(hf + 1) * 3 * HS, :].rearrange("(c i s) n -> s c i n", c=3, s=2)[s]
                        dst = qb[par][64 * s + KS:64 * s + KS + 3].rearrange("p (i s) n -> p s i n", s=2)[:, s, :,
                                                                            hf * HALF:(hf + 1) * HALF]
                        sp.dma_start(dst, src).then_inc(max_ld[hf][par], 16)

                def store_stacks(b):
                    wait_apart(sp, split_ok, 4 * (b + 1))
                    for stack, tiles, order in ((q_stack, parts[0], Q_PART), (k_stack, parts[1], K_PART)):
                        for c, j in enumerate(order):
                            dst = stack[bass.ds(b * NH * KS, NH * KS), :].rearrange("(h c d) n -> c h d n", h=NH, d=DH)[c]
                            sp.dma_start(dst, tiles[j][:]).then_inc(stack_st, 16)

                def store_first_stacks():
                    for j in range(3):
                        for which, stack, order in ((0, q_stack, Q_PART), (1, k_stack, K_PART)):
                            if j == 0:
                                sp.wait_ge(part_one, 2 * which + 2)
                            elif j == 1:
                                sp.wait_ge(rest_ok, 2 * which + 2)
                            else:
                                sp.wait_ge(split_ok, 2 * which + 2)
                            for c in range(len(order)):
                                if order[c] == j:
                                    dst = stack[0:NH * KS, :].rearrange("(h c d) n -> c h d n", h=NH, d=DH)[c]
                                    sp.dma_start(dst, parts[which][j][:]).then_inc(stack_st, 16)

                def store_x2(at, b):
                    wait_apart(sp, c_evac, at["o_p1"] + 1)
                    sp.dma_start(last[bass.ds(b * S, S), :].rearrange("(t p) d -> p t d", p=P), x2[:]).then_inc(x2_st, 16)

                sp.dma_start(x1[:], mid[0:S, :].rearrange("(t p) d -> p t d", p=P)).then_inc(x1_ld, 16)
                store_first_stacks()
                wait_apart(sp, stack_st, STORES)
                wait_apart(sp, cleared, 2)
                load_q(qa[0], 0, 0, qa_ld[0])
                load_k(0, 0)
                load_q(qb[0], 0, 0, qb_ld[0])
                load_q(qa[1], 0, 1, qa_ld[1])
                load_k(0, 1)
                move(pro_at[("max1", 0)], 1, 0, 0, 0)
                sweep(nc.sync, step)
                b = B - 1
                wait_apart(sp, r_rows, B + b)
                sp.dma_start(x2[:], mid[b * S:(b + 1) * S, :].rearrange("(t p) d -> p t d", p=P)).then_inc(x2_ld, 16)
                store_x2(tail_at, b)
                wait_apart(sp, x2_st, 16 * B)

            @block.tensor
            def _(pe):
                def score(par, g, b, n, u, pair):
                    hf, kb = UNITS[u]
                    q0, w = unit_queries(u)
                    wait(pe, exp_done[pair], NU * n + u)
                    for s in range(2):
                        i = nc.tensor.matmul(two[pair][:, s, 0:w], kp[g][:, pair, kb * P:(kb + 1) * P],
                                             qb[par][:, 2 * pair + s, q0:q0 + w], start=True, stop=True)
                    i.then_inc(st_full[pair], 1)

                def maxima(n, g, b, a0, a1):
                    par = g % 2
                    for a in range(a0, a1):
                        qt, heads, k0, w, diag, _ = AUNITS[a]
                        if a == 0:
                            pe.wait_ge(qa_ld[par], LOADS * uses_of(b, g))
                            pe.wait_ge(kp_ld[g], LOADS * (b + 1))
                        wait(pe, a_done, NA * n + a - 1)
                        if diag:
                            nc.tensor.matmul(a_bank[a % 2], identb[:], causal[:].rearrange("p h k -> p (h k)"),
                                             start=True, stop=False)
                        for j, h in enumerate(heads):
                            i = nc.tensor.matmul(a_bank[a % 2][:, j * w:(j + 1) * w], qa[par][:, h, qt * P:(qt + 1) * P],
                                                 kp[g][:, h // 2, k0:k0 + w], start=not diag,
                                                 stop=not diag or j == len(heads) - 1)
                        i.then_inc(a_full, 1)

                def uses_of(b, g):
                    return 2 * b + g // 2 + 1

                def values(par, n, u, side):
                    hf, kb = UNITS[u]
                    q0, w = unit_queries(u)
                    sides = 2 if w > HALF // 2 else 1
                    if side == sides:
                        return
                    c0, cw = side * w // 2, w // sides
                    if u in (0, T) and side == 0:
                        wait(pe, o_done, 2 * n + u // T)
                        if u == 0:
                            pe.wait_ge(v_copied, n + 1)
                    if side == 0:
                        if u in MASKED:
                            pe.wait_ge(masked, len(MASKED) * n + MASKED.index(u) + 1)
                        else:
                            pe.wait_ge(exp_done[1], NU * n + u + 1)
                    q = q0 - hf * HALF + c0
                    for h in range(HS):
                        i = nc.tensor.matmul(o_bank[VW * h:VW * h + VW, q:q + cw],
                                             vs[par][:, kb, h, :], pt[u % PTS][:, h, c0:c0 + cw],
                                             start=u in (0, T) and side == 0,
                                             stop=u in (T - 1, NU - 1) and side == sides - 1)
                    if side == sides - 1:
                        i.then_inc(pv_done, 1)

                def bank_free(use):
                    wait(pe, c_evac, use)

                def max_rows_of(use, n, hf):
                    bank_free(use)
                    wait_apart(pe, parts_ok, 2 * n + (1 if hf else 2))
                    nc.tensor.transpose(m_bank[0:MR, 0:P], m_parts[hf][:].rearrange("p c h t -> p (c h t)"),
                                        identb[:]).then_inc(c_full, 1)

                def turn(use, src, half, to=c_bank):
                    if to is c_bank:
                        bank_free(use)
                    for t in range(4):
                        i = nc.tensor.transpose(to[:, t * P:(t + 1) * P], src(4 * half + t), ident[:])
                    i.then_inc(c_full, 1)

                def context(use, n, hf):
                    pe.wait_ge(o_done, 2 * n + (1 if hf else 2))
                    turn(use, lambda t: o_sb[:, t * P:(t + 1) * P], hf)

                def project(use, w, half, to, ready):
                    bank_free(ready)
                    nc.tensor.matmul(to, w[:], xnT[:, half * 512:half * 512 + 512], start=True,
                                     stop=True).then_inc(c_full, 1)

                def by_token(use, srcT, w, half, to, ready):
                    bank_free(ready)
                    for t in range(4):
                        c = (4 * half + t) * P
                        i = nc.tensor.matmul(to[:, t * P:(t + 1) * P], srcT[:, c:c + P], w[:], start=True, stop=True)
                    i.then_inc(c_full, 1)

                def norm_task(at, name, b):
                    if name == "x_t0":
                        pe.wait_ge(n_done, b + 1)
                    to = bank_of(at, name)
                    ready = at[name] if to is c_bank else at["x_t1"] + 1
                    if name in ("x_t0", "x_t1"):
                        turn(at[name], lambda t: xn[:, t, :], int(name[-1]), to)
                    elif name[0] in "qk":
                        project(at[name], wqT if name[0] == "q" else wkT, int(name[-1]), to, ready)
                    else:
                        by_token(at[name], xnT, wvT, int(name[-1]), to, ready)

                def out_task(at, name, call):
                    to = bank_of(at, name)
                    if name in ("o_t0", "o_t1"):
                        if to is not c_bank:
                            bank_free(at[name])
                        turn(at[name], lambda t: ctx[:, t, :], int(name[-1]), to)
                    elif name in ("o_p0", "o_p1"):
                        by_token(at[name], ctxT, woT, int(name[-1]), to,
                                 at[name] if to is c_bank else at["o_t1"] + 1)
                    elif name in ("r_t0", "r_t1"):
                        if to is c_bank or name == "r_t0":
                            bank_free(at[name])
                        router_transpose(pe, call, 0, int(name[-1]), to, c_full)
                    elif name == "r_lg":
                        bank_free(at[name])
                        router_logits(pe, to, c_full)
                    else:
                        bank_free(at[name])
                        router_ranks(pe, call, to, c_full)

                def step(bt, g):
                    b, at = bt.b, bt.at
                    n, par = NG * b + g, g % 2
                    more = not (bt.final and g == NG - 1)
                    nb, ng = (b, g + 1) if g < NG - 1 else (b + 1, 0)
                    pe.wait_ge(qb_ld[par], LOADS * uses_of(b, g))
                    for u in range(NU):
                        if u == 0:
                            pe.wait_ge(max_ld[1][par], 32 * uses_of(b, g))
                        if u == T:
                            pe.wait_ge(max_ld[0][par], 32 * uses_of(b, g))
                        a0, a3 = A_FROM[u], A_FROM[u + 1]
                        for i in range(4):
                            if i < 2:
                                score(par, g, b, n, u, i)
                            elif u >= LAG:
                                values(par, n, u - LAG, i - 2)
                            elif not (bt.first and g == 0):
                                values(1 - par, n - 1, NU - LAG + u, i - 2)
                            if more and a0 + i < a3:
                                maxima(n + 1, ng, nb, a0 + i, a0 + i + 1)
                        if u == 1:
                            max_rows_of(at[("max0", g)], n, 0)
                        if u == 2 and ("ctx0", g - 1) in at:
                            context(at[("ctx0", g - 1)], n - 1, 0)
                        if g == 0 and not bt.first and 3 <= u <= 6:
                            out_task(at, ("o_t0", "o_t1", "o_p0", "o_p1")[u - 3], B + b - 1)
                        if g == 1 and not bt.final and 3 <= u <= 7:
                            norm_task(at, ("x_t0", "x_t1", "q0", "q1", "k0")[u - 3], b + 1)
                        if g == 2 and not bt.first and 3 <= u <= 5:
                            out_task(at, ("r_t0", "r_t1", "r_lg")[u - 3], B + b - 1)
                        if g == 3 and not bt.final and 3 <= u <= 4:
                            norm_task(at, ("v0", "v1")[u - 3], b + 1)
                        if u == U_MA and more:
                            max_rows_of(at[("max1", g + 1)], n + 1, 1)
                        if u == 9 and g == 1 and not bt.final:
                            norm_task(at, "k1", b + 1)
                        if u == 9 and g == 2 and not bt.first:
                            out_task(at, "r_rk", B + b - 1)
                        if u == NU - 1:
                            context(at[("ctx1", g)], n, 1)

                for name in PRO[:-1]:
                    norm_task(pro_at, name, 0)
                pe.wait_ge(cleared, 2)
                maxima(0, 0, 0, 0, NA1 + 4)
                max_rows_of(pro_at[("max1", 0)], 0, 1)
                maxima(0, 0, 0, NA1 + 4, NA)
                sweep(nc.tensor, step)
                for u in range(NU - LAG, NU):
                    for side in range(2):
                        values((NG * B - 1) % 2, NG * B - 1, u, side)
                context(tail_at[("ctx0", NG - 1)], NG * B - 1, 0)
                for name in TAIL[1:]:
                    out_task(tail_at, name, 2 * B - 1)

            @block.scalar
            def _(act):
                def take(use, dst, src=None):
                    act.wait_ge(c_full, use + 1)
                    nc.scalar.copy(dst, c_bank if src is None else src).then_inc(c_evac, 1)

                def take_max(use, k, hf):
                    wait(act, max_st, 16 * k)
                    take(use, m_rows[hf][:], m_bank[0:MR, 0:P])

                def take_o(n, hf, read):
                    act.wait_ge(pv_done, NU * n + (T if hf else NU))
                    wait(act, c_full, read)
                    nc.scalar.copy(o_sb[:, hf * HALF:(hf + 1) * HALF], o_bank).then_inc(o_done, 1)

                def first_part(use, b, which, half, src):
                    act.wait_ge(c_full, use + 1)
                    if half == 0:
                        wait(act, stack_st, STORES * b)
                    nc.scalar.activation(parts[which][0][:, half * 512:half * 512 + 512], src, ACT.Identity,
                                         bias=(bq_c, bk_c)[which][:]).then_inc(part_one, 1)

                def norm_task(at, name, b):
                    half = int(name[-1])
                    if name[0] == "x":
                        take(at[name], xnT[:, half * 512:half * 512 + 512], bank_of(at, name))
                    elif name[0] in "qk":
                        first_part(at[name], b, "qk".index(name[0]), half, bank_of(at, name))

                def second_part(use, which, half):
                    s = slice(half * 512, half * 512 + 512)
                    act.wait_ge(c_evac, use + 1)
                    nc.scalar.copy(parts[which][1][:, s], rest[:, half, :]).then_inc(rest_ok, 1)

                def out_take(at, name):
                    half = int(name[-1])
                    dst = ctxT if name[0] == "o" else xT
                    take(at[name], dst[:, half * 512:half * 512 + 512], bank_of(at, name))

                def norm(b, t0, t1):
                    act.wait_ge(n_rstd, b + 1)
                    for t in range(t0, t1):
                        i = nc.scalar.activation(xn[:, t, :], x1[:, t, :], ACT.Identity, scale=n_rs[:, t:t + 1],
                                                 bias=n_shift[:, t:t + 1])
                    if t1 == T:
                        i.then_inc(n_done, 1)

                def norm_out(k, t0, t1):
                    if t0 == 0:
                        act.wait_ge(r_shift, k + 1)
                        act.wait_ge(r_num, k + 1)
                    for t in range(t0, t1):
                        i = nc.scalar.activation(rows[0][:, t, 0:D], x2[:, t, :], ACT.Identity, scale=rstd[:, t:t + 1],
                                                 bias=shift[:, t:t + 1])
                    if t1 == T:
                        i.then_inc(r_rows, 1)

                def step(bt, g):
                    b, at = bt.b, bt.at
                    n = NG * b + g
                    more = not (bt.final and g == NG - 1)
                    for u in range(NU):
                        q0, w = unit_queries(u)
                        for pair in range(2):
                            if pair == 0:
                                wait(act, pv_done, NU * n + u - PTS + 1)
                            act.wait_ge(st_full[pair], NU * n + u + 1)
                            nc.scalar.activation(pt[u % PTS][:, 2 * pair:2 * pair + 2, 0:w], two[pair][:, :, 0:w], ACT.Exp,
                                                 scale=SCALE).then_inc(exp_done[pair], 1)
                        if u == LAG - 1 and not (bt.first and g == 0):
                            take_o(n - 1, 0, at[("max0", g)])
                        if u == 1:
                            take_max(at[("max0", g)], 2 * n + 1, 0)
                        if g == 0 and not bt.first and 3 <= u <= 4:
                            out_take(at, ("o_t0", "o_t1")[u - 3])
                        if g == 1 and not bt.final and 3 <= u <= 7:
                            norm_task(at, ("x_t0", "x_t1", "q0", "q1", "k0")[u - 3], b + 1)
                        if g == 1 and not bt.final and u in (6, 7, 8, 10):
                            k = (6, 7, 8, 10).index(u)
                            second_part(at[("q0", "q1", "k0", "k1")[k]], k // 2, k % 2)
                        if g == 2 and not bt.first and 3 <= u <= 4:
                            out_take(at, ("r_t0", "r_t1")[u - 3])
                        if g == 0 and not bt.final and u >= 10:
                            norm(b + 1, (u - 10) * T // 2, (u - 9) * T // 2)
                        if g == 1 and not bt.first and 1 <= u <= 2:
                            norm_out(b - 1, (u - 1) * T // 2, u * T // 2)
                        if u == T + LAG - 1:
                            take_o(n, 1, at[("max0", g)] + 1)
                        if u == U_MA and more:
                            take_max(at[("max1", g + 1)], 2 * n + 2, 1)
                        if u == 9 and g == 1 and not bt.final:
                            norm_task(at, "k1", b + 1)
                        if u == 9 and g == 2 and not bt.first:
                            router_exp(act, B + b - 1)

                for name in ("x_t0", "x_t1", "q0", "q1"):
                    norm_task(pro_at, name, 0)
                second_part(pro_at["q0"], 0, 0)
                norm_task(pro_at, "k0", 0)
                second_part(pro_at["q1"], 0, 1)
                norm_task(pro_at, "k1", 0)
                second_part(pro_at["k0"], 1, 0)
                second_part(pro_at["k1"], 1, 1)
                take_max(pro_at[("max1", 0)], 0, 1)
                sweep(nc.scalar, step)
                take_o(NG * B - 1, 0, tail_at[("ctx0", NG - 1)])
                for name in ("o_t0", "o_t1"):
                    out_take(tail_at, name)
                for name in ("r_t0", "r_t1"):
                    out_take(tail_at, name)
                router_exp(act, 2 * B - 1)

            @block.vector
            def _(dve):
                def reduce(n, a):
                    qt, heads, k0, w, diag, at = AUNITS[a]
                    dve.wait_ge(a_full, NA * n + a + 1)
                    nc.vector.tensor_reduce(m_units[:, qt, at, heads[0]:heads[-1] + 1],
                                            a_bank[a % 2].rearrange("p (h k) -> p h k", k=w), AX.X,
                                            ALU.max).then_inc(a_done, 1)
                    if a in (NA1 - 1, NA - 1):
                        hf = int(a < NA1)
                        wait(dve, parts_ok, 2 * n - hf)
                        dve.wait_ge(a_done, NA * n + a + 1)
                        nc.vector.tensor_reduce(m_of[hf][:], m_units[:, hf * T // 2:(hf + 1) * T // 2, :, :]
                                                .rearrange("p t c h -> p h t c"), AX.X, ALU.max).then_inc(half_ok, 1)

                def context(use, n, g, hf):
                    dve.wait_ge(c_full, use + 1)
                    v = c_bank.rearrange("p (t h w) -> p t h w", t=4, h=HS)
                    nc.vector.reciprocal(recip[:], v[:, :, :, DH]).then_inc(ctx_chain, 1)
                    dve.wait_ge(ctx_chain, 2 * n + (1 if hf else 2))
                    nc.vector.tensor_tensor(
                        ctx[:, 4 * hf:4 * hf + 4, g * HS * DH:(g + 1) * HS * DH].rearrange("p t (h d) -> p t h d", h=HS),
                        v[:, :, :, 0:DH], recip[:, :, :, None].broadcast_to([P, 4, HS, DH]), ALU.mult).then_inc(c_evac, 1)

                def sums(b):
                    dve.wait_ge(x1_ld, 16 * (b + 1))
                    for t in range(T):
                        i = nc.vector.bn_stats(n_st[:, t, :], x1[:, t, :])
                    i.then_inc(n_chain, 1)

                def moments(b):
                    wait_apart(dve, n_chain, 2 * b + 1)
                    for t in range(T):
                        i = nc.vector.bn_aggr(n_mv[:, t, :], n_st[:, t, :])
                    i.then_inc(n_chain, 1)
                    dve.wait_ge(n_chain, 2 * b + 2)
                    nc.vector.tensor_scalar(n_negm[:], n_mv[:, :, 0], -1.0, None, ALU.mult)
                    nc.vector.tensor_scalar(n_var[:], n_mv[:, :, 1], EPS, None, ALU.add).then_inc(n_stat, 1)

                def norm(b):
                    dve.wait_ge(n_rstd, b + 1)
                    for t in range(T):
                        i = nc.vector.tensor_scalar(xn[:, t, :], x1[:, t, :], n_mv[:, t, 0:1], n_rs[:, t:t + 1],
                                                    ALU.subtract, ALU.mult)
                    i.then_inc(n_done, 1)

                def third_part(which, half):
                    s = slice(half * 512, half * 512 + 512)
                    dve.wait_ge(rest_ok, 2 * which + half + 1)
                    nc.vector.tensor_tensor(parts[which][2][:, s], rest[:, half, :], parts[which][1][:, s],
                                            ALU.subtract).then_inc(split_ok, 1)

                def remainder(use, b, which, half, src):
                    k = 4 * b + 2 * which + half
                    dve.wait_ge(part_one, k + 1)
                    wait(dve, split_ok, k - 1)
                    nc.vector.scalar_tensor_tensor(rest[:, half, :], src, (bq_c, bk_c)[which][:],
                                                   parts[which][0][:, half * 512:half * 512 + 512],
                                                   ALU.add, ALU.subtract).then_inc(c_evac, 1)

                def norm_task(at, name, b):
                    half = int(name[-1])
                    if name[0] in "qk":
                        remainder(at[name], b, "qk".index(name[0]), half, bank_of(at, name))
                    elif name[0] == "v":
                        dve.wait_ge(c_full, at[name] + 1)
                        nc.vector.tensor_tensor(
                            v_all[:, bass.ds(b * T + 4 * half, 4), :, 0:DH],
                            bank_of(at, name).rearrange("p (t h d) -> p t h d", t=4, d=DH),
                            bv_r[:].rearrange("p (h d) -> p h d", d=DH)[:, None, :, :].broadcast_to([P, 4, NH, DH]),
                            ALU.add).then_inc(c_evac, 1)

                def add_out(at, name, b):
                    half = int(name[-1])
                    dve.wait_ge(c_full, at[name] + 1)
                    dve.wait_ge(x2_bias, b + 1)
                    v = x2[:, 4 * half:4 * half + 4, :]
                    nc.vector.tensor_tensor(v, bank_of(at, name).rearrange("p (t d) -> p t d", t=4), v,
                                            ALU.add).then_inc(c_evac, 1)

                held = {}

                def out_task(at, name, b):
                    call = B + b
                    if name in ("o_p0", "o_p1"):
                        add_out(at, name, b)
                    elif name == "r_lg":
                        dve.wait_ge(c_full, at[name] + 1)
                        held["step"] = router_top2(dve, bank_of(at, name), call * ROUTER_STEPS + 2, c_evac, at[name] + 1)
                    elif name == "r_rk":
                        dve.wait_ge(c_full, at[name] + 1)
                        router_rank(bank_of(at, name), c_evac, held["step"])

                def step(bt, g):
                    b, at = bt.b, bt.at
                    n = NG * b + g
                    more = not (bt.final and g == NG - 1)
                    for u in range(NU):
                        for a in range(A_FROM[u], A_FROM[u + 1]) if more else ():
                            reduce(n + 1, a)
                            if g == 0 and not bt.first and NA1 <= a < NA1 + T:
                                t = a - NA1
                                if t == 0:
                                    dve.wait_ge(c_evac, at["o_p1"] + 1)
                                router_sums(x2, t, t + 1)
                        if u == 2 and ("ctx0", g - 1) in at:
                            context(at[("ctx0", g - 1)], n - 1, (g - 1) % NG, 0)
                        if g == 0 and not bt.first and 5 <= u <= 6:
                            out_task(at, ("o_p0", "o_p1")[u - 5], b - 1)
                        if g == 0 and not bt.final and u == 7:
                            sums(b + 1)
                        if g == 0 and not bt.final and u == 8:
                            moments(b + 1)
                        if g == 0 and not bt.first and u == NU - 1:
                            router_moments(dve, (B + b - 1) * ROUTER_STEPS)
                        if g == 1 and not bt.first and u == 0:
                            router_numbers(dve, 0, b - 1 + R2_USE).then_inc(r_num, 1)
                        if g == 1 and not bt.final and 5 <= u <= 7:
                            norm_task(at, ("q0", "q1", "k0")[u - 5], b + 1)
                        if g == 1 and not bt.final and u == 9:
                            norm_task(at, "k1", b + 1)
                        if g == 2 and not bt.first and u == 6:
                            out_task(at, "r_lg", b - 1)
                        if g == 3 and not bt.final and 3 <= u <= 4:
                            norm_task(at, ("v0", "v1")[u - 3], b + 1)
                        if g == 2 and not bt.first and u == 9:
                            out_task(at, "r_rk", b - 1)
                        if g == 2 and not bt.first and u == 10:
                            router_rows(dve, B + b - 1, 0, held["step"])
                        if u == NU - 1:
                            context(at[("ctx1", g)], n, g, 1)

                nc.vector.memset(m_units[:], NEG)
                nc.vector.tensor_copy(tok_id[:], tok_id0[:])
                nc.vector.memset(taken[:], 0.0)
                sums(0)
                moments(0)
                nc.vector.memset(qa[0][:], 0.0)
                norm(0)
                for t_ in qa[1:] + qb:
                    i = nc.vector.memset(t_[:], 0.0)
                i.then_inc(cleared, 1)
                norm_task(pro_at, "q0", 0)
                norm_task(pro_at, "q1", 0)
                third_part(0, 0)
                norm_task(pro_at, "k0", 0)
                third_part(0, 1)
                norm_task(pro_at, "k1", 0)
                third_part(1, 0)
                third_part(1, 1)
                norm_task(pro_at, "v0", 0)
                norm_task(pro_at, "v1", 0)
                for a in range(NA):
                    reduce(0, a)
                sweep(nc.vector, step)
                b = B - 1
                context(tail_at[("ctx0", NG - 1)], NG * B - 1, NG - 1, 0)
                for half in range(2):
                    out_task(tail_at, ("o_p0", "o_p1")[half], b)
                    dve.wait_ge(c_evac, tail_at["o_p0"] + half + 1)
                    router_sums(x2, half * T // 2, (half + 1) * T // 2)
                router_moments(dve, (B + b) * ROUTER_STEPS)
                router_norm(dve, x2, B + b, 0, b + R2_USE)
                out_task(tail_at, "r_lg", b)
                out_task(tail_at, "r_rk", b)
                router_rows(dve, B + b, 0, held["step"])
                dve.wait_ge(r_chain, 2 * B * ROUTER_STEPS)
                router_windows(dve, win2, 0)

            @block.gpsimd
            def _(pool):
                PART_STEPS = 4

                def split_max(n, hf, k, used):
                    wait_apart(pool, half_ok, 2 * n + (1 if hf else 2))
                    wait_apart(pool, c_full, used)
                    wait_apart(pool, parts_ok, k)
                    base, c = PART_STEPS * k, [0]

                    def step(i):
                        c[0] += 1
                        i.then_inc(p_chain, 1)
                        wait_apart(pool, p_chain, base + c[0])

                    mp = m_parts[hf]
                    step(nc.gpsimd.tensor_scalar(m_neg[:], m_of[hf][:], -1.0, None, ALU.mult))
                    step(nc.gpsimd.tensor_copy(mp[:, 0], m_neg[:]))
                    step(nc.gpsimd.tensor_tensor(m_neg[:], m_neg[:], mp[:, 0], ALU.subtract))
                    step(nc.gpsimd.tensor_copy(mp[:, 1], m_neg[:]))
                    nc.gpsimd.tensor_tensor(mp[:, 2], m_neg[:], mp[:, 1], ALU.subtract).then_inc(parts_ok, 1)

                def third_part(b, which, half):
                    k = 4 * b + 2 * which + half
                    s = slice(half * 512, half * 512 + 512)
                    wait_apart(pool, rest_ok, k + 1)
                    nc.gpsimd.tensor_tensor(parts[which][2][:, s], rest[:, half, :], parts[which][1][:, s],
                                            ALU.subtract).then_inc(split_ok, 1)

                def copy_v(b, g, n, ready):
                    wait_apart(pool, pv_done, NU * (n - 1))
                    if g == 0:
                        wait_apart(pool, c_evac, ready)
                    nc.gpsimd.tensor_copy(vs[g % 2][:, :, :, 0:DH + 1],
                                          v_all[:, bass.ds(b * T, T), g * HS:(g + 1) * HS, :]).then_inc(v_copied, 1)

                def mask(n, u):
                    wait_apart(pool, exp_done[1], NU * n + u + 1)
                    v = pt[u % PTS][:, :, 0:P]
                    nc.gpsimd.affine_select(out=v, in_=v, compare_op=ALU.is_ge, fill=0.0, base=0,
                                            pattern=[[0, HS], [1, P]], channel_multiplier=-1).then_inc(masked, 1)

                def rstd1(b):
                    wait_apart(pool, n_stat, b + 1)
                    nc.gpsimd.tensor_tensor(n_rs[:], n_var[:], half_neg[:], ALU.pow).then_inc(n_pow, 1)
                    wait_apart(pool, n_pow, b + 1)
                    nc.gpsimd.tensor_tensor(n_shift[:], n_negm[:], n_rs[:], ALU.mult).then_inc(n_rstd, 1)

                def bias_x2(b):
                    wait_apart(pool, x2_ld, 16 * (b + 1))
                    nc.gpsimd.tensor_tensor(x2[:], x2[:], bo_r[:, None, :].broadcast_to([P, T, D]), ALU.add).then_inc(x2_bias, 1)

                def step(bt, g):
                    b, at = bt.b, bt.at
                    n = NG * b + g
                    more = not (bt.final and g == NG - 1)
                    nb, ng = (b, g + 1) if g < NG - 1 else (b + 1, 0)
                    for u in range(NU):
                        if u == (8 if g == 3 else LAG) and more:
                            copy_v(nb, ng, n + 1, at[("max1", g + 1)])
                        if u in MASKED:
                            mask(n, u)
                        if g == 0 and not bt.first and u == 3:
                            bias_x2(b - 1)
                        if u == 7 and more:
                            split_max(n + 1, 1, 2 * n + 2, at[("max0", g)] + 1)
                        if g == 0 and not bt.final and u == 9:
                            rstd1(b + 1)
                        if g == 1 and not bt.final and u in (6, 7, 8, 10):
                            k = (6, 7, 8, 10).index(u)
                            third_part(b + 1, k // 2, k % 2)
                        if g == 1 and not bt.first and u == 0:
                            router_rstd(pool, B + b - 1)
                            router_shift(pool, b - 1)
                        if g == 3 and not bt.first:
                            if u == 0:
                                wait_apart(pool, r_idx, B + b)
                            for k in (range(3 * u, 3 * u + 3) if u < 4 else range(u + 8, min(u + 9, TOPK * T))):
                                router_scatter(pool, 0, k)
                        if u == NU - 1 and more:
                            split_max(n + 1, 0, 2 * n + 3, at[("max1", g + 1)] + 1)

                nc.gpsimd.memset(kp[0][:], 1.0)
                rstd1(0)
                for t_ in kp[1:]:
                    i = nc.gpsimd.memset(t_[:], 1.0)
                i.then_inc(cleared, 1)
                for t_ in vs:
                    nc.gpsimd.memset(t_[:], 0.0)
                nc.gpsimd.memset(v_all[:, :, :, DH], 1.0).then_inc(v_ones, 1)
                wait_apart(pool, v_ones, 1)
                copy_v(0, 0, 0, pro_at["v1"] + 1)
                split_max(0, 1, 0, 0)
                split_max(0, 0, 1, 0)
                sweep(nc.gpsimd, step)
                b = B - 1
                bias_x2(b)
                router_rstd(pool, B + b)
                wait_apart(pool, r_idx, 2 * B)
                for k in range(TOPK * T):
                    router_scatter(pool, 0, k)
                wait_apart(pool, scattered[0], (R2_USE + B) * 16 * TOPK * T)

        experts(2, last, True)


_INS = ["L0_attn_x", "L0_attn_wq", "L0_attn_bq", "L0_attn_wk", "L0_attn_bk", "L0_attn_wv", "L0_attn_bv", "L0_attn_wo",
        "L0_attn_bo", "L0_ffn_gate_w", "L0_ffn_c_fc", "L0_ffn_fc_bias", "L0_ffn_c_proj", "L0_ffn_proj_bias"]
_OUTS = [((4, 1024, 128), "float32")]


def kernel(**inputs):
    import numpy as _np
    import concourse.bacc as _bacc
    from concourse import mybir as _mybir
    from concourse.bass_utils import run_bass_kernel_spmd as _run

    nc = _bacc.Bacc("TRN2", target_bir_lowering=False, num_devices=1)
    arrays, args = {}, []
    for name in _INS:
        a = _np.ascontiguousarray(inputs[name])
        arrays[f"in_{name}_dram"] = a
        args.append(nc.dram_tensor(f"in_{name}_dram", a.shape, _mybir.dt.from_np(a.dtype), kind="ExternalInput").ap())
    for i, (shape, dtype) in enumerate(_OUTS):
        dt = _mybir.dt.from_np(_np.dtype(dtype))
        args.append(nc.dram_tensor(f"out_{i}_dram", shape, dt, kind="ExternalOutput").ap())
    macaron_block_kernel(nc, *args)
    r = _run(nc, [arrays], core_ids=[0])
    got = tuple(r.results[0][f"out_{i}_dram"] for i in range(len(_OUTS)))
    return got[0]
```
